# Optimizing a Trainium2 kernel written in Bass

```python
import numpy as np
import jax
import jax.numpy as jnp

def _softmax(x, axis=-1):
    return jax.nn.softmax(x, axis=axis)

def _gelu(x):
    return jax.nn.gelu(x, approximate=True)

def _silu(x):
    return jax.nn.silu(x)

def _sigmoid(x):
    return jax.nn.sigmoid(x)

def _layernorm(x, axis=-1, eps=1e-05):
    m = jnp.mean(x, axis=axis, keepdims=True)
    v = jnp.var(x, axis=axis, keepdims=True)
    return (x - m) / jnp.sqrt(v + eps)

def _scatter_add(tgt, idx, src, axis=0):
    return tgt.at[idx].add(src)

def _segment_sum(src, seg, n):
    return jax.ops.segment_sum(src, seg, n)
kernel_name = 'mk_gnn_preln_d4_gnn_r16_62891c'

def setup_inputs(seed: int=0):
    np.random.seed(seed)
    _w = jnp.asarray

    def _rec_inputs():
        import jax
        import jax.numpy as jnp
        _gk = jax.random.key(seed)
        x = -0.000202 + 1 * jax.random.normal(jax.random.fold_in(_gk, 1), (3125, 128), jnp.float32)
        src = jax.random.randint(jax.random.fold_in(_gk, 2), (100000,), 0, 3125, jnp.int32)
        dst = jnp.minimum((3125 * jax.random.uniform(jax.random.fold_in(_gk, 3), (100000,)) ** 2.0).astype(jnp.int32), 49999)
        _o = jnp.argsort(dst, stable=True)
        src = src[_o]
        dst = dst[_o]
        edge_attr_64 = -7.08334e-05 + 0.999895 * jax.random.normal(jax.random.fold_in(_gk, 11), (100000, 64), jnp.float32)
        edge_type_16 = jax.random.randint(jax.random.fold_in(_gk, 14), (100000,), 0, 16, jnp.int32)
        return (x, src, dst, edge_attr_64, edge_type_16)
    x, src, dst, edge_attr_64, edge_type_16 = _rec_inputs()

    def _L0_gnn_setup():
        import jax, jax.numpy as jnp
        import numpy as np
        N, E = (3125, 37500)
        NODE_DIM, EDGE_DIM, MSG_DIM = (128, 64, 128)
        key = jax.random.key(seed)
        ks = jax.random.split(key, 8)
        s = 0.05
        return {'node_features': jax.random.normal(ks[0], (N, NODE_DIM), jnp.float32), 'edge_features': jax.random.normal(ks[1], (E, EDGE_DIM), jnp.float32), 'edge_index': jax.random.randint(ks[2], (2, E), 0, N, jnp.int32), 'We1': jax.random.normal(ks[3], (2 * NODE_DIM + EDGE_DIM, 32), jnp.float32) * s, 'be1': jnp.zeros((32,), jnp.float32), 'We2': jax.random.normal(ks[4], (32, MSG_DIM), jnp.float32) * s, 'be2': jnp.zeros((MSG_DIM,), jnp.float32), 'Wn1': jax.random.normal(ks[5], (NODE_DIM + MSG_DIM, 64), jnp.float32) * s, 'bn1': jnp.zeros((64,), jnp.float32), 'Wn2': jax.random.normal(ks[6], (64, MSG_DIM), jnp.float32) * s, 'bn2': jnp.zeros((MSG_DIM,), jnp.float32)}
    _L0_gnn_all = _L0_gnn_setup()
    _L0_gnn_in = {k: v for k, v in _L0_gnn_all.items() if k in ('We1', 'be1', 'We2', 'be2', 'Wn1', 'bn1', 'Wn2', 'bn2')}
    del _L0_gnn_all

    def _L1_gnn_setup():
        import jax, jax.numpy as jnp
        import numpy as np
        N_NODES = 3125
        ELU_ALPHA = 0.2

        def _elu(v, alpha):
            return jnp.where(v > 0, v, alpha * jnp.expm1(v))
        key = jax.random.key(seed)
        k1, k2, k3, k4, k5 = jax.random.split(key, 5)
        fin, H, F = (128, 4, 32)
        E = 100000
        return {'x': jax.random.normal(k1, (N_NODES, fin), dtype=jnp.float32), 'W': jax.random.normal(k2, (fin, H * F), dtype=jnp.float32) * (1.414 / np.sqrt(fin)), 'a_src': jax.random.normal(k3, (H, F), dtype=jnp.float32) * 0.1, 'a_tgt': jax.random.normal(k4, (H, F), dtype=jnp.float32) * 0.1, 'edge_index': jax.random.randint(k5, (E, 2), 0, N_NODES, dtype=jnp.int64)}
    _L1_gnn_all = _L1_gnn_setup()
    _L1_gnn_in = {k: v for k, v in _L1_gnn_all.items() if k in ('W', 'a_src', 'a_tgt')}
    del _L1_gnn_all

    def _L2_gnn_setup():
        import jax, jax.numpy as jnp
        import numpy as np
        N = 3125
        E = 100000
        IN_C = 128
        OUT_C = 128
        HEADS = 8
        HFD = OUT_C // HEADS
        NEG_SLOPE = 0.2
        key = jax.random.key(seed)
        k1, k2, k3, k4, k5 = jax.random.split(key, 5)
        node_feats = jax.random.normal(k1, (N, IN_C), dtype=jnp.float32)
        edge_index = jax.random.randint(k2, (2, E), 0, N, dtype=jnp.int64)
        W = jax.random.normal(k3, (OUT_C, IN_C), dtype=jnp.float32) * (1.0 / np.sqrt(IN_C))
        a_left = jax.random.normal(k4, (HFD, HEADS), dtype=jnp.float32) * 0.1
        a_right = jax.random.normal(k5, (HFD, HEADS), dtype=jnp.float32) * 0.1
        bias = jnp.zeros((OUT_C,), dtype=jnp.float32)
        return {'node_feats': node_feats, 'edge_index': edge_index, 'W': W, 'a_left': a_left, 'a_right': a_right, 'bias': bias}
    _L2_gnn_all = _L2_gnn_setup()
    _L2_gnn_in = {k: v for k, v in _L2_gnn_all.items() if k in ('W', 'a_left', 'a_right', 'bias')}
    del _L2_gnn_all

    def _L3_gnn_setup():
        import jax, jax.numpy as jnp
        import numpy as np
        N_NODES = 6250
        N_EDGES = 37500
        D_IN = 128
        D_OUT = 128
        N_REL = 16
        N_BASES = 8
        key = jax.random.key(seed)
        ks = jax.random.split(key, 6)
        x = jax.random.normal(ks[0], (N_NODES, D_IN), dtype=jnp.float32)
        edge_index = jax.random.randint(ks[1], (2, N_EDGES), 0, N_NODES, dtype=jnp.int64)
        edge_type = jax.random.randint(ks[2], (N_EDGES,), 0, N_REL, dtype=jnp.int64)
        b_lim = float(np.sqrt(6.0 / (D_IN + D_OUT)))
        c_lim = float(np.sqrt(6.0 / (N_REL + N_BASES)))
        w_lim = float(np.sqrt(6.0 / (D_IN + D_OUT)))
        bases = jax.random.uniform(ks[3], (N_BASES, D_IN, D_OUT), jnp.float32, -b_lim, b_lim)
        coefficients = jax.random.uniform(ks[4], (N_REL, N_BASES), jnp.float32, -c_lim, c_lim)
        w_self = jax.random.uniform(ks[5], (D_OUT, D_IN), jnp.float32, -w_lim, w_lim)
        return {'x': x, 'edge_index': edge_index, 'edge_type': edge_type, 'bases': bases, 'coefficients': coefficients, 'w_self': w_self}
    _L3_gnn_all = _L3_gnn_setup()
    _L3_gnn_in = {k: v for k, v in _L3_gnn_all.items() if k in ('bases', 'coefficients', 'w_self')}
    del _L3_gnn_all
    return {'x': x, 'src': src, 'dst': dst, 'edge_attr_64': edge_attr_64, 'edge_type_16': edge_type_16, 'L0_gnn_We1': _L0_gnn_in['We1'], 'L0_gnn_be1': _L0_gnn_in['be1'], 'L0_gnn_We2': _L0_gnn_in['We2'], 'L0_gnn_be2': _L0_gnn_in['be2'], 'L0_gnn_Wn1': _L0_gnn_in['Wn1'], 'L0_gnn_bn1': _L0_gnn_in['bn1'], 'L0_gnn_Wn2': _L0_gnn_in['Wn2'], 'L0_gnn_bn2': _L0_gnn_in['bn2'], 'L1_gnn_W': _L1_gnn_in['W'], 'L1_gnn_a_src': _L1_gnn_in['a_src'], 'L1_gnn_a_tgt': _L1_gnn_in['a_tgt'], 'L2_gnn_W': _L2_gnn_in['W'], 'L2_gnn_a_left': _L2_gnn_in['a_left'], 'L2_gnn_a_right': _L2_gnn_in['a_right'], 'L2_gnn_bias': _L2_gnn_in['bias'], 'L3_gnn_bases': _L3_gnn_in['bases'], 'L3_gnn_coefficients': _L3_gnn_in['coefficients'], 'L3_gnn_w_self': _L3_gnn_in['w_self']}

def reference(x, src, dst, edge_attr_64, edge_type_16, L0_gnn_We1, L0_gnn_be1, L0_gnn_We2, L0_gnn_be2, L0_gnn_Wn1, L0_gnn_bn1, L0_gnn_Wn2, L0_gnn_bn2, L1_gnn_W, L1_gnn_a_src, L1_gnn_a_tgt, L2_gnn_W, L2_gnn_a_left, L2_gnn_a_right, L2_gnn_bias, L3_gnn_bases, L3_gnn_coefficients, L3_gnn_w_self):
    import jax
    import jax.numpy as jnp

    def _L0_gnn_ref(node_features, edge_features, edge_index, We1, be1, We2, be2, Wn1, bn1, Wn2, bn2):
        import jax, jax.numpy as jnp
        import numpy as np
        N, E = (3125, 37500)
        NODE_DIM, EDGE_DIM, MSG_DIM = (128, 64, 128)
        src, dst = (edge_index[0], edge_index[1])
        src_f = node_features[src]
        dst_f = node_features[dst]
        edge_in = jnp.concatenate([src_f, dst_f, edge_features], axis=1)
        h = jax.nn.relu(edge_in @ We1 + be1)
        edge_msg = jax.nn.relu(h @ We2 + be2)
        node_in = jnp.concatenate([dst_f, edge_msg], axis=1)
        h2 = jax.nn.relu(node_in @ Wn1 + bn1)
        node_msg = jax.nn.relu(h2 @ Wn2 + bn2)
        agg = jax.ops.segment_sum(node_msg, dst, num_segments=node_features.shape[0])
        return node_features + agg

    def _L1_gnn_ref(x, W, a_src, a_tgt, edge_index):
        import jax, jax.numpy as jnp
        import numpy as np
        N_NODES = 3125
        ELU_ALPHA = 0.2

        def _elu(v, alpha):
            return jnp.where(v > 0, v, alpha * jnp.expm1(v))
        N = x.shape[0]
        H, F = a_src.shape
        xp = (x @ W).reshape(N, H, F)
        s_src = jnp.einsum('nhf,hf->nh', xp, a_src)
        s_tgt = jnp.einsum('nhf,hf->nh', xp, a_tgt)
        src = edge_index[:, 0]
        tgt = edge_index[:, 1]
        e = _elu(s_src[src] + s_tgt[tgt], ELU_ALPHA)
        m = jax.ops.segment_max(e, tgt, num_segments=N)
        m = jnp.where(jnp.isfinite(m), m, 0.0)
        ex = jnp.exp(e - m[tgt])
        denom = jax.ops.segment_sum(ex, tgt, num_segments=N)
        alpha = ex / denom[tgt]
        msg = alpha[:, :, None] * xp[src]
        out = jax.ops.segment_sum(msg, tgt, num_segments=N)
        return out.reshape(N, H * F)

    def _L2_gnn_ref(node_feats, edge_index, W, a_left, a_right, bias):
        import jax, jax.numpy as jnp
        import numpy as np
        N = 3125
        E = 100000
        IN_C = 128
        OUT_C = 128
        HEADS = 8
        HFD = OUT_C // HEADS
        NEG_SLOPE = 0.2
        n = node_feats.shape[0]
        emb = (node_feats @ W.T).reshape(n, HEADS, HFD)
        left = jnp.einsum('nhc,ch->nh', emb, a_left)
        right = jnp.einsum('nhc,ch->nh', emb, a_right)
        src = edge_index[0]
        dst = edge_index[1]
        e = left[src] + right[dst]
        e = jnp.where(e >= 0, e, NEG_SLOPE * e)
        w = jnp.exp(e)
        denom = jax.ops.segment_sum(w, dst, num_segments=n)
        attn = w / denom[dst]
        msg = emb[src] * attn[:, :, None]
        out = jax.ops.segment_sum(msg, dst, num_segments=n)
        out = out.reshape(n, HEADS * HFD) + bias
        return out

    def _L3_gnn_ref(x, edge_index, edge_type, bases, coefficients, w_self):
        import jax, jax.numpy as jnp
        import numpy as np
        N_NODES = 6250
        N_EDGES = 37500
        D_IN = 128
        D_OUT = 128
        N_REL = 16
        N_BASES = 8
        out = x @ w_self.T
        weights = jnp.einsum('rb,bio->rio', coefficients, bases)
        row, col = (edge_index[0], edge_index[1])
        xc = x[col]
        n_rel = weights.shape[0]
        msg = jnp.zeros((xc.shape[0], w_self.shape[0]), dtype=x.dtype)
        for r in range(n_rel):
            sel = (edge_type == r)[:, None]
            msg = msg + jnp.where(sel, xc @ weights[r], jnp.zeros((), x.dtype))
        out = out.at[row].add(msg)
        return out
    edge_index = jnp.stack([src, dst])
    edge_index_t = jnp.stack([src, dst], axis=1)
    h = jnp.maximum(_layernorm(x, axis=-1), 0.0)
    x = x + _L0_gnn_ref(h, edge_attr_64, edge_index, L0_gnn_We1, L0_gnn_be1, L0_gnn_We2, L0_gnn_be2, L0_gnn_Wn1, L0_gnn_bn1, L0_gnn_Wn2, L0_gnn_bn2)
    h = jnp.maximum(_layernorm(x, axis=-1), 0.0)
    x = x + _L1_gnn_ref(h, L1_gnn_W, L1_gnn_a_src, L1_gnn_a_tgt, edge_index_t)
    h = jnp.maximum(_layernorm(x, axis=-1), 0.0)
    x = x + _L2_gnn_ref(h, edge_index, L2_gnn_W, L2_gnn_a_left, L2_gnn_a_right, L2_gnn_bias)
    h = jnp.maximum(_layernorm(x, axis=-1), 0.0)
    x = x + _L3_gnn_ref(h, edge_index, edge_type_16, L3_gnn_bases, L3_gnn_coefficients, L3_gnn_w_self)
    return x

_drawn_inputs = setup_inputs


def setup_inputs(seed=0):
    import zlib

    import numpy as np

    out = dict(_drawn_inputs(seed))
    spreads = {'L0_gnn_be1': (0.0, 0.8),
     'L0_gnn_be2': (0.0, 0.1),
     'L0_gnn_bn1': (0.0, 0.1),
     'L0_gnn_bn2': (0.0, 0.1),
     'L2_gnn_bias': (0.0, 0.432)}
    factors = {'edge_attr_64': 8.0,
     'L1_gnn_a_src': 4.37,
     'L1_gnn_a_tgt': 8.0,
     'L2_gnn_a_left': 8.0,
     'L2_gnn_a_right': 8.0}
    for name, (base, spread) in spreads.items():
        noise = np.random.default_rng([zlib.crc32(name.encode()), seed]).standard_normal(out[name].shape)
        drawn = base * np.exp(spread * noise) if base else spread * noise
        out[name] = jnp.asarray(drawn.astype(out[name].dtype))
    for name, factor in factors.items():
        out[name] = (out[name] * factor).astype(out[name].dtype)
    return out
```

```python
from contextlib import ExitStack

import concourse.bass as bass
from concourse import mybir

ALU = mybir.AluOpType
ACT = mybir.ActivationFunctionType
AX = mybir.AxisListType
F32 = mybir.dt.float32
I32 = mybir.dt.int32

P = 128
N_NODES = 3125
N_BINS = -(-N_NODES // P)
N_ROWS = N_BINS * P
FULL = N_NODES // P
LAST = N_NODES - FULL * P
D = 128
N_EDGES = 100000
SORT_P = 125
SORT_J = N_EDGES // SORT_P
TILES = 4
BLOCK = TILES * P
N_BLOCKS = (N_EDGES + N_BINS * (BLOCK - 1)) // BLOCK
UNROLL = 4
N_BLOCKS = -(-N_BLOCKS // UNROLL) * UNROLL
N_POS = N_BLOCKS * BLOCK
EDGE_D = 64
N_REL, N_BASES = 16, 8
EPS = 1e-5
BIG = 1e30
DW = 4
SW = 2


def pipeline(eng, stages):
    deepest = max(lag for lag, _ in stages)
    head = -(-(deepest + UNROLL) // UNROLL) * UNROLL

    def step(k):
        for lag, fn in stages:
            if 0 <= k - lag < N_BLOCKS:
                fn(k - lag, (k - lag) // UNROLL, (k - lag) % UNROLL)

    for k in range(head):
        step(k)
    with eng.Fori(head // UNROLL, N_BLOCKS // UNROLL) as i:
        for c in range(UNROLL):
            for lag, fn in stages:
                at = c - lag
                fn(i * UNROLL + at, i + at // UNROLL, at % UNROLL)
    for k in range(N_BLOCKS, N_BLOCKS + deepest):
        step(k)


class Chain:

    def __init__(self, eng, sem):
        self.eng, self.sem, self.n = eng, sem, 0

    def do(self, ins):
        self.n += 1
        ins.then_inc(self.sem, 1)
        self.eng.wait_ge(self.sem, self.n)


class Core:

    def __init__(self, nc, tag):
        self.nc, self.tag, self.ctx, self.taken = nc, tag, ExitStack(), []

    def __enter__(self):
        return self

    def __exit__(self, kind, *a):
        if kind is None:
            self.ctx.close()
            self.nc.clear_and_free_semaphores(self.taken)
            self.nc.all_engine_barrier()

    def sb(self, name, shape, dt=F32):
        return self.ctx.enter_context(self.nc.sbuf_tensor(f"{self.tag}_{name}", shape, dt))

    def ps(self, name, shape=(P, 512)):
        return self.ctx.enter_context(self.nc.psum_tensor(f"{self.tag}_ps_{name}", list(shape), F32))

    def sem(self, name):
        self.taken.append(self.nc.alloc_semaphore(name=f"{self.tag}_s_{name}"))
        return self.taken[-1]

    def sems(self, name, n):
        return [self.sem(f"{name}{i}") for i in range(n)]

    def block(self):
        return self.ctx.enter_context(self.nc.Block())


def constants(nc, g):
    with Core(nc, "con") as c:
        s_c = c.sem("c")
        block = c.block()

        @block.gpsimd
        def _(gp):
            ch = Chain(gp, s_c)
            ch.do(gp.memset(g.ident[:], 0.0))
            ch.do(gp.affine_select(out=g.ident[:], in_=g.ident[:], compare_op=ALU.not_equal, fill=1.0,
                                   base=0, pattern=[[-1, P]], channel_multiplier=1))
            ch.do(gp.memset(g.ones[:], 1.0))
            ch.do(gp.affine_select(out=g.earlier[:], in_=g.ones[:], compare_op=ALU.is_gt, fill=0.0,
                                   base=0, pattern=[[1, P]], channel_multiplier=-1))
            ch.do(gp.iota(g.iota[:], pattern=[[1, P]], base=0, channel_multiplier=0,
                          allow_small_or_imprecise_dtypes=True))
            ch.do(gp.iota(g.iota_blocks[:], pattern=[[1, N_BLOCKS]], base=0, channel_multiplier=0,
                          allow_small_or_imprecise_dtypes=True))


def setup(nc, g, args):
    with Core(nc, "set") as c:
        s_w, s_x, s_z = c.sem("w"), c.sem("x"), c.sem("z")
        block = c.block()
        loads = [
            (g.we1_src[:], args["We1"][0:D, :]), (g.we1_dst[:], args["We1"][D:2 * D, :]),
            (g.we1_edge[:], args["We1"][2 * D:2 * D + EDGE_D, :]), (g.we2[:], args["We2"]),
            (g.wn1_dst[:], args["Wn1"][0:D, :]), (g.wn1_msg[:], args["Wn1"][D:2 * D, :]),
            (g.wn2b[0:64, :], args["Wn2"]), (g.wn2b[64:65, :], args["bn2"].unsqueeze(0)),
            (g.be2[:], args["be2"].unsqueeze(1)),
            (g.bias0[:, 0:32], args["be1"].partition_broadcast(P)),
            (g.bias0[:, 32:96], args["bn1"].partition_broadcast(P)),
            (g.w1[:], args["W1"]), (g.w2[:], args["W2"]),
            (g.a1[:, 0, :], args["a_src"].rearrange("h f -> (h f)").partition_broadcast(P)),
            (g.a1[:, 1, :], args["a_tgt"].rearrange("h f -> (h f)").partition_broadcast(P)),
            (g.a2[:, 0, :], args["a_left"].rearrange("c h -> (c h)").partition_broadcast(P)),
            (g.a2[:, 1, :], args["a_right"].rearrange("c h -> (c h)").partition_broadcast(P)),
            (g.bias2[:], args["bias"].partition_broadcast(P)),
            (g.bases[:], args["bases"].rearrange("b i o -> i b o")),
            (g.coef[:], args["coefficients"].rearrange("r b -> (r b)").partition_broadcast(P)),
            (g.w_self[:], args["w_self"]),
            (g.X[:, 0:FULL, :], args["x"][0:FULL * P, :].rearrange("(a b) f -> b a f", b=P)),
        ]

        @block.vector
        def _(v):
            v.memset(g.X[:, FULL, :], 0.0).then_inc(s_z, 1)

        @block.sync
        def _(sp):
            for dst, src in loads:
                sp.dma_start(dst, src).then_inc(s_w, 16)
            sp.wait_ge(s_z, 1)
            sp.dma_start(g.X[0:LAST, FULL, :], args["x"][FULL * P:N_NODES, :]).then_inc(s_x, 16)
            sp.wait_ge(s_w, 16 * len(loads))
            sp.wait_ge(s_x, 16)


def sort_edges(nc, g, tag, key, words, width, rec_dram, rec, bin_of):
    with Core(nc, tag) as c:
        key_i = c.sb("key", [SORT_P, SORT_J], I32)
        bin_i = c.sb("bin_i", [SORT_P, SORT_J], I32)
        bin_f = c.sb("bin_f", [SORT_P, SORT_J])
        hot = c.sb("hot", [SORT_P, SORT_J])
        pick = c.sb("pick", [SORT_P, SORT_J])
        pos = c.sb("pos", [SORT_P, SORT_J])
        pos_i = c.sb("pos_i", [SORT_P, SORT_J], I32)
        rank = c.sb("rank", [SORT_P, N_BINS, SORT_J])
        recs = c.sb("recs", [SORT_P, SORT_J, width], I32)
        extra = c.sb("extra", [SORT_P, 2, SORT_J], I32)
        extra_f = c.sb("extra_f", [SORT_P, 2, SORT_J])
        empty = c.sb("empty", [P, N_POS // P, width], I32)
        total = c.sb("total", [P, N_BINS], I32)
        blocks = c.sb("blocks", [P, N_BINS])
        upto = c.sb("upto", [P, N_BINS])
        base = c.sb("base", [P, N_BINS])
        bins_f = c.sb("bins_f", [1, N_BLOCKS])
        p_before, p_total = c.ps("before"), c.ps("total")
        s_in, s_v, s_mm, s_cnt, s_done = c.sem("in"), c.sem("v"), c.sem("mm"), c.sem("cnt"), c.sem("done")
        s_id, s_e, s_em, s_sc, s_ld, s_emp = (c.sem(n) for n in ("id", "e", "em", "sc", "ld", "emp"))
        block = c.block()
        n_load = 1 + sum(w[0] in ("load", "pair") for w in words) + sum(w[0] == "pair" for w in words)

        @block.sync
        def _(sp):
            sp.dma_start(key_i[:], key.rearrange("(p j) -> p j", p=SORT_P)).then_inc(s_in, 16)
            for w, what in enumerate(words):
                if what[0] in ("load", "pair"):
                    sp.dma_start(extra[:, 0, :], what[1].rearrange("(p j) -> p j", p=SORT_P)).then_inc(s_in, 16)
                if what[0] == "pair":
                    sp.dma_start(extra[:, 1, :], what[2].rearrange("(p j) -> p j", p=SORT_P)).then_inc(s_in, 16)
            sp.wait_ge(s_emp, 1)
            sp.dma_start(rec_dram.rearrange("(k p t) w -> p k (t w)", p=P, t=TILES),
                         empty[:].rearrange("p (k t) w -> p k (t w)", t=TILES)).then_inc(s_em, 16)
            sp.wait_ge(s_sc, 16 * SORT_J)
            sp.dma_start(rec[:].rearrange("p (k t) w -> p k (t w)", t=TILES),
                         rec_dram.rearrange("(k p t) w -> p k (t w)", p=P, t=TILES)).then_inc(s_ld, 16)
            sp.wait_ge(s_ld, 16)

        @block.vector
        def _(v):
            ch = Chain(v, s_v)
            ch.do(v.memset(empty[:], 0))
            v.memset(empty[:, :, 1:2].bitcast(F32), -1.0).then_inc(s_emp, 1)
            v.wait_ge(s_in, 16 * n_load)
            ch.do(v.tensor_single_scalar(bin_i[:], key_i[:], 7, ALU.logical_shift_right))
            ch.do(v.tensor_copy(bin_f[:], bin_i[:]))
            for a in range(N_BINS):
                ch.do(v.tensor_single_scalar(hot[:], bin_f[:], float(a), ALU.is_equal))
                ch.do(v.tensor_tensor_scan(rank[:, a, :], hot[:], hot[:], 0.0, ALU.add, ALU.max))
            ch.do(v.tensor_copy(hot[:, 0:N_BINS], rank[:, :, SORT_J - 1]))
            v.sem_inc(s_cnt, 1)
            for w, what in enumerate(words):
                if what[0] == "load":
                    ch.do(v.tensor_copy(recs[:, :, w], extra[:, 0, :]))
                if what[0] == "pair":
                    ch.do(v.tensor_copy(extra_f[:, 0, :], extra[:, 0, :]))
                    ch.do(v.tensor_copy(extra_f[:, 1, :], extra[:, 1, :]))
                    ch.do(v.scalar_tensor_tensor(extra_f[:, 0, :], extra_f[:, 0, :], float(N_REL),
                                                 extra_f[:, 1, :], ALU.mult, ALU.add))
                    ch.do(v.tensor_copy(recs[:, :, w], extra_f[:, 0, :]))
                if what[0] == "local":
                    ch.do(v.tensor_single_scalar(bin_i[:], key_i[:], P - 1, ALU.bitwise_and))
                    ch.do(v.tensor_copy(recs[:, :, w].bitcast(F32), bin_i[:]))
                if what[0] == "id":
                    v.wait_ge(s_id, 1)
                    ch.do(v.tensor_copy(recs[:, :, w], extra_f[:, 0, :].bitcast(I32)))
                if what[0] == "zero":
                    ch.do(v.memset(recs[:, :, w:w + 1], 0))
            v.wait_ge(s_mm, 2)
            ch.do(v.tensor_single_scalar(upto[:], p_total[:, 0:N_BINS], float(BLOCK - 1), ALU.add))
            ch.do(v.tensor_copy(total[:], upto[:]))
            ch.do(v.tensor_single_scalar(total[:], total[:], BLOCK.bit_length() - 1, ALU.logical_shift_right))
            ch.do(v.tensor_copy(blocks[:], total[:]))
            ch.do(v.tensor_tensor_scan(upto[:], blocks[:], blocks[:], 0.0, ALU.add, ALU.max))
            ch.do(v.tensor_tensor(base[:], upto[:], blocks[:], ALU.subtract))
            ch.do(v.tensor_scalar(base[:], base[:], float(BLOCK), -1.0, ALU.mult, ALU.add))
            ch.do(v.tensor_tensor(base[0:SORT_P, :], base[0:SORT_P, :], p_before[0:SORT_P, 0:N_BINS], ALU.add))
            ch.do(v.memset(bins_f[:], 0.0))
            for a in range(N_BINS - 1):
                ch.do(v.scalar_tensor_tensor(bins_f[:], g.iota_blocks[:], upto[0:1, a:a + 1], bins_f[:],
                                             ALU.is_ge, ALU.add))
            ch.do(v.tensor_copy(bin_of[:], bins_f[:]))
            ch.do(v.memset(pos[:], 0.0))
            for a in range(N_BINS):
                ch.do(v.tensor_scalar(rank[:, a, :], rank[:, a, :], base[0:SORT_P, a:a + 1], None, ALU.add))
                ch.do(v.scalar_tensor_tensor(pick[:], bin_f[:], float(a), rank[:, a, :], ALU.is_equal, ALU.mult))
                ch.do(v.tensor_tensor(pos[:], pos[:], pick[:], ALU.add))
            v.tensor_copy(pos_i[:], pos[:]).then_inc(s_done, 1)

        @block.tensor
        def _(pe):
            pe.wait_ge(s_cnt, 1)
            pe.matmul(p_before[:, 0:N_BINS], g.earlier[0:SORT_P, :], hot[:, 0:N_BINS],
                      start=True, stop=True).then_inc(s_mm, 1)
            pe.matmul(p_total[:, 0:N_BINS], g.ones[0:SORT_P, :], hot[:, 0:N_BINS],
                      start=True, stop=True).then_inc(s_mm, 1)

        @block.gpsimd
        def _(gp):
            if ("id",) in words:
                gp.iota(extra_f[:, 0, :].bitcast(I32), pattern=[[1, SORT_J]], base=0,
                        channel_multiplier=SORT_J).then_inc(s_id, 1)
            gp.wait_ge(s_done, 1)
            gp.wait_ge(s_em, 16)
            for j in range(SORT_J):
                gp.indirect_dma_start(rec_dram, bass.IndirectOffsetOnAxis(pos_i[:, j:j + 1], axis=0),
                                      recs[:, j, :], None).then_inc(s_sc, 16)


def layer_norm(v, ch, g, c, s_var, s_std, act_done):
    full = [P, N_BINS, D]
    ch.do(v.tensor_reduce(g.mu[:], g.X[:], AX.X, ALU.add))
    ch.do(v.tensor_single_scalar(g.mu[:], g.mu[:], 1.0 / D, ALU.mult))
    ch.do(v.tensor_tensor(g.H[:], g.X[:], g.mu[:].unsqueeze(2).broadcast_to(full), ALU.subtract))
    ch.do(v.tensor_tensor(g.TMP[:], g.H[:], g.H[:], ALU.mult))
    ch.do(v.tensor_reduce(g.var[:], g.TMP[:], AX.X, ALU.add))
    ch.do(v.tensor_scalar(g.var[:], g.var[:], 1.0 / D, EPS, ALU.mult, ALU.add))
    v.sem_inc(s_var, 1)
    v.wait_ge(s_std, 1)
    ch.do(v.reciprocal(g.var[:], g.std[:]))
    ch.do(v.scalar_tensor_tensor(g.H[:], g.H[:], 0.0, g.var[:].unsqueeze(2).broadcast_to(full),
                                 ALU.max, ALU.mult))


def node_phase(nc, g, layer, tables):
    with Core(nc, f"n{layer}") as c:
        ht = c.sb("ht", [D, N_ROWS])
        wt = c.sb("wt", [D, D])
        p_t = [c.ps(f"t{i}") for i in range(2)]
        p_m = [c.ps(f"m{i}") for i in range(4)]
        s_var, s_std, s_h, s_v = c.sem("var"), c.sem("std"), c.sem("h"), c.sem("v")
        s_t, s_tc, s_w, s_wc, s_m, s_mc, s_tab = (c.sem(n) for n in ("t", "tc", "w", "wc", "m", "mc", "tab"))
        s_row, s_wall = c.sem("row"), c.sem("wall")
        groups = [range(a, min(a + 4, N_BINS)) for a in range(0, N_BINS, 4)]
        if layer == 0:
            stage = c.sb("stage", [P, N_BINS, 32])
        if layer in (1, 2):
            heads = 4 if layer == 1 else 8
            f = D // heads
            stage = c.sb("stage", [P, N_BINS, heads, f + 1])
        if layer == 3:
            wall = c.sb("wall", [D, N_REL, D])
            stage = c.sb("stage", [P, 2, N_REL * D])
        block = c.block()

        @block.scalar
        def _(act):
            act.wait_ge(s_var, 1)
            act.activation(g.std[:], g.var[:], ACT.Sqrt).then_inc(s_std, 1)
            for n, bins in enumerate(groups):
                act.wait_ge(s_t, n + 1)
                act.copy(ht[:, bins[0] * P:(bins[-1] + 1) * P],
                         p_t[n % 2][:, 0:len(bins) * P]).then_inc(s_tc, 1)

        @block.tensor
        def _(pe):
            if layer in (2, 3):
                pe.transpose(p_m[3][:, 0:D], (g.w2 if layer == 2 else g.w_self)[:], g.ident[:]).then_inc(s_w, 1)
            pe.wait_ge(s_h, 1)
            for n, bins in enumerate(groups):
                if n >= 2:
                    pe.wait_ge(s_tc, n - 1)
                for a in bins:
                    mm = pe.transpose(p_t[n % 2][:, (a - bins[0]) * P:(a - bins[0] + 1) * P],
                                      g.H[:, a, :], g.ident[:])
                mm.then_inc(s_t, 1)
            if layer in (2, 3):
                pe.wait_ge(s_wc, 1)
            if layer == 3:
                pe.wait_ge(s_wall, 1)
            n_m = 0
            for a in range(N_BINS):
                pe.wait_ge(s_tc, a // 4 + 1)
                lhs = ht[:, a * P:(a + 1) * P]

                def out(width, parts):
                    nonlocal n_m
                    if n_m >= 4:
                        pe.wait_ge(s_mc, n_m - 3)
                    bank = p_m[n_m % 4]
                    for at, w in parts:
                        mm = pe.matmul(bank[:, at:at + w.shape[-1]], lhs, w, start=True, stop=True)
                    mm.then_inc(s_m, 1)
                    n_m += 1

                if layer == 0:
                    out(P, [(0, g.we1_src[:]), (32, g.we1_dst[:]), (64, g.wn1_dst[:])])
                if layer == 1:
                    out(P, [(0, g.w1[:])])
                if layer == 2:
                    out(P, [(0, wt[:])])
                if layer == 3:
                    out(P, [(0, wt[:])])
                    for r in range(0, N_REL, 4):
                        out(512, [(0, wall[:, r:r + 4, :].rearrange("i r o -> i (r o)"))])

        @block.vector
        def _(v):
            ch = Chain(v, s_v)
            if layer in (2, 3):
                v.wait_ge(s_w, 1)
                v.tensor_copy(wt[:], p_m[3][:, 0:D]).then_inc(s_wc, 1)
            if layer == 3:
                for r in range(N_REL):
                    for b in range(N_BASES):
                        w = g.coef[:, r * N_BASES + b:r * N_BASES + b + 1]
                        if b == 0:
                            ch.do(v.tensor_scalar(wall[:, r, :], g.bases[:, b, :], w, None, ALU.mult))
                        else:
                            ch.do(v.scalar_tensor_tensor(wall[:, r, :], g.bases[:, b, :], w, wall[:, r, :],
                                                         ALU.mult, ALU.add))
                v.sem_inc(s_wall, 1)
            layer_norm(v, ch, g, c, s_var, s_std, None)
            v.sem_inc(s_h, 1)
            if layer == 0:
                for a in range(N_BINS):
                    v.wait_ge(s_m, a + 1)
                    v.tensor_copy(stage[:, a, :], p_m[a % 4][:, 0:32])
                    v.tensor_tensor(g.dst0[:, a, :], p_m[a % 4][:, 32:P], g.bias0[:], ALU.add).then_inc(s_mc, 1)
                v.wait_ge(s_mc, N_BINS)
                ch.do(v.tensor_tensor(g.X[:], g.X[:], g.H[:], ALU.add))
            if layer in (1, 2):
                for a in range(N_BINS):
                    v.wait_ge(s_m, a + 1)
                    v.tensor_copy(stage[:, a, :, 0:f],
                                  p_m[a % 4][:, 0:D].rearrange("p (h f) -> p h f", h=heads)).then_inc(s_mc, 1)
                v.wait_ge(s_mc, N_BINS)
                shape = [P, N_BINS, heads, f]
                for side in range(2):
                    if layer == 1:
                        a_row = g.a1[:, side, :].rearrange("p (h f) -> p h f", h=heads)
                    else:
                        a_row = g.a2[:, side, :].rearrange("p (f h) -> p h f", h=heads)
                    prod = g.TMP[:].rearrange("p a (h f) -> p a h f", h=heads)
                    for a in range(N_BINS):
                        ins = v.tensor_tensor(prod[:, a], stage[:, a, :, 0:f], a_row, ALU.mult)
                    ch.do(ins)
                    where = stage[:, :, :, f] if side == 0 else g.tgt[:, :, 0:heads]
                    ch.do(v.tensor_reduce(where, prod, AX.X, ALU.add))
            if layer == 3:
                for a in range(N_BINS):
                    for part in range(5):
                        n = 5 * a + part
                        v.wait_ge(s_m, n + 1)
                        if part == 0:
                            v.tensor_tensor(g.X[:, a, :], g.X[:, a, :], p_m[n % 4][:, 0:D],
                                            ALU.add).then_inc(s_mc, 1)
                            continue
                        if part == 1 and a >= 2:
                            v.wait_ge(s_row[a % 2] if isinstance(s_row, list) else s_row, 16 * (a - 1))
                        v.tensor_copy(stage[:, a % 2, (part - 1) * 512:part * 512],
                                      p_m[n % 4][:]).then_inc(s_mc, 1)
            v.sem_inc(s_tab, 1)

        @block.sync
        def _(sp):
            if layer == 3:
                rows = tables.rearrange("(a n r) f -> a n (r f)", a=N_BINS, n=P)
                for a in range(N_BINS):
                    sp.wait_ge(s_mc, 5 * a + 5)
                    if a >= 1:
                        sp.wait_ge(s_row, 16 * a)
                    sp.dma_start(rows[a], stage[:, a % 2, :]).then_inc(s_row, 16)
                sp.wait_ge(s_row, 16 * N_BINS)
            else:
                sp.wait_ge(s_tab, 1)
                src = stage[:] if layer == 0 else stage[:].rearrange("p a h f -> p a (h f)")
                sp.dma_start(tables.rearrange("(a n) f -> n a f", a=N_BINS), src).then_inc(s_row, 16)
                sp.wait_ge(s_row, 16)


def rec_f(rec, k):
    return rec[:, bass.ds(k * TILES, TILES), 1:2].bitcast(F32).broadcast_to([P, TILES, P])


def ge(eng, sem, value):
    if isinstance(value, int) and value <= 0:
        return
    eng.wait_ge(sem, value)


def tick(eng, sem):
    eng.sem_inc(sem, 1)


def gather_stages(act, gp, rec, words, index, rows, tables, s_ix, s_g, s_tick, s_free):
    per = 16 * TILES * len(words)

    def lay(k, q, b):
        ge(act, s_g[b], q * per)
        for n, w in enumerate(words):
            ins = act.copy(index[b][:, n, :], rec[:, bass.ds(k * TILES, TILES), w])
        ins.then_inc(s_ix, 1)

    def gather(k, q, b):
        ge(gp, s_free, k - (UNROLL - 1))
        gp.wait_ge(s_ix, k + 1)
        tick(gp, s_tick)
        for n in range(len(words)):
            for t in range(TILES):
                gp.indirect_dma_start(rows[n][b][:, t, :], None, tables[n],
                                      bass.IndirectOffsetOnAxis(index[b][:, n, t:t + 1], axis=0)).then_inc(s_g[b], 16)

    return lay, gather


def edge_mlp(nc, g, edge_attr):
    with Core(nc, "mlp") as c:
        hot = [c.sb(f"hot{b}", [P, TILES, P]) for b in range(UNROLL)]
        index = [c.sb(f"index{b}", [P, 2, TILES], I32) for b in range(UNROLL)]
        row_s = [c.sb(f"row_s{b}", [P, TILES, 32]) for b in range(UNROLL)]
        row_e = [c.sb(f"row_e{b}", [P, TILES, EDGE_D]) for b in range(UNROLL)]
        hot_t = [c.sb(f"hot_t{b}", [P, BLOCK]) for b in range(2)]
        edge_t = [c.sb(f"edge_t{b}", [EDGE_D, BLOCK]) for b in range(2)]
        dst = [c.sb(f"dst{b}", [P, 96]) for b in range(2)]
        h1 = [c.sb(f"h1{b}", [32, BLOCK]) for b in range(2)]
        em = [c.sb(f"em{b}", [P, BLOCK]) for b in range(2)]
        h2 = [c.sb(f"h2{b}", [EDGE_D + 1, BLOCK]) for b in range(2)]
        nm = [c.sb(f"nm{b}", [P, TILES, D]) for b in range(2)]
        p_hot, p_edge, p_h1, p_em, p_h2, p_nm, p_sum = (c.ps(n) for n in "hot edge h1 em h2 nm sum".split())
        s_g, s_tick = c.sems("g", UNROLL), c.sem("tick")
        (s_ix, s_init, s_hot, s_turn, s_turned, s_dst, s_h1, s_h1r, s_em, s_emr, s_h2, s_h2r, s_nm, s_nmr,
         s_sum, s_acc) = (c.sem(n) for n in "ix init hot turn turned dst h1 h1r em emr h2 h2r nm nmr sum acc".split())
        block = c.block()

        @block.gpsimd
        def _(gp):
            for b in range(2):
                gp.memset(h2[b][EDGE_D:EDGE_D + 1, :], 1.0).then_inc(s_init, 1)
                gp.wait_ge(s_init, b + 1)
            gp.memset(g.acc[:, :, 0:D], 0.0).then_inc(s_init, 1)
            _, gather = gather_stages(None, gp, g.rec_d, (0, 2), index, (row_s, row_e), (g.tab0, edge_attr),
                                      s_ix, s_g, s_tick, s_h1)
            pipeline(gp, [(0, gather)])

        @block.scalar
        def _(act):
            lay, _ = gather_stages(act, None, g.rec_d, (0, 2), index, (row_s, row_e), (g.tab0, edge_attr),
                                   s_ix, s_g, s_tick, s_h1)

            def turned(k, q, b):
                act.wait_ge(s_turn, k + 1)
                ge(act, s_h2, k - 1)
                act.copy(hot_t[b % 2][:], p_hot[:])
                act.copy(edge_t[b % 2][:], p_edge[0:EDGE_D, :]).then_inc(s_turned, 1)

            def h1_relu(k, q, b):
                act.wait_ge(s_h1, k + 1)
                ge(act, s_em, k - 1)
                act.activation(h1[b % 2][:], p_h1[0:32, :], ACT.Relu).then_inc(s_h1r, 1)

            def em_relu(k, q, b):
                act.wait_ge(s_em, k + 1)
                ge(act, s_h2, k - 1)
                act.activation(em[b % 2][:], p_em[:], ACT.Relu, bias=g.be2[:]).then_inc(s_emr, 1)

            def h2_relu(k, q, b):
                act.wait_ge(s_h2, k + 1)
                ge(act, s_nm, k - 1)
                act.activation(h2[b % 2][0:EDGE_D, :], p_h2[0:EDGE_D, :], ACT.Relu).then_inc(s_h2r, 1)

            pipeline(act, [(0, lay), (3, turned), (4, h2_relu), (3, h1_relu), (3, em_relu)])

        @block.tensor
        def _(pe):
            pe.wait_ge(s_init, 3)

            def turn(k, q, b):
                ge(pe, s_turned, k)
                pe.wait_ge(s_hot, k + 1)
                for t in range(TILES):
                    pe.transpose(p_hot[:, t * P:(t + 1) * P], hot[b][:, t, :], g.ident[:])
                pe.wait_ge(s_g[b], 32 * TILES * (q + 1))
                tick(pe, s_tick)
                for t in range(TILES):
                    mm = pe.transpose(p_edge[0:EDGE_D, t * P:(t + 1) * P], row_e[b][:, t, :], g.ident[:])
                mm.then_inc(s_turn, 1)

            def mm_h1(k, q, b):
                ge(pe, s_h1r, k)
                pe.wait_ge(s_turned, k + 1)
                pe.wait_ge(s_dst, k + 1)
                tick(pe, s_tick)
                pe.matmul(p_h1[0:32, :], g.we1_edge[:], edge_t[b % 2][:], start=True, stop=False)
                pe.matmul(p_h1[0:32, :], dst[b % 2][:, 0:32], hot_t[b % 2][:], start=False, stop=False)
                for t in range(TILES):
                    mm = pe.matmul(p_h1[0:32, t * P:(t + 1) * P], row_s[b][:, t, :], g.ident[:],
                                   start=False, stop=(t == TILES - 1))
                mm.then_inc(s_h1, 1)

            def mm_em(k, q, b):
                ge(pe, s_emr, k)
                pe.wait_ge(s_h1r, k + 1)
                tick(pe, s_tick)
                pe.matmul(p_em[:], g.we2[:], h1[b % 2][:], start=True, stop=True).then_inc(s_em, 1)

            def mm_h2(k, q, b):
                ge(pe, s_h2r, k)
                pe.wait_ge(s_emr, k + 1)
                pe.matmul(p_h2[0:EDGE_D, :], g.wn1_msg[:], em[b % 2][:], start=True, stop=False)
                pe.matmul(p_h2[0:EDGE_D, :], dst[b % 2][:, 32:96], hot_t[b % 2][:],
                          start=False, stop=True).then_inc(s_h2, 1)

            def mm_nm(k, q, b):
                ge(pe, s_nmr, k)
                pe.wait_ge(s_h2r, k + 1)
                tick(pe, s_tick)
                for t in range(TILES):
                    mm = pe.matmul(p_nm[:, t * P:(t + 1) * P], h2[b % 2][:, t * P:(t + 1) * P], g.wn2b[:],
                                   start=True, stop=True)
                mm.then_inc(s_nm, 1)

            def mm_sum(k, q, b):
                ge(pe, s_acc, k)
                pe.wait_ge(s_nmr, k + 1)
                for t in range(TILES):
                    mm = pe.matmul(p_sum[:, 0:D], hot[b][:, t, :], nm[b % 2][:, t, :],
                                   start=(t == 0), stop=(t == TILES - 1))
                mm.then_inc(s_sum, 1)

            pipeline(pe, [(0, turn), (1, mm_h2), (0, mm_h1), (1, mm_nm), (0, mm_em), (1, mm_sum)])

        @block.vector
        def _(v):
            v.wait_ge(s_init, 3)

            def make_hot(k, q, b):
                ge(v, s_sum, k - (UNROLL - 1))
                v.tensor_tensor(hot[b][:], g.iota[:].unsqueeze(1).broadcast_to([P, TILES, P]), rec_f(g.rec_d, k),
                                ALU.is_equal).then_inc(s_hot, 1)

            def bring_dst(k, q, b):
                ge(v, s_h2, k - 1)
                a = bin_register(v, g.bin_d, k, s_tick)
                v.tensor_copy(dst[b % 2][:].unsqueeze(1), g.dst0[:, bass.ds(a, 1), :]).then_inc(s_dst, 1)

            def nm_relu(k, q, b):
                v.wait_ge(s_nm, k + 1)
                ge(v, s_sum, k - 1)
                v.tensor_scalar_max(nm[b % 2][:].rearrange("p t f -> p (t f)"), p_nm[:], 0.0).then_inc(s_nmr, 1)

            pipeline(v, [(0, make_hot), (0, bring_dst), (2, nm_relu),
                         (2, add_sum(v, g, g.bin_d, p_sum, D, 1, s_sum, s_acc, s_tick))])


def bin_register(v, bin_of, k, s_tick):
    tick(v, s_tick)
    return v.value_load(bin_of[0:1, bass.ds(k, 1)], min_val=0, max_val=N_BINS - 1)


def add_sum(v, g, bin_of, p_sum, width, ring, s_sum, s_acc, s_tick):
    def fn(k, q, b):
        bank = p_sum if ring == 1 else p_sum[b % ring]
        v.wait_ge(s_sum, k + 1)
        ge(v, s_acc, k)
        a = bin_register(v, bin_of, k, s_tick)
        there = g.acc[:, bass.ds(a, 1), 0:width]
        v.tensor_tensor(there, there, bank[:, 0:width].unsqueeze(1), ALU.add).then_inc(s_acc, 1)
    return fn


def finish(nc, g, layer, out=None):
    with Core(nc, f"f{layer}") as c:
        s_v, s_o = c.sem("v"), c.sem("o")
        block = c.block()

        @block.vector
        def _(v):
            ch = Chain(v, s_v)
            if layer in (1, 2):
                heads = 4 if layer == 1 else 8
                f = D // heads
                acc = g.acc[:, :, 0:heads * (f + 1)].rearrange("p a (h f) -> p a h f", h=heads)
                den = g.den[:, :, 0:heads]
                tmp = g.TMP[:].rearrange("p a (h f) -> p a h f", h=heads)
                ch.do(v.scalar_tensor_tensor(den, acc[:, :, :, f], 0.0, acc[:, :, :, f], ALU.is_equal, ALU.add))
                ch.do(v.reciprocal(den, den))
                for a in range(N_BINS):
                    ins = v.tensor_tensor(tmp[:, a], acc[:, a, :, 0:f],
                                          den[:, a, :].unsqueeze(2).broadcast_to([P, heads, f]), ALU.mult)
                ch.do(ins)
                if layer == 2:
                    ch.do(v.tensor_tensor(g.TMP[:], g.TMP[:],
                                          g.bias2[:].unsqueeze(1).broadcast_to([P, N_BINS, D]), ALU.add))
                ch.do(v.tensor_tensor(g.X[:], g.X[:], g.TMP[:], ALU.add))
            else:
                ch.do(v.tensor_tensor(g.X[:], g.X[:], g.acc[:, :, 0:D], ALU.add))
            n_done[0] = ch.n

        if out is not None:
            @block.sync
            def _(sp):
                sp.wait_ge(s_v, n_done[0])
                sp.dma_start(out[0:FULL * P, :].rearrange("(a b) f -> b a f", b=P), g.X[:, 0:FULL, :]).then_inc(s_o, 16)
                sp.dma_start(out[FULL * P:N_NODES, :], g.X[0:LAST, FULL, :]).then_inc(s_o, 16)
                sp.wait_ge(s_o, 32)


n_done = [0]


def relation_sum(nc, g):
    with Core(nc, "rel") as c:
        hot = [c.sb(f"hot{b}", [P, TILES, P]) for b in range(UNROLL)]
        index = [c.sb(f"index{b}", [P, 1, TILES], I32) for b in range(UNROLL)]
        row = [c.sb(f"row{b}", [P, TILES, D]) for b in range(UNROLL)]
        p_sum = [c.ps(f"sum{b}") for b in range(2)]
        s_g, s_tick = c.sems("g", UNROLL), c.sem("tick")
        s_ix, s_init, s_hot, s_sum, s_acc = (c.sem(n) for n in "ix init hot sum acc".split())
        block = c.block()
        io = (g.rec_s, (0,), index, (row,), (g.tab3,), s_ix, s_g, s_tick, s_sum)

        @block.gpsimd
        def _(gp):
            gp.memset(g.acc[:, :, 0:D], 0.0).then_inc(s_init, 1)
            pipeline(gp, [(0, gather_stages(None, gp, *io)[1])])

        @block.scalar
        def _(act):
            pipeline(act, [(0, gather_stages(act, None, *io)[0])])

        @block.tensor
        def _(pe):
            def mm_sum(k, q, b):
                ge(pe, s_acc, k - 1)
                pe.wait_ge(s_hot, k + 1)
                pe.wait_ge(s_g[b], 16 * TILES * (q + 1))
                for t in range(TILES):
                    mm = pe.matmul(p_sum[b % 2][:, 0:D], hot[b][:, t, :], row[b][:, t, :],
                                   start=(t == 0), stop=(t == TILES - 1))
                mm.then_inc(s_sum, 1)
            pipeline(pe, [(0, mm_sum)])

        @block.vector
        def _(v):
            v.wait_ge(s_init, 1)

            def make_hot(k, q, b):
                ge(v, s_sum, k - (UNROLL - 1))
                v.tensor_tensor(hot[b][:], g.iota[:].unsqueeze(1).broadcast_to([P, TILES, P]), rec_f(g.rec_s, k),
                                ALU.is_equal).then_inc(s_hot, 1)
            pipeline(v, [(0, make_hot), (1, add_sum(v, g, g.bin_s, p_sum, D, 2, s_sum, s_acc, s_tick))])


def segment_max(nc, g, staged):
    HEADS, W = 4, 132
    with Core(nc, "max") as c:
        hot = [c.sb(f"hot{b}", [P, TILES, P]) for b in range(UNROLL)]
        index = [c.sb(f"index{b}", [P, 1, TILES], I32) for b in range(UNROLL)]
        row = [c.sb(f"row{b}", [P, TILES, W]) for b in range(UNROLL)]
        mask = [c.sb(f"mask{b}", [P, BLOCK]) for b in range(2)]
        junk = c.sb("junk", [P, HEADS, BLOCK])
        top = [c.sb(f"top{b}", [P, HEADS]) for b in range(UNROLL)]
        p_hot = [c.ps(f"hot{b}") for b in range(2)]
        p_s = [c.ps(f"s{h}") for h in range(HEADS)]
        s_g, s_st, s_tick = c.sems("g", UNROLL), c.sems("st", UNROLL), c.sem("tick")
        s_ix, s_init, s_hot, s_turn, s_mask, s_all, s_red, s_top = (
            c.sem(n) for n in "ix init hot turn mask all red top".split())
        s_used = c.sem("used")
        block = c.block()
        io = (g.rec_d, (0,), index, (row,), (g.tab1,), s_ix, s_g, s_tick, s_used)

        @block.gpsimd
        def _(gp):
            gp.memset(g.top[:], -BIG).then_inc(s_init, 1)
            pipeline(gp, [(0, gather_stages(None, gp, *io)[1])])

        @block.sync
        def _(sp):
            def keep(k, q, b):
                sp.wait_ge(s_g[b], 16 * TILES * (q + 1))
                sp.dma_start(staged[bass.ds(k, 1)].rearrange("k p f -> (k p) f"),
                             row[b][:].rearrange("p t f -> p (t f)")).then_inc(s_st[b], 16)

            def kept(k, q, b):
                sp.wait_ge(s_st[b], 16 * (q + 1))
                tick(sp, s_tick)
                sp.wait_ge(s_all, HEADS * (k + 1))
                sp.sem_inc(s_used, 1)
            pipeline(sp, [(0, keep), (1, kept)])

        @block.scalar
        def _(act):
            lay = gather_stages(act, None, *io)[0]

            def make_mask(k, q, b):
                act.wait_ge(s_turn, k + 1)
                ge(act, s_red, HEADS * (k - 1))
                act.activation(mask[b % 2][:], p_hot[b % 2][:], ACT.Copy, scale=BIG, bias=-BIG).then_inc(s_mask, 1)
            pipeline(act, [(0, lay), (2, make_mask)])

        @block.tensor
        def _(pe):
            def turn(k, q, b):
                ge(pe, s_mask, k - 1)
                pe.wait_ge(s_hot, k + 1)
                for t in range(TILES):
                    mm = pe.transpose(p_hot[b % 2][:, t * P:(t + 1) * P], hot[b][:, t, :], g.ident[:])
                mm.then_inc(s_turn, 1)

            def spread(k, q, b):
                pe.wait_ge(s_g[b], 16 * TILES * (q + 1))
                for h in range(HEADS):
                    ge(pe, s_red, HEADS * (k - 1) + h + 1)
                    for t in range(TILES):
                        at = h * 33 + 32
                        mm = pe.transpose(p_s[h][:, t * P:(t + 1) * P],
                                          row[b][:, t, at:at + 1].broadcast_to([P, P]), g.ident[:])
                    mm.then_inc(s_all, 1)
            pipeline(pe, [(0, turn), (1, spread)])

        @block.vector
        def _(v):
            v.wait_ge(s_init, 1)

            def make_hot(k, q, b):
                ge(v, s_turn, k - (UNROLL - 1))
                v.tensor_tensor(hot[b][:], g.iota[:].unsqueeze(1).broadcast_to([P, TILES, P]), rec_f(g.rec_d, k),
                                ALU.is_equal).then_inc(s_hot, 1)

            def reduce(k, q, b):
                v.wait_ge(s_mask, k + 1)
                ge(v, s_top, k - (UNROLL - 1))
                for h in range(HEADS):
                    v.wait_ge(s_all, HEADS * k + h + 1)
                    ge(v, s_red, HEADS * (k - 1) + h + 1)
                    tick(v, s_tick)
                    v.tensor_tensor_reduce(out=junk[:, h, :], in0=mask[b % 2][:], in1=p_s[h][:], scale=1.0,
                                           scalar=-BIG, op0=ALU.add, op1=ALU.max,
                                           accum_out=top[b][:, h:h + 1]).then_inc(s_red, 1)

            def keep_top(k, q, b):
                v.wait_ge(s_red, HEADS * (k + 1))
                ge(v, s_top, k)
                a = bin_register(v, g.bin_d, k, s_tick)
                there = g.top[:, bass.ds(a, 1), :]
                v.tensor_tensor(there, there, top[b][:].unsqueeze(1), ALU.max).then_inc(s_top, 1)
            pipeline(v, [(0, make_hot), (1, reduce), (2, keep_top)])


def target_terms(nc, g):
    H = 4
    with Core(nc, "tt") as c:
        low = c.sb("low", [P, N_BINS, H])
        ex = c.sb("ex", [P, N_BINS, H])
        s_v, s_lo, s_ex = c.sem("v"), c.sem("lo"), c.sem("ex")
        block = c.block()

        @block.vector
        def _(v):
            ch = Chain(v, s_v)
            top = g.tgt[:, :, H:2 * H]
            ch.do(v.tensor_tensor(top, g.top[:], g.tgt[:, :, 0:H], ALU.add))
            ch.do(v.tensor_single_scalar(low[:], top, 0.0, ALU.min))
            v.sem_inc(s_lo, 1)
            v.wait_ge(s_ex, 1)
            ch.do(v.tensor_scalar(ex[:], ex[:], 0.2, -0.2, ALU.mult, ALU.add))
            ch.do(v.scalar_tensor_tensor(top, top, 0.0, ex[:], ALU.max, ALU.add))

        @block.scalar
        def _(act):
            act.wait_ge(s_lo, 1)
            act.activation(ex[:], low[:], ACT.Exp).then_inc(s_ex, 1)


def attention_sum(nc, g, layer, staged):
    heads = 4 if layer == 1 else 8
    f = D // heads
    W = heads * (f + 1)
    T = 2 * heads if layer == 1 else heads
    with Core(nc, f"att{layer}") as c:
        hot = [c.sb(f"hot{b}", [P, TILES, P]) for b in range(UNROLL)]
        index = [c.sb(f"index{b}", [P, 1, TILES], I32) for b in range(UNROLL)]
        row = [c.sb(f"row{b}", [P, TILES, heads, f + 1]) for b in range(UNROLL)]
        hot_t = [c.sb(f"hot_t{b}", [P, BLOCK]) for b in range(2)]
        tgt = [c.sb(f"tgt{b}", [P, T]) for b in range(2)]
        val = [c.sb(f"val{b}", [P, TILES, heads]) for b in range(2)]
        low = [c.sb(f"low{b}", [P, TILES, heads]) for b in range(2)]
        neg = [c.sb(f"neg{b}", [P, TILES, heads]) for b in range(2)]
        wgt = [c.sb(f"wgt{b}", [P, TILES, heads]) for b in range(2)]
        p_hot = [c.ps(f"hot{b}") for b in range(2)]
        p_t = [c.ps(f"t{b}") for b in range(2)]
        p_sum = [c.ps(f"sum{b}") for b in range(2)]
        s_g, s_tick = c.sems("g", UNROLL), c.sem("tick")
        (s_ix, s_init, s_hot, s_turn, s_turned, s_tgt, s_t, s_v1, s_v2, s_neg, s_v3, s_v4, s_val, s_wgt, s_msg,
         s_sum, s_acc) = (c.sem(n) for n in
                          "ix init hot turn turned tgt t v1 v2 neg v3 v4 val wgt msg sum acc".split())
        block = c.block()
        lands = 16 if layer == 1 else 16 * TILES
        flat = [r[:].rearrange("p t h f -> p t (h f)") for r in row]
        io = (g.rec_d, (0,), index, (flat,), (g.tab2,), s_ix, s_g, s_tick, s_sum)

        @block.gpsimd
        def _(gp):
            gp.memset(g.acc[:, :, 0:W], 0.0).then_inc(s_init, 1)
            if layer == 2:
                pipeline(gp, [(0, gather_stages(None, gp, *io)[1])])

        if layer == 1:
            @block.sync
            def _(sp):
                def load(k, q, b):
                    ge(sp, s_sum, k - (UNROLL - 1))
                    sp.dma_start(row[b][:].rearrange("p t h f -> p (t h f)"),
                                 staged[bass.ds(k, 1)].rearrange("k p f -> (k p) f")).then_inc(s_g[b], 16)
                pipeline(sp, [(0, load)])

        @block.scalar
        def _(act):
            lay = gather_stages(act, None, *io)[0]

            def turned(k, q, b):
                act.wait_ge(s_turn, k + 1)
                ge(act, s_t, k - 1)
                act.copy(hot_t[b % 2][:], p_hot[b % 2][:]).then_inc(s_turned, 1)

            def negative(k, q, b):
                act.wait_ge(s_v2, k + 1)
                ge(act, s_v4, k - 1)
                act.activation(neg[b % 2][:], low[b % 2][:], ACT.Exp).then_inc(s_neg, 1)

            def weight(k, q, b):
                act.wait_ge(s_val, k + 1)
                ge(act, s_msg, k - 1)
                act.activation(wgt[b % 2][:], val[b % 2][:], ACT.Exp).then_inc(s_wgt, 1)
            if layer == 1:
                pipeline(act, [(0, turned), (1, negative), (1, weight)])
            else:
                pipeline(act, [(0, lay), (2, turned), (3, weight)])

        @block.tensor
        def _(pe):
            def turn(k, q, b):
                ge(pe, s_turned, k - 1)
                pe.wait_ge(s_hot, k + 1)
                for t in range(TILES):
                    mm = pe.transpose(p_hot[b % 2][:, t * P:(t + 1) * P], hot[b][:, t, :], g.ident[:])
                mm.then_inc(s_turn, 1)

            def take(k, q, b):
                ge(pe, s_val, k - 1)
                pe.wait_ge(s_turned, k + 1)
                pe.wait_ge(s_tgt, k + 1)
                for t in range(TILES):
                    mm = pe.matmul(p_t[b % 2][:, t * T:(t + 1) * T], hot_t[b % 2][:, t * P:(t + 1) * P],
                                   tgt[b % 2][:], start=True, stop=True)
                mm.then_inc(s_t, 1)

            def mm_sum(k, q, b):
                ge(pe, s_acc, k - 1)
                pe.wait_ge(s_msg, k + 1)
                for t in range(TILES):
                    mm = pe.matmul(p_sum[b % 2][:, 0:W], hot[b][:, t, :], flat[b][:, t, :],
                                   start=(t == 0), stop=(t == TILES - 1))
                mm.then_inc(s_sum, 1)
            pipeline(pe, [(0, turn), (1, take), (2, mm_sum)])

        @block.vector
        def _(v):
            v.wait_ge(s_init, 1)

            def make_hot(k, q, b):
                ge(v, s_sum, k - (UNROLL - 1))
                v.tensor_tensor(hot[b][:], g.iota[:].unsqueeze(1).broadcast_to([P, TILES, P]), rec_f(g.rec_d, k),
                                ALU.is_equal).then_inc(s_hot, 1)

            def bring_tgt(k, q, b):
                ge(v, s_t, k - 1)
                a = bin_register(v, g.bin_d, k, s_tick)
                v.tensor_copy(tgt[b % 2][:].unsqueeze(1), g.tgt[:, bass.ds(a, 1), 0:T]).then_inc(s_tgt, 1)

            def score(k, q, b):
                v.wait_ge(s_g[b], lands * (q + 1))
                v.wait_ge(s_t, k + 1)
                ge(v, s_wgt, k - 1)
                there = p_t[b % 2][:, 0:TILES * T].rearrange("p (t w) -> p t w", t=TILES)
                v.tensor_tensor(val[b % 2][:], row[b][:, :, :, f], there[:, :, 0:heads], ALU.add).then_inc(s_v1, 1)
                v.wait_ge(s_v1, k + 1)
                if layer == 1:
                    v.tensor_scalar_min(low[b % 2][:], val[b % 2][:], 0.0).then_inc(s_v2, 1)
                    v.wait_ge(s_neg, k + 1)
                    v.tensor_scalar(neg[b % 2][:], neg[b % 2][:], 0.2, -0.2, ALU.mult, ALU.add).then_inc(s_v3, 1)
                    v.wait_ge(s_v3, k + 1)
                    v.scalar_tensor_tensor(val[b % 2][:], val[b % 2][:], 0.0, neg[b % 2][:],
                                           ALU.max, ALU.add).then_inc(s_v4, 1)
                    v.wait_ge(s_v4, k + 1)
                    v.tensor_tensor(val[b % 2][:], val[b % 2][:], there[:, :, heads:T], ALU.subtract).then_inc(s_val, 1)
                else:
                    v.scalar_tensor_tensor(val[b % 2][:], val[b % 2][:], 0.2, val[b % 2][:],
                                           ALU.mult, ALU.max).then_inc(s_val, 1)

            def message(k, q, b):
                v.wait_ge(s_wgt, k + 1)
                w = wgt[b % 2][:]
                v.tensor_copy(row[b][:, :, :, f], w)
                for t in range(TILES):
                    ins = v.tensor_tensor(row[b][:, t, :, 0:f], row[b][:, t, :, 0:f],
                                          wgt[b % 2][:, t, :].unsqueeze(2).broadcast_to([P, heads, f]), ALU.mult)
                ins.then_inc(s_msg, 1)

            pipeline(v, [(0, make_hot), (0, bring_tgt), (1, score), (1, message),
                         (2, add_sum(v, g, g.bin_d, p_sum, W, 2, s_sum, s_acc, s_tick))])


class Shared:
    pass


def graph_layers(nc, args, out):
    g = Shared()
    with ExitStack() as ctx:
        def sb(name, shape, dt=F32):
            return ctx.enter_context(nc.sbuf_tensor(name, shape, dt))

        def dram(name, shape, dt=F32):
            return nc.dram_tensor(name, shape, dt).ap()

        g.ident, g.ones, g.earlier = sb("ident", [P, P]), sb("ones", [P, P]), sb("earlier", [P, P])
        g.iota, g.iota_blocks = sb("iota", [P, P]), sb("iota_blocks", [1, N_BLOCKS])
        g.rec_d, g.rec_s = sb("rec_d", [P, N_POS // P, DW], I32), sb("rec_s", [P, N_POS // P, SW], I32)
        g.bin_d, g.bin_s = sb("bin_d", [1, N_BLOCKS], I32), sb("bin_s", [1, N_BLOCKS], I32)
        rec_d_dram, rec_s_dram = dram("rec_d_dram", [N_POS, DW], I32), dram("rec_s_dram", [N_POS, SW], I32)
        constants(nc, g)
        sort_edges(nc, g, "by_d", args["dst"], [("load", args["src"]), ("local",), ("id",), ("zero",)], DW,
                   rec_d_dram, g.rec_d, g.bin_d)
        sort_edges(nc, g, "by_s", args["src"], [("pair", args["dst"], args["type"]), ("local",)], SW,
                   rec_s_dram, g.rec_s, g.bin_s)

        g.X, g.H, g.TMP = (sb(n, [P, N_BINS, D]) for n in ("X", "H", "TMP"))
        g.mu, g.var, g.std = (sb(n, [P, N_BINS]) for n in ("mu", "var", "std"))
        g.acc = sb("acc", [P, N_BINS, 136])
        g.den, g.tgt, g.top = sb("den", [P, N_BINS, 8]), sb("tgt", [P, N_BINS, 8]), sb("top", [P, N_BINS, 4])
        g.we1_src, g.we1_dst, g.we1_edge = sb("we1_src", [D, 32]), sb("we1_dst", [D, 32]), sb("we1_edge", [EDGE_D, 32])
        g.we2, g.wn1_dst, g.wn1_msg = sb("we2", [32, D]), sb("wn1_dst", [D, 64]), sb("wn1_msg", [D, 64])
        g.wn2b, g.be2, g.bias0 = sb("wn2b", [65, D]), sb("be2", [P, 1]), sb("bias0", [P, 96])
        g.w1, g.w2, g.w_self = sb("w1", [D, D]), sb("w2", [D, D]), sb("w_self", [D, D])
        g.a1, g.a2, g.bias2 = sb("a1", [P, 2, D]), sb("a2", [P, 2, D]), sb("bias2", [P, D])
        g.bases, g.coef = sb("bases", [D, N_BASES, D]), sb("coef", [P, N_REL * N_BASES])
        g.dst0 = sb("dst0", [P, N_BINS, 96])
        g.tab0, g.tab1, g.tab2 = dram("tab0", [N_ROWS, 32]), dram("tab1", [N_ROWS, 132]), dram("tab2", [N_ROWS, 136])
        g.tab3 = dram("tab3", [N_ROWS * N_REL, D])
        staged = dram("staged", [N_BLOCKS, P, TILES * 132])
        setup(nc, g, args)
        node_phase(nc, g, 0, g.tab0)
        edge_mlp(nc, g, args["edge_attr"])
        finish(nc, g, 0)
        node_phase(nc, g, 1, g.tab1)
        segment_max(nc, g, staged)
        target_terms(nc, g)
        attention_sum(nc, g, 1, staged)
        finish(nc, g, 1)
        node_phase(nc, g, 2, g.tab2)
        attention_sum(nc, g, 2, None)
        finish(nc, g, 2)
        node_phase(nc, g, 3, g.tab3)
        relation_sum(nc, g)
        finish(nc, g, 3, out)


_INS = {
    "x": "x", "src": "src", "dst": "dst", "edge_attr": "edge_attr_64", "type": "edge_type_16",
    "We1": "L0_gnn_We1", "be1": "L0_gnn_be1", "We2": "L0_gnn_We2", "be2": "L0_gnn_be2",
    "Wn1": "L0_gnn_Wn1", "bn1": "L0_gnn_bn1", "Wn2": "L0_gnn_Wn2", "bn2": "L0_gnn_bn2",
    "W1": "L1_gnn_W", "a_src": "L1_gnn_a_src", "a_tgt": "L1_gnn_a_tgt",
    "W2": "L2_gnn_W", "a_left": "L2_gnn_a_left", "a_right": "L2_gnn_a_right", "bias": "L2_gnn_bias",
    "bases": "L3_gnn_bases", "coefficients": "L3_gnn_coefficients", "w_self": "L3_gnn_w_self",
}


def kernel(**inputs):
    import numpy as _np
    import concourse.bacc as _bacc
    from concourse import mybir as _mybir
    from concourse.bass_utils import run_bass_kernel_spmd as _run

    nc = _bacc.Bacc("TRN2", target_bir_lowering=False, num_devices=1)
    arrays, args = {}, {}
    for short, name in _INS.items():
        a = _np.ascontiguousarray(inputs[name])
        arrays[f"in_{name}"] = a
        args[short] = nc.dram_tensor(f"in_{name}", a.shape, _mybir.dt.from_np(a.dtype), kind="ExternalInput").ap()
    out = nc.dram_tensor("out_x", (N_NODES, D), F32, kind="ExternalOutput").ap()
    graph_layers(nc, args, out)
    r = _run(nc, [arrays], core_ids=[0])
    return r.results[0]["out_x"]
```

```python
from contextlib import ExitStack

import concourse.bass as bass
from concourse import mybir

ALU = mybir.AluOpType
ACT = mybir.ActivationFunctionType
AX = mybir.AxisListType
F32 = mybir.dt.float32
I32 = mybir.dt.int32

P = 128
N_NODES = 3125
N_BINS = -(-N_NODES // P)
N_ROWS = N_BINS * P
FULL = N_NODES // P
LAST = N_NODES - FULL * P
D = 128
N_EDGES = 100000
SORT_P = 125
SORT_J = N_EDGES // SORT_P
TILES = 4
BLOCK = TILES * P
N_BLOCKS = (N_EDGES + N_BINS * (BLOCK - 1)) // BLOCK
UNROLL = 10
N_BLOCKS = -(-N_BLOCKS // UNROLL) * UNROLL
N_POS = N_BLOCKS * BLOCK
EDGE_D = 64
N_REL, N_BASES = 16, 8
HID1, HID2 = 32, 64
IN_D = EDGE_D + HID1
EPS = 1e-5
BIG = 1e30
DW = 4
SW = 2


def pipeline(eng, stages):
    deepest = max(lag for lag, _ in stages)
    head = -(-(deepest + UNROLL) // UNROLL) * UNROLL

    def step(k):
        for lag, fn in stages:
            if 0 <= k - lag < N_BLOCKS:
                fn(k - lag, (k - lag) // UNROLL, (k - lag) % UNROLL)

    for k in range(head):
        step(k)
    with eng.Fori(head // UNROLL, N_BLOCKS // UNROLL) as i:
        for c in range(UNROLL):
            for lag, fn in stages:
                at = c - lag
                fn(i * UNROLL + at, i + at // UNROLL, at % UNROLL)
    for k in range(N_BLOCKS, N_BLOCKS + deepest):
        step(k)


class Shared:
    pass


class Chain:

    def __init__(self, eng, sem):
        self.eng, self.sem, self.n = eng, sem, 0

    def do(self, ins):
        self.n += 1
        ins.then_inc(self.sem, 1)
        self.eng.wait_ge(self.sem, self.n)


class Core:

    def __init__(self, nc, tag):
        self.nc, self.tag, self.ctx, self.taken = nc, tag, ExitStack(), []

    def __enter__(self):
        return self

    def __exit__(self, kind, *a):
        if kind is None:
            self.ctx.close()
            self.nc.clear_and_free_semaphores(self.taken)
            self.nc.all_engine_barrier()

    def sb(self, name, shape, dt=F32):
        return self.ctx.enter_context(self.nc.sbuf_tensor(f"{self.tag}_{name}", shape, dt))

    def ps(self, name, shape=(P, 512)):
        return self.ctx.enter_context(self.nc.psum_tensor(f"{self.tag}_ps_{name}", list(shape), F32))

    def sem(self, name):
        self.taken.append(self.nc.alloc_semaphore(name=f"{self.tag}_s_{name}"))
        return self.taken[-1]

    def sems(self, name, n):
        return [self.sem(f"{name}{i}") for i in range(n)]

    def block(self):
        return self.ctx.enter_context(self.nc.Block())


def constants(nc, g):
    with Core(nc, "con") as c:
        s_c = c.sem("c")
        block = c.block()

        @block.gpsimd
        def _(gp):
            ch = Chain(gp, s_c)
            ch.do(gp.memset(g.ident[:], 0.0))
            ch.do(gp.affine_select(out=g.ident[:], in_=g.ident[:], compare_op=ALU.not_equal, fill=1.0,
                                   base=0, pattern=[[-1, P]], channel_multiplier=1))
            ch.do(gp.memset(g.ones[:], 1.0))
            ch.do(gp.affine_select(out=g.earlier[:], in_=g.ones[:], compare_op=ALU.is_gt, fill=0.0,
                                   base=0, pattern=[[1, P]], channel_multiplier=-1))
            ch.do(gp.iota(g.iota[:], pattern=[[1, P]], base=0, channel_multiplier=0,
                          allow_small_or_imprecise_dtypes=True))
            ch.do(gp.iota(g.iota_blocks[:], pattern=[[1, N_BLOCKS]], base=0, channel_multiplier=0,
                          allow_small_or_imprecise_dtypes=True))


def setup(nc, g, args):
    with Core(nc, "set") as c:
        s_w, s_x, s_z = c.sem("w"), c.sem("x"), c.sem("z")
        block = c.block()
        loads = [
            (g.we1_src[:], args["We1"][0:D, :]), (g.we1_dst[:], args["We1"][D:2 * D, :]),
            (g.we1_row[0:EDGE_D, :], args["We1"][2 * D:2 * D + EDGE_D, :]), (g.we2[:], args["We2"]),
            (g.wn1_dst[:], args["Wn1"][0:D, :]), (g.wn1_msg[:], args["Wn1"][D:2 * D, :]),
            (g.wn2b[0:64, :], args["Wn2"]), (g.wn2b[64:65, :], args["bn2"].unsqueeze(0)),
            (g.be2[:], args["be2"].unsqueeze(1)),
            (g.bias0[:, 0:HID2], args["bn1"].partition_broadcast(P)),
            (g.bias0[:, HID2:IN_D], args["be1"].partition_broadcast(P)),
            (g.w1[:], args["W1"]), (g.w2[:], args["W2"]),
            (g.a1[:, 0, :], args["a_src"].rearrange("h f -> (h f)").partition_broadcast(P)),
            (g.a1[:, 1, :], args["a_tgt"].rearrange("h f -> (h f)").partition_broadcast(P)),
            (g.a2[:, 0, :], args["a_left"].rearrange("c h -> (c h)").partition_broadcast(P)),
            (g.a2[:, 1, :], args["a_right"].rearrange("c h -> (c h)").partition_broadcast(P)),
            (g.bias2[:], args["bias"].partition_broadcast(P)),
            (g.bases[:], args["bases"].rearrange("b i o -> i b o")),
            (g.coef[:], args["coefficients"].rearrange("r b -> (r b)").partition_broadcast(P)),
            (g.w_self[:], args["w_self"]),
            (g.X[:, 0:FULL, :], args["x"][0:FULL * P, :].rearrange("(a b) f -> b a f", b=P)),
        ]

        @block.vector
        def _(v):
            v.memset(g.X[:, FULL, :], 0.0).then_inc(s_z, 1)
            v.tensor_copy(g.we1_row[EDGE_D:IN_D, :], g.ident[EDGE_D:IN_D, EDGE_D:IN_D]).then_inc(s_z, 1)

        @block.sync
        def _(sp):
            for dst, src in loads:
                sp.dma_start(dst, src).then_inc(s_w, 16)
            sp.wait_ge(s_z, 2)
            sp.dma_start(g.X[0:LAST, FULL, :], args["x"][FULL * P:N_NODES, :]).then_inc(s_x, 16)
            sp.wait_ge(s_w, 16 * len(loads))
            sp.wait_ge(s_x, 16)


def bin_counts(v, ch, sort, key_i):
    ch.do(v.tensor_single_scalar(sort.bin_i[:], key_i[:], P.bit_length() - 1, ALU.logical_shift_right))
    ch.do(v.tensor_copy(sort.bin_f[:], sort.bin_i[:]))
    for a in range(N_BINS):
        ch.do(v.tensor_single_scalar(sort.hot[:], sort.bin_f[:], float(a), ALU.is_equal))
        ch.do(v.tensor_tensor_scan(sort.rank[:, a, :], sort.hot[:], sort.hot[:], 0.0, ALU.add, ALU.max))
    ch.do(v.tensor_copy(sort.counts[:, 0:N_BINS], sort.rank[:, :, SORT_J - 1]))


def block_tables(v, ch, g, sort, bins_i, bins_f, starts):
    total = sort.p_total[:, 0:N_BINS]
    ch.do(v.tensor_single_scalar(sort.upto[:], total, float(BLOCK - 1), ALU.add))
    ch.do(v.tensor_copy(sort.blocks_i[:], sort.upto[:]))
    ch.do(v.tensor_single_scalar(sort.blocks_i[:], sort.blocks_i[:], BLOCK.bit_length() - 1,
                                 ALU.logical_shift_right))
    ch.do(v.tensor_copy(sort.blocks[:], sort.blocks_i[:]))
    ch.do(v.tensor_tensor_scan(sort.upto[:], sort.blocks[:], sort.blocks[:], 0.0, ALU.add, ALU.max))
    ch.do(v.tensor_tensor(sort.base[:], sort.upto[:], sort.blocks[:], ALU.subtract))
    ch.do(v.tensor_scalar(sort.base[:], sort.base[:], float(BLOCK), -1.0, ALU.mult, ALU.add))
    ch.do(v.tensor_tensor(sort.base[0:SORT_P, :], sort.base[0:SORT_P, :], sort.p_before[0:SORT_P, 0:N_BINS],
                          ALU.add))
    ch.do(v.memset(bins_f[:], 0.0))
    for a in range(N_BINS - 1):
        ch.do(v.scalar_tensor_tensor(bins_f[:], g.iota_blocks[:], sort.upto[:, a:a + 1], bins_f[:],
                                     ALU.is_ge, ALU.add))
    ch.do(v.tensor_copy(bins_i[:], bins_f[0:1, :]))
    if starts is None:
        return
    ch.do(v.scalar_tensor_tensor(sort.step[:], sort.blocks[:], float(-BLOCK), total, ALU.mult, ALU.add))
    ch.do(v.tensor_single_scalar(sort.step[:, N_BINS - 1:N_BINS], sort.step[:, N_BINS - 1:N_BINS],
                                 float(N_POS), ALU.add))
    ch.do(v.tensor_single_scalar(starts[:], g.iota_blocks[:], float(BLOCK), ALU.mult))
    for a in range(N_BINS):
        ch.do(v.tensor_scalar(sort.past[:], g.iota_blocks[:], sort.upto[:, a:a + 1], sort.step[:, a:a + 1],
                              ALU.is_ge, ALU.mult))
        ch.do(v.tensor_tensor(starts[:], starts[:], sort.past[:], ALU.add))


def positions(v, ch, sort):
    ch.do(v.memset(sort.pos[:], 0.0))
    for a in range(N_BINS):
        ch.do(v.tensor_scalar(sort.rank[:, a, :], sort.rank[:, a, :], sort.base[0:SORT_P, a:a + 1], None, ALU.add))
        ch.do(v.scalar_tensor_tensor(sort.pick[:], sort.bin_f[:], float(a), sort.rank[:, a, :],
                                     ALU.is_equal, ALU.mult))
        ch.do(v.tensor_tensor(sort.pos[:], sort.pos[:], sort.pick[:], ALU.add))


def as_blocks(rec_dram):
    return rec_dram.rearrange("(k p t) w -> p k (t w)", p=P, t=TILES)


def order_edges(nc, g, args, edges_dram, rec_d_dram, rec_s_dram):
    with Core(nc, "ord") as c:
        sort = Shared()
        src_i, dst_i, type_i = (c.sb(n, [SORT_P, SORT_J], I32) for n in ("src_i", "dst_i", "type_i"))
        next_i = c.sb("next_i", [SORT_P, 1], I32)
        dst_f, next_f = c.sb("dst_f", [SORT_P, SORT_J]), c.sb("next_f", [SORT_P, 1])
        src_f, id_f = c.sb("src_f", [SORT_P, SORT_J]), c.sb("id_f", [SORT_P, SORT_J])
        sort.bin_i = c.sb("bin_i", [SORT_P, SORT_J], I32)
        sort.bin_f, sort.hot, sort.pick, sort.pos = (
            c.sb(n, [SORT_P, SORT_J]) for n in ("bin_f", "hot", "pick", "pos"))
        pos_i = c.sb("pos_i", [SORT_P, SORT_J], I32)
        sort.rank = c.sb("rank", [SORT_P, N_BINS, SORT_J])
        sort.counts = c.sb("counts", [SORT_P, N_BINS + 1])
        sort.blocks_i = c.sb("blocks_i", [P, N_BINS], I32)
        sort.blocks, sort.upto, sort.base, sort.step = (
            c.sb(n, [P, N_BINS]) for n in ("blocks", "upto", "base", "step"))
        sort.past = c.sb("past", [P, N_BLOCKS])
        bins_f, starts, bins_sf = (c.sb(n, [P, N_BLOCKS]) for n in ("bins_f", "starts", "bins_sf"))
        down = c.sb("down", [SORT_P, 1])
        recs = c.sb("recs", [SORT_P, SORT_J, DW], I32)
        valid = c.sb("valid", [P, N_BLOCKS, TILES])
        sort.p_before, sort.p_total = c.ps("before"), c.ps("total")
        s_in, s_z, s_v, s_cnt, s_mm, s_flag, s_recs, s_out, s_emp, s_em, s_done, s_sc, s_ld, s_id, s_rec, s_vu = (
            c.sem(n) for n in "in z v cnt mm flag recs out emp em done sc ld id rec vu".split())
        block = c.block()
        by_edge = "(p j) -> p j"

        @block.sync
        def _(sp):
            for tile, key in ((dst_i, "dst"), (src_i, "src"), (type_i, "type")):
                sp.dma_start(tile[:], args[key].rearrange(by_edge, p=SORT_P)).then_inc(s_in, 16)
            sp.wait_ge(s_z, 1)
            sp.dma_start(next_i[0:SORT_P - 1, :],
                         args["dst"].rearrange(by_edge, p=SORT_P)[1:SORT_P, 0:1],
                         allow_slow_non_contiguous=True).then_inc(s_in, 16)
            sp.wait_ge(s_recs, 1)
            sp.dma_start(edges_dram.rearrange("(p j) w -> p (j w)", p=SORT_P),
                         recs[:].rearrange("p j w -> p (j w)")).then_inc(s_out, 16)
            sp.wait_ge(s_emp, 4)
            sp.dma_start(as_blocks(rec_s_dram), g.rec_s[:].rearrange("p (k t) w -> p k (t w)", t=TILES)
                         ).then_inc(s_em, 16)
            sp.dma_start(as_blocks(rec_d_dram), g.rec_d[:].rearrange("p (k t) w -> p k (t w)", t=TILES)
                         ).then_inc(s_em, 16)
            sp.wait_ge(s_out, 16)
            sp.wait_ge(s_em, 32)
            sp.wait_ge(s_flag, 1)
            unsorted = sp.value_load(g.unsorted[0:1, 0:1], min_val=0, max_val=1)
            with sp.If(unsorted < 1):
                with sp.Fori(0, N_BLOCKS) as k:
                    start = sp.value_load(g.start[0:1, bass.ds(k, 1)], min_val=0, max_val=N_EDGES - BLOCK)
                    sp.dma_start(g.rec_d[:, bass.ds(k * TILES, TILES), :].rearrange("p t w -> p (t w)"),
                                 edges_dram[bass.ds(start, BLOCK), :].rearrange("(p t) w -> p (t w)", p=P)
                                 ).then_inc(s_ld, 16)
                sp.wait_ge(s_ld, 16 * N_BLOCKS)
            with sp.If(unsorted > 0):
                sp.wait_ge(s_sc, 16 * SORT_J)
                sp.dma_start(g.rec_d[:].rearrange("p (k t) w -> p k (t w)", t=TILES),
                             as_blocks(rec_d_dram)).then_inc(s_ld, 16)
                sp.wait_ge(s_ld, 16)
            sp.sem_inc(s_rec, 1)

        @block.vector
        def _(v):
            ch = Chain(v, s_v)
            v.memset(next_i[:], N_NODES).then_inc(s_z, 1)
            v.wait_ge(s_in, 64)
            ch.do(v.tensor_copy(dst_f[:], dst_i[:]))
            ch.do(v.tensor_copy(next_f[:], next_i[:]))
            ch.do(v.tensor_copy(recs[:, :, 0], src_i[:]))
            ch.do(v.tensor_copy(recs[:, :, 1].bitcast(F32), dst_f[:]))
            v.wait_ge(s_id, 1)
            ch.do(v.tensor_copy(id_f[:], sort.pos[:].bitcast(I32)))
            ch.do(v.tensor_copy(recs[:, :, 3].bitcast(F32), id_f[:]))
            ch.do(v.tensor_copy(recs[:, :, 2], sort.pos[:].bitcast(I32)))
            v.sem_inc(s_recs, 1)
            ch.do(v.tensor_tensor(sort.hot[:, 0:SORT_J - 1], dst_f[:, 0:SORT_J - 1], dst_f[:, 1:SORT_J], ALU.is_gt))
            ch.do(v.tensor_tensor(sort.hot[:, SORT_J - 1:SORT_J], dst_f[:, SORT_J - 1:SORT_J], next_f[:], ALU.is_gt))
            ch.do(v.tensor_reduce(down[:], sort.hot[:], AX.X, ALU.max))
            bin_counts(v, ch, sort, dst_i)
            ch.do(v.tensor_copy(sort.counts[:, N_BINS:N_BINS + 1], down[:]))
            v.sem_inc(s_cnt, 1)
            v.wait_ge(s_mm, 2)
            block_tables(v, ch, g, sort, g.bin_d, bins_f, starts)
            ch.do(v.tensor_single_scalar(sort.past[:], starts[:], float(N_EDGES - BLOCK), ALU.min))
            ch.do(v.tensor_copy(g.start[:], sort.past[0:1, :]))
            ch.do(v.tensor_single_scalar(g.unsorted[:], sort.p_total[0:1, N_BINS:N_BINS + 1], 1.0, ALU.min))
            v.sem_inc(s_flag, 1)
            unsorted = v.value_load(g.unsorted[0:1, 0:1], min_val=0, max_val=1)
            with v.If(unsorted > 0):
                s_u = Chain(v, s_vu)
                positions(v, s_u, sort)
                s_u.do(v.tensor_copy(pos_i[:], sort.pos[:]))
                v.wait_ge(s_out, 16)
                s_u.do(v.memset(recs[:, :, 3:4].bitcast(F32), float(2 * N_POS)))
                v.sem_inc(s_done, 1)
            ch.do(v.tensor_copy(dst_f[:], dst_i[:]))
            ch.do(v.tensor_copy(src_f[:], type_i[:]))
            ch.do(v.scalar_tensor_tensor(src_f[:], dst_f[:], float(N_REL), src_f[:], ALU.mult, ALU.add))
            ch.do(v.tensor_copy(g.recs_s[:, :, 0], src_f[:]))
            ch.do(v.tensor_single_scalar(sort.bin_i[:], src_i[:], P - 1, ALU.bitwise_and))
            ch.do(v.tensor_copy(g.recs_s[:, :, 1].bitcast(F32), sort.bin_i[:]))
            bin_counts(v, ch, sort, src_i)
            v.sem_inc(s_cnt, 1)
            v.wait_ge(s_mm, 4)
            block_tables(v, ch, g, sort, g.bin_s, bins_sf, None)
            positions(v, ch, sort)
            ch.do(v.tensor_copy(g.pos_s[:], sort.pos[:]))
            v.wait_ge(s_rec, 1)
            words = g.rec_d[:].rearrange("p (k t) w -> p k t w", t=TILES)
            local, edge = words[:, :, :, 1].bitcast(F32), words[:, :, :, 3].bitcast(F32)
            wide = [P, N_BLOCKS, TILES]
            ch.do(v.tensor_tensor(valid[:], edge, starts[:].unsqueeze(2).broadcast_to(wide), ALU.is_ge))
            ch.do(v.scalar_tensor_tensor(local, bins_f[:].unsqueeze(2).broadcast_to(wide), float(-P), local,
                                         ALU.mult, ALU.add))
            ch.do(v.scalar_tensor_tensor(local, local, 1.0, valid[:], ALU.add, ALU.mult))
            ch.do(v.tensor_single_scalar(local, local, -1.0, ALU.add))

        @block.tensor
        def _(pe):
            for n, width in enumerate((N_BINS + 1, N_BINS)):
                pe.wait_ge(s_cnt, n + 1)
                pe.matmul(sort.p_before[:, 0:width], g.earlier[0:SORT_P, :], sort.counts[:, 0:width],
                          start=True, stop=True).then_inc(s_mm, 1)
                pe.matmul(sort.p_total[:, 0:width], g.ones[0:SORT_P, :], sort.counts[:, 0:width],
                          start=True, stop=True).then_inc(s_mm, 1)

        @block.gpsimd
        def _(gp):
            gp.iota(sort.pos[:].bitcast(I32), pattern=[[1, SORT_J]], base=0,
                    channel_multiplier=SORT_J).then_inc(s_id, 1)
            for n, rec in enumerate((g.rec_s, g.rec_d)):
                gp.memset(rec[:], 0).then_inc(s_emp, 1)
                gp.wait_ge(s_emp, 2 * n + 1)
                gp.memset(rec[:, :, 1:2].bitcast(F32), float(-2 * N_ROWS)).then_inc(s_emp, 1)
                gp.wait_ge(s_emp, 2 * n + 2)
            gp.wait_ge(s_flag, 1)
            unsorted = gp.value_load(g.unsorted[0:1, 0:1], min_val=0, max_val=1)
            with gp.If(unsorted > 0):
                gp.wait_ge(s_done, 1)
                gp.wait_ge(s_em, 32)
                for j in range(SORT_J):
                    gp.indirect_dma_start(rec_d_dram, bass.IndirectOffsetOnAxis(pos_i[:, j:j + 1], axis=0),
                                          recs[:, j, :], None).then_inc(s_sc, 16)


def layer_norm(v, ch, g, c, s_var, s_std, act_done):
    full = [P, N_BINS, D]
    ch.do(v.tensor_reduce(g.mu[:], g.X[:], AX.X, ALU.add))
    ch.do(v.tensor_single_scalar(g.mu[:], g.mu[:], 1.0 / D, ALU.mult))
    ch.do(v.tensor_tensor(g.H[:], g.X[:], g.mu[:].unsqueeze(2).broadcast_to(full), ALU.subtract))
    ch.do(v.tensor_tensor(g.TMP[:], g.H[:], g.H[:], ALU.mult))
    ch.do(v.tensor_reduce(g.var[:], g.TMP[:], AX.X, ALU.add))
    ch.do(v.tensor_scalar(g.var[:], g.var[:], 1.0 / D, EPS, ALU.mult, ALU.add))
    v.sem_inc(s_var, 1)
    v.wait_ge(s_std, 1)
    ch.do(v.reciprocal(g.var[:], g.std[:]))
    ch.do(v.scalar_tensor_tensor(g.H[:], g.H[:], 0.0, g.var[:].unsqueeze(2).broadcast_to(full),
                                 ALU.max, ALU.mult))


def node_phase(nc, g, layer, tables):
    with Core(nc, f"n{layer}") as c:
        ht = c.sb("ht", [D, N_ROWS])
        wt = c.sb("wt", [D, D])
        p_t = [c.ps(f"t{i}") for i in range(2)]
        p_m = [c.ps(f"m{i}") for i in range(4)]
        s_var, s_std, s_h, s_v = c.sem("var"), c.sem("std"), c.sem("h"), c.sem("v")
        s_t, s_tc, s_w, s_wc, s_m, s_mc, s_tab = (c.sem(n) for n in ("t", "tc", "w", "wc", "m", "mc", "tab"))
        s_row, s_wall = c.sem("row"), c.sem("wall")
        groups = [range(a, min(a + 4, N_BINS)) for a in range(0, N_BINS, 4)]
        if layer == 0:
            stage = c.sb("stage", [P, N_BINS, 32])
        if layer in (1, 2):
            heads = 4 if layer == 1 else 8
            f = D // heads
            stage = c.sb("stage", [P, N_BINS, heads, f + 1])
        if layer == 3:
            wall = c.sb("wall", [D, N_REL, D])
            stage = c.sb("stage", [P, 2, N_REL * D])
        block = c.block()

        @block.scalar
        def _(act):
            act.wait_ge(s_var, 1)
            act.activation(g.std[:], g.var[:], ACT.Sqrt).then_inc(s_std, 1)
            for n, bins in enumerate(groups):
                act.wait_ge(s_t, n + 1)
                act.copy(ht[:, bins[0] * P:(bins[-1] + 1) * P],
                         p_t[n % 2][:, 0:len(bins) * P]).then_inc(s_tc, 1)

        @block.tensor
        def _(pe):
            if layer in (2, 3):
                pe.transpose(p_m[3][:, 0:D], (g.w2 if layer == 2 else g.w_self)[:], g.ident[:]).then_inc(s_w, 1)
            pe.wait_ge(s_h, 1)
            for n, bins in enumerate(groups):
                if n >= 2:
                    pe.wait_ge(s_tc, n - 1)
                for a in bins:
                    mm = pe.transpose(p_t[n % 2][:, (a - bins[0]) * P:(a - bins[0] + 1) * P],
                                      g.H[:, a, :], g.ident[:])
                mm.then_inc(s_t, 1)
            if layer in (2, 3):
                pe.wait_ge(s_wc, 1)
            if layer == 3:
                pe.wait_ge(s_wall, 1)
            n_m = 0
            for a in range(N_BINS):
                pe.wait_ge(s_tc, a // 4 + 1)
                lhs = ht[:, a * P:(a + 1) * P]

                def out(width, parts):
                    nonlocal n_m
                    if n_m >= 4:
                        pe.wait_ge(s_mc, n_m - 3)
                    bank = p_m[n_m % 4]
                    for at, w in parts:
                        mm = pe.matmul(bank[:, at:at + w.shape[-1]], lhs, w, start=True, stop=True)
                    mm.then_inc(s_m, 1)
                    n_m += 1

                if layer == 0:
                    out(P, [(0, g.we1_src[:]), (HID1, g.wn1_dst[:]), (HID1 + HID2, g.we1_dst[:])])
                if layer == 1:
                    out(P, [(0, g.w1[:])])
                if layer == 2:
                    out(P, [(0, wt[:])])
                if layer == 3:
                    out(P, [(0, wt[:])])
                    for r in range(0, N_REL, 4):
                        out(512, [(0, wall[:, r:r + 4, :].rearrange("i r o -> i (r o)"))])

        @block.vector
        def _(v):
            ch = Chain(v, s_v)
            if layer in (2, 3):
                v.wait_ge(s_w, 1)
                v.tensor_copy(wt[:], p_m[3][:, 0:D]).then_inc(s_wc, 1)
            if layer == 3:
                for r in range(N_REL):
                    for b in range(N_BASES):
                        w = g.coef[:, r * N_BASES + b:r * N_BASES + b + 1]
                        if b == 0:
                            ch.do(v.tensor_scalar(wall[:, r, :], g.bases[:, b, :], w, None, ALU.mult))
                        else:
                            ch.do(v.scalar_tensor_tensor(wall[:, r, :], g.bases[:, b, :], w, wall[:, r, :],
                                                         ALU.mult, ALU.add))
                v.sem_inc(s_wall, 1)
            layer_norm(v, ch, g, c, s_var, s_std, None)
            v.sem_inc(s_h, 1)
            if layer == 0:
                for a in range(N_BINS):
                    v.wait_ge(s_m, a + 1)
                    v.tensor_copy(stage[:, a, :], p_m[a % 4][:, 0:32])
                    v.tensor_tensor(g.dst0[:, a, :], p_m[a % 4][:, 32:P], g.bias0[:], ALU.add).then_inc(s_mc, 1)
                v.wait_ge(s_mc, N_BINS)
                ch.do(v.tensor_tensor(g.X[:], g.X[:], g.H[:], ALU.add))
            if layer in (1, 2):
                for a in range(N_BINS):
                    v.wait_ge(s_m, a + 1)
                    v.tensor_copy(stage[:, a, :, 0:f],
                                  p_m[a % 4][:, 0:D].rearrange("p (h f) -> p h f", h=heads)).then_inc(s_mc, 1)
                v.wait_ge(s_mc, N_BINS)
                shape = [P, N_BINS, heads, f]
                for side in range(2):
                    if layer == 1:
                        a_row = g.a1[:, side, :].rearrange("p (h f) -> p h f", h=heads)
                    else:
                        a_row = g.a2[:, side, :].rearrange("p (f h) -> p h f", h=heads)
                    prod = g.TMP[:].rearrange("p a (h f) -> p a h f", h=heads)
                    for a in range(N_BINS):
                        ins = v.tensor_tensor(prod[:, a], stage[:, a, :, 0:f], a_row, ALU.mult)
                    ch.do(ins)
                    where = stage[:, :, :, f] if side == 0 else g.tgt[:, :, 0:heads]
                    ch.do(v.tensor_reduce(where, prod, AX.X, ALU.add))
            if layer == 3:
                for a in range(N_BINS):
                    for part in range(5):
                        n = 5 * a + part
                        v.wait_ge(s_m, n + 1)
                        if part == 0:
                            v.tensor_tensor(g.X[:, a, :], g.X[:, a, :], p_m[n % 4][:, 0:D],
                                            ALU.add).then_inc(s_mc, 1)
                            continue
                        if part == 1 and a >= 2:
                            v.wait_ge(s_row[a % 2] if isinstance(s_row, list) else s_row, 16 * (a - 1))
                        v.tensor_copy(stage[:, a % 2, (part - 1) * 512:part * 512],
                                      p_m[n % 4][:]).then_inc(s_mc, 1)
            v.sem_inc(s_tab, 1)

        @block.sync
        def _(sp):
            if layer == 3:
                rows = tables.rearrange("(a n r) f -> a n (r f)", a=N_BINS, n=P)
                for a in range(N_BINS):
                    sp.wait_ge(s_mc, 5 * a + 5)
                    if a >= 1:
                        sp.wait_ge(s_row, 16 * a)
                    sp.dma_start(rows[a], stage[:, a % 2, :]).then_inc(s_row, 16)
                sp.wait_ge(s_row, 16 * N_BINS)
            else:
                sp.wait_ge(s_tab, 1)
                src = stage[:] if layer == 0 else stage[:].rearrange("p a h f -> p a (h f)")
                sp.dma_start(tables.rearrange("(a n) f -> n a f", a=N_BINS), src).then_inc(s_row, 16)
                sp.wait_ge(s_row, 16)


def rec_f(rec, k):
    return rec[:, bass.ds(k * TILES, TILES), 1:2].bitcast(F32).broadcast_to([P, TILES, P])


def ge(eng, sem, value):
    if isinstance(value, int) and value <= 0:
        return
    eng.wait_ge(sem, value)


def tick(eng, sem):
    eng.sem_inc(sem, 1)


def gather_stages(act, gp, rec, words, index, rows, tables, s_ix, s_g, s_tick, s_free):
    per = 16 * TILES * len(rows)

    def lay(k, q, b):
        ge(act, s_g[b], q * per)
        for n, w in enumerate(words):
            ins = act.copy(index[b][:, n, :], rec[:, bass.ds(k * TILES, TILES), w])
        ins.then_inc(s_ix, 1)

    def gather(k, q, b):
        ge(gp, s_free, k - (UNROLL - 1))
        gp.wait_ge(s_ix, k + 1)
        tick(gp, s_tick)
        for n in range(len(rows)):
            for t in range(TILES):
                gp.indirect_dma_start(rows[n][b][:, t, :], None, tables[n],
                                      bass.IndirectOffsetOnAxis(index[b][:, n, t:t + 1], axis=0)).then_inc(s_g[b], 16)

    return lay, gather


def edge_mlp(nc, g, edge_attr):
    with Core(nc, "mlp") as c:
        hot = [c.sb(f"hot{b}", [P, TILES, P]) for b in range(UNROLL)]
        index = [c.sb(f"index{b}", [P, 2, TILES], I32) for b in range(UNROLL)]
        row = [c.sb(f"row{b}", [P, TILES, IN_D]) for b in range(UNROLL)]
        hot_t = [c.sb(f"hot_t{b}", [P, BLOCK]) for b in range(2)]
        row_t = [c.sb(f"row_t{b}", [IN_D, BLOCK]) for b in range(2)]
        dst = [c.sb(f"dst{b}", [P, 96]) for b in range(2)]
        h1 = [c.sb(f"h1{b}", [32, BLOCK]) for b in range(2)]
        em = [c.sb(f"em{b}", [P, BLOCK]) for b in range(2)]
        h2 = [c.sb(f"h2{b}", [EDGE_D + 1, BLOCK]) for b in range(2)]
        nm = [c.sb(f"nm{b}", [P, TILES, D]) for b in range(2)]
        p_hot, p_row, p_em, p_nm, p_sum = (c.ps(n) for n in "hot row em nm sum".split())
        p_h = [c.ps(f"h{b}") for b in range(2)]
        s_g, s_tick = c.sems("g", UNROLL), c.sem("tick")
        (s_ix, s_init, s_hot, s_turn, s_turned, s_dst, s_h1, s_h1r, s_em, s_emr, s_h2, s_h2r, s_nm, s_nmr,
         s_sum, s_acc) = (c.sem(n) for n in "ix init hot turn turned dst h1 h1r em emr h2 h2r nm nmr sum acc".split())
        s_e = c.sems("e", UNROLL)
        block = c.block()
        src_rows = [r[:, :, EDGE_D:IN_D] for r in row]
        io = (g.rec_d, (0, 2), index, (src_rows,), (g.tab0,), s_ix, s_g, s_tick, s_turn)

        @block.gpsimd
        def _(gp):
            for b in range(2):
                gp.memset(h2[b][EDGE_D:EDGE_D + 1, :], 1.0).then_inc(s_init, 1)
                gp.wait_ge(s_init, b + 1)
            gp.memset(g.acc[:, :, 0:D], 0.0).then_inc(s_init, 1)
            unsorted = gp.value_load(g.unsorted[0:1, 0:1], min_val=0, max_val=1)

            def gather_edges(k, q, b):
                with gp.If(unsorted > 0):
                    for t in range(TILES):
                        gp.indirect_dma_start(row[b][:, t, 0:EDGE_D], None, edge_attr,
                                              bass.IndirectOffsetOnAxis(index[b][:, 1, t:t + 1], axis=0)
                                              ).then_inc(s_e[b], 16)
            pipeline(gp, [(0, gather_stages(None, gp, *io)[1]), (0, gather_edges)])

        @block.sync
        def _(sp):
            unsorted = sp.value_load(g.unsorted[0:1, 0:1], min_val=0, max_val=1)

            def load_edges(k, q, b):
                ge(sp, s_turn, k - (UNROLL - 1))
                tick(sp, s_tick)
                start = sp.value_load(g.start[0:1, bass.ds(k, 1)], min_val=0, max_val=N_EDGES - BLOCK)
                sp.dma_start(row[b][:, :, 0:EDGE_D],
                             edge_attr[bass.ds(start, BLOCK), :].rearrange("(p t) f -> p t f", p=P)
                             ).then_inc(s_e[b], 16 * TILES)
            with sp.If(unsorted < 1):
                pipeline(sp, [(0, load_edges)])

        @block.scalar
        def _(act):
            lay = gather_stages(act, None, *io)[0]

            def lay_both(k, q, b):
                ge(act, s_e[b], 16 * TILES * q)
                lay(k, q, b)

            def turned(k, q, b):
                act.wait_ge(s_turn, k + 1)
                ge(act, s_h1, k - 1)
                act.copy(hot_t[b % 2][:], p_hot[:])
                act.copy(row_t[b % 2][:], p_row[0:IN_D, :]).then_inc(s_turned, 1)

            def h1_relu(k, q, b):
                act.wait_ge(s_h1, k + 1)
                ge(act, s_em, k - 1)
                act.activation(h1[b % 2][:], p_h[b % 2][HID2:HID2 + HID1, :], ACT.Relu).then_inc(s_h1r, 1)

            def em_relu(k, q, b):
                act.wait_ge(s_em, k + 1)
                ge(act, s_h2, k - 1)
                act.activation(em[b % 2][:], p_em[:], ACT.Relu, bias=g.be2[:]).then_inc(s_emr, 1)

            def h2_relu(k, q, b):
                act.wait_ge(s_h2, k + 1)
                ge(act, s_nm, k - 1)
                act.activation(h2[b % 2][0:HID2, :], p_h[b % 2][0:HID2, :], ACT.Relu).then_inc(s_h2r, 1)

            pipeline(act, [(0, lay_both), (3, turned), (4, h2_relu), (3, h1_relu), (3, em_relu)])

        @block.tensor
        def _(pe):
            pe.wait_ge(s_init, 3)

            def turn(k, q, b):
                ge(pe, s_turned, k)
                pe.wait_ge(s_hot, k + 1)
                for t in range(TILES):
                    pe.transpose(p_hot[:, t * P:(t + 1) * P], hot[b][:, t, :], g.ident[:])
                pe.wait_ge(s_e[b], 16 * TILES * (q + 1))
                pe.wait_ge(s_g[b], 16 * TILES * (q + 1))
                tick(pe, s_tick)
                for t in range(TILES):
                    mm = pe.transpose(p_row[0:IN_D, t * P:(t + 1) * P], row[b][:, t, :], g.ident[:])
                mm.then_inc(s_turn, 1)

            def mm_h1(k, q, b):
                ge(pe, s_h2r, k - 1)
                pe.wait_ge(s_turned, k + 1)
                pe.wait_ge(s_dst, k + 1)
                tick(pe, s_tick)
                pe.matmul(p_h[b % 2][0:IN_D, :], dst[b % 2][:], hot_t[b % 2][:], start=True, stop=False)
                pe.matmul(p_h[b % 2][HID2:HID2 + HID1, :], g.we1_row[:], row_t[b % 2][:],
                          start=False, stop=True).then_inc(s_h1, 1)

            def mm_em(k, q, b):
                ge(pe, s_emr, k)
                pe.wait_ge(s_h1r, k + 1)
                tick(pe, s_tick)
                pe.matmul(p_em[:], g.we2[:], h1[b % 2][:], start=True, stop=True).then_inc(s_em, 1)

            def mm_h2(k, q, b):
                pe.wait_ge(s_emr, k + 1)
                tick(pe, s_tick)
                pe.matmul(p_h[b % 2][0:HID2, :], g.wn1_msg[:], em[b % 2][:],
                          start=False, stop=True).then_inc(s_h2, 1)

            def mm_nm(k, q, b):
                ge(pe, s_nmr, k)
                pe.wait_ge(s_h2r, k + 1)
                tick(pe, s_tick)
                for t in range(TILES):
                    mm = pe.matmul(p_nm[:, t * P:(t + 1) * P], h2[b % 2][:, t * P:(t + 1) * P], g.wn2b[:],
                                   start=True, stop=True)
                mm.then_inc(s_nm, 1)

            def mm_sum(k, q, b):
                ge(pe, s_acc, k)
                pe.wait_ge(s_nmr, k + 1)
                for t in range(TILES):
                    mm = pe.matmul(p_sum[:, 0:D], hot[b][:, t, :], nm[b % 2][:, t, :],
                                   start=(t == 0), stop=(t == TILES - 1))
                mm.then_inc(s_sum, 1)

            pipeline(pe, [(1, turn), (2, mm_h2), (1, mm_h1), (2, mm_nm), (1, mm_em), (2, mm_sum)])

        @block.vector
        def _(v):
            v.wait_ge(s_init, 3)

            def make_hot(k, q, b):
                ge(v, s_sum, k - (UNROLL - 1))
                v.tensor_tensor(hot[b][:], g.iota[:].unsqueeze(1).broadcast_to([P, TILES, P]), rec_f(g.rec_d, k),
                                ALU.is_equal).then_inc(s_hot, 1)

            def bring_dst(k, q, b):
                ge(v, s_h1, k - 1)
                a = bin_register(v, g.bin_d, k, s_tick)
                v.tensor_copy(dst[b % 2][:].unsqueeze(1), g.dst0[:, bass.ds(a, 1), :]).then_inc(s_dst, 1)

            def nm_relu(k, q, b):
                v.wait_ge(s_nm, k + 1)
                ge(v, s_sum, k - 1)
                v.tensor_scalar_max(nm[b % 2][:].rearrange("p t f -> p (t f)"), p_nm[:], 0.0).then_inc(s_nmr, 1)

            pipeline(v, [(0, make_hot), (0, bring_dst), (3, nm_relu),
                         (3, add_sum(v, g, g.bin_d, p_sum, D, 1, s_sum, s_acc, s_tick))])


def bin_register(v, bin_of, k, s_tick):
    tick(v, s_tick)
    return v.value_load(bin_of[0:1, bass.ds(k, 1)], min_val=0, max_val=N_BINS - 1)


def add_sum(v, g, bin_of, p_sum, width, ring, s_sum, s_acc, s_tick):
    def fn(k, q, b):
        bank = p_sum if ring == 1 else p_sum[b % ring]
        v.wait_ge(s_sum, k + 1)
        ge(v, s_acc, k)
        a = bin_register(v, bin_of, k, s_tick)
        there = g.acc[:, bass.ds(a, 1), 0:width]
        v.tensor_tensor(there, there, bank[:, 0:width].unsqueeze(1), ALU.add).then_inc(s_acc, 1)
    return fn


def finish(nc, g, layer, out=None):
    with Core(nc, f"f{layer}") as c:
        s_v, s_o = c.sem("v"), c.sem("o")
        block = c.block()

        @block.vector
        def _(v):
            ch = Chain(v, s_v)
            if layer in (1, 2):
                heads = 4 if layer == 1 else 8
                f = D // heads
                acc = g.acc[:, :, 0:heads * (f + 1)].rearrange("p a (h f) -> p a h f", h=heads)
                den = g.den[:, :, 0:heads]
                tmp = g.TMP[:].rearrange("p a (h f) -> p a h f", h=heads)
                ch.do(v.scalar_tensor_tensor(den, acc[:, :, :, f], 0.0, acc[:, :, :, f], ALU.is_equal, ALU.add))
                ch.do(v.reciprocal(den, den))
                for a in range(N_BINS):
                    ins = v.tensor_tensor(tmp[:, a], acc[:, a, :, 0:f],
                                          den[:, a, :].unsqueeze(2).broadcast_to([P, heads, f]), ALU.mult)
                ch.do(ins)
                if layer == 2:
                    ch.do(v.tensor_tensor(g.TMP[:], g.TMP[:],
                                          g.bias2[:].unsqueeze(1).broadcast_to([P, N_BINS, D]), ALU.add))
                ch.do(v.tensor_tensor(g.X[:], g.X[:], g.TMP[:], ALU.add))
            else:
                ch.do(v.tensor_tensor(g.X[:], g.X[:], g.acc[:, :, 0:D], ALU.add))
            n_done[0] = ch.n

        if out is not None:
            @block.sync
            def _(sp):
                sp.wait_ge(s_v, n_done[0])
                sp.dma_start(out[0:FULL * P, :].rearrange("(a b) f -> b a f", b=P), g.X[:, 0:FULL, :]).then_inc(s_o, 16)
                sp.dma_start(out[FULL * P:N_NODES, :], g.X[0:LAST, FULL, :]).then_inc(s_o, 16)
                sp.wait_ge(s_o, 32)


n_done = [0]


def relation_sum(nc, g):
    with Core(nc, "rel") as c:
        hot = [c.sb(f"hot{b}", [P, TILES, P]) for b in range(UNROLL)]
        index = [c.sb(f"index{b}", [P, 1, TILES], I32) for b in range(UNROLL)]
        row = [c.sb(f"row{b}", [P, TILES, D]) for b in range(UNROLL)]
        p_sum = [c.ps(f"sum{b}") for b in range(2)]
        s_g, s_tick = c.sems("g", UNROLL), c.sem("tick")
        s_ix, s_init, s_hot, s_sum, s_acc = (c.sem(n) for n in "ix init hot sum acc".split())
        block = c.block()
        io = (g.rec_s, (0,), index, (row,), (g.tab3,), s_ix, s_g, s_tick, s_sum)

        @block.gpsimd
        def _(gp):
            gp.memset(g.acc[:, :, 0:D], 0.0).then_inc(s_init, 1)
            pipeline(gp, [(0, gather_stages(None, gp, *io)[1])])

        @block.scalar
        def _(act):
            pipeline(act, [(0, gather_stages(act, None, *io)[0])])

        @block.tensor
        def _(pe):
            def mm_sum(k, q, b):
                ge(pe, s_acc, k - 1)
                pe.wait_ge(s_hot, k + 1)
                pe.wait_ge(s_g[b], 16 * TILES * (q + 1))
                for t in range(TILES):
                    mm = pe.matmul(p_sum[b % 2][:, 0:D], hot[b][:, t, :], row[b][:, t, :],
                                   start=(t == 0), stop=(t == TILES - 1))
                mm.then_inc(s_sum, 1)
            pipeline(pe, [(0, mm_sum)])

        @block.vector
        def _(v):
            v.wait_ge(s_init, 1)

            def make_hot(k, q, b):
                ge(v, s_sum, k - (UNROLL - 1))
                v.tensor_tensor(hot[b][:], g.iota[:].unsqueeze(1).broadcast_to([P, TILES, P]), rec_f(g.rec_s, k),
                                ALU.is_equal).then_inc(s_hot, 1)
            pipeline(v, [(0, make_hot), (1, add_sum(v, g, g.bin_s, p_sum, D, 2, s_sum, s_acc, s_tick))])


def segment_max(nc, g, staged):
    HEADS, W = 4, 132
    with Core(nc, "max") as c:
        hot = [c.sb(f"hot{b}", [P, TILES, P]) for b in range(UNROLL)]
        index = [c.sb(f"index{b}", [P, 1, TILES], I32) for b in range(UNROLL)]
        row = [c.sb(f"row{b}", [P, TILES, W]) for b in range(UNROLL)]
        mask = [c.sb(f"mask{b}", [P, BLOCK]) for b in range(2)]
        junk = c.sb("junk", [P, HEADS, BLOCK])
        top = [c.sb(f"top{b}", [P, HEADS]) for b in range(UNROLL)]
        p_hot = [c.ps(f"hot{b}") for b in range(2)]
        p_s = [c.ps(f"s{h}") for h in range(HEADS)]
        s_g, s_st, s_tick = c.sems("g", UNROLL), c.sems("st", UNROLL), c.sem("tick")
        s_ix, s_init, s_hot, s_turn, s_mask, s_all, s_red, s_top = (
            c.sem(n) for n in "ix init hot turn mask all red top".split())
        s_used = c.sem("used")
        block = c.block()
        io = (g.rec_d, (0,), index, (row,), (g.tab1,), s_ix, s_g, s_tick, s_used)

        @block.gpsimd
        def _(gp):
            gp.memset(g.top[:], -BIG).then_inc(s_init, 1)
            pipeline(gp, [(0, gather_stages(None, gp, *io)[1])])

        @block.sync
        def _(sp):
            def keep(k, q, b):
                sp.wait_ge(s_g[b], 16 * TILES * (q + 1))
                sp.dma_start(staged[bass.ds(k, 1)].rearrange("k p f -> (k p) f"),
                             row[b][:].rearrange("p t f -> p (t f)")).then_inc(s_st[b], 16)

            def kept(k, q, b):
                sp.wait_ge(s_st[b], 16 * (q + 1))
                tick(sp, s_tick)
                sp.wait_ge(s_all, HEADS * (k + 1))
                sp.sem_inc(s_used, 1)
            pipeline(sp, [(0, keep), (3, kept)])

        @block.scalar
        def _(act):
            lay = gather_stages(act, None, *io)[0]

            def make_mask(k, q, b):
                act.wait_ge(s_turn, k + 1)
                ge(act, s_red, HEADS * (k - 1))
                act.activation(mask[b % 2][:], p_hot[b % 2][:], ACT.Copy, scale=BIG, bias=-BIG).then_inc(s_mask, 1)
            pipeline(act, [(0, lay), (2, make_mask)])

        @block.tensor
        def _(pe):
            def turn(k, q, b):
                ge(pe, s_mask, k - 1)
                pe.wait_ge(s_hot, k + 1)
                for t in range(TILES):
                    mm = pe.transpose(p_hot[b % 2][:, t * P:(t + 1) * P], hot[b][:, t, :], g.ident[:])
                mm.then_inc(s_turn, 1)

            def spread(k, q, b):
                pe.wait_ge(s_g[b], 16 * TILES * (q + 1))
                for h in range(HEADS):
                    ge(pe, s_red, HEADS * (k - 1) + h + 1)
                    for t in range(TILES):
                        at = h * 33 + 32
                        mm = pe.transpose(p_s[h][:, t * P:(t + 1) * P],
                                          row[b][:, t, at:at + 1].broadcast_to([P, P]), g.ident[:])
                    mm.then_inc(s_all, 1)
            pipeline(pe, [(1, turn), (2, spread)])

        @block.vector
        def _(v):
            v.wait_ge(s_init, 1)

            def make_hot(k, q, b):
                ge(v, s_turn, k - (UNROLL - 1))
                v.tensor_tensor(hot[b][:], g.iota[:].unsqueeze(1).broadcast_to([P, TILES, P]), rec_f(g.rec_d, k),
                                ALU.is_equal).then_inc(s_hot, 1)

            def reduce(k, q, b):
                v.wait_ge(s_mask, k + 1)
                ge(v, s_top, k - (UNROLL - 1))
                for h in range(HEADS):
                    v.wait_ge(s_all, HEADS * k + h + 1)
                    ge(v, s_red, HEADS * (k - 1) + h + 1)
                    tick(v, s_tick)
                    v.tensor_tensor_reduce(out=junk[:, h, :], in0=mask[b % 2][:], in1=p_s[h][:], scale=1.0,
                                           scalar=-BIG, op0=ALU.add, op1=ALU.max,
                                           accum_out=top[b][:, h:h + 1]).then_inc(s_red, 1)

            def keep_top(k, q, b):
                v.wait_ge(s_red, HEADS * (k + 1))
                ge(v, s_top, k)
                a = bin_register(v, g.bin_d, k, s_tick)
                there = g.top[:, bass.ds(a, 1), :]
                v.tensor_tensor(there, there, top[b][:].unsqueeze(1), ALU.max).then_inc(s_top, 1)
            pipeline(v, [(0, make_hot), (2, reduce), (3, keep_top)])


def target_terms(nc, g):
    H = 4
    with Core(nc, "tt") as c:
        low = c.sb("low", [P, N_BINS, H])
        ex = c.sb("ex", [P, N_BINS, H])
        s_v, s_lo, s_ex = c.sem("v"), c.sem("lo"), c.sem("ex")
        block = c.block()

        @block.vector
        def _(v):
            ch = Chain(v, s_v)
            top = g.tgt[:, :, H:2 * H]
            ch.do(v.tensor_tensor(top, g.top[:], g.tgt[:, :, 0:H], ALU.add))
            ch.do(v.tensor_single_scalar(low[:], top, 0.0, ALU.min))
            v.sem_inc(s_lo, 1)
            v.wait_ge(s_ex, 1)
            ch.do(v.tensor_scalar(ex[:], ex[:], 0.2, -0.2, ALU.mult, ALU.add))
            ch.do(v.scalar_tensor_tensor(top, top, 0.0, ex[:], ALU.max, ALU.add))

        @block.scalar
        def _(act):
            act.wait_ge(s_lo, 1)
            act.activation(ex[:], low[:], ACT.Exp).then_inc(s_ex, 1)


def attention_sum(nc, g, layer, staged, rec_s_dram=None):
    heads = 4 if layer == 1 else 8
    f = D // heads
    W = heads * (f + 1)
    T = 2 * heads if layer == 1 else heads
    with Core(nc, f"att{layer}") as c:
        hot = [c.sb(f"hot{b}", [P, TILES, P]) for b in range(UNROLL)]
        index = [c.sb(f"index{b}", [P, 1, TILES], I32) for b in range(UNROLL)]
        row = [c.sb(f"row{b}", [P, TILES, heads, f + 1]) for b in range(UNROLL)]
        hot_t = [c.sb(f"hot_t{b}", [P, BLOCK]) for b in range(2)]
        tgt = [c.sb(f"tgt{b}", [P, T]) for b in range(2)]
        val = [c.sb(f"val{b}", [P, TILES, heads]) for b in range(2)]
        low = [c.sb(f"low{b}", [P, TILES, heads]) for b in range(2)]
        neg = [c.sb(f"neg{b}", [P, TILES, heads]) for b in range(2)]
        wgt = [c.sb(f"wgt{b}", [P, TILES, heads]) for b in range(2)]
        p_hot = [c.ps(f"hot{b}") for b in range(2)]
        p_t = [c.ps(f"t{b}") for b in range(2)]
        p_sum = [c.ps(f"sum{b}") for b in range(2)]
        s_g, s_tick = c.sems("g", UNROLL), c.sem("tick")
        (s_ix, s_init, s_hot, s_turn, s_turned, s_tgt, s_t, s_v1, s_v2, s_neg, s_v3, s_v4, s_val, s_wgt, s_msg,
         s_sum, s_acc) = (c.sem(n) for n in
                          "ix init hot turn turned tgt t v1 v2 neg v3 v4 val wgt msg sum acc".split())
        block = c.block()
        s_sc, s_ld = c.sem("sc"), c.sem("ld")
        lands = 16 if layer == 1 else 16 * TILES
        flat = [r[:].rearrange("p t h f -> p t (h f)") for r in row]
        io = (g.rec_d, (0,), index, (flat,), (g.tab2,), s_ix, s_g, s_tick, s_sum)

        @block.gpsimd
        def _(gp):
            gp.memset(g.acc[:, :, 0:W], 0.0).then_inc(s_init, 1)
            if layer == 2:
                pipeline(gp, [(0, gather_stages(None, gp, *io)[1])])
            else:
                for j in range(SORT_J):
                    gp.indirect_dma_start(rec_s_dram, bass.IndirectOffsetOnAxis(g.pos_s[:, j:j + 1], axis=0),
                                          g.recs_s[:, j, :], None).then_inc(s_sc, 16)

        if layer == 1:
            @block.sync
            def _(sp):
                def load(k, q, b):
                    ge(sp, s_sum, k - (UNROLL - 1))
                    sp.dma_start(row[b][:].rearrange("p t h f -> p (t h f)"),
                                 staged[bass.ds(k, 1)].rearrange("k p f -> (k p) f")).then_inc(s_g[b], 16)
                pipeline(sp, [(0, load)])
                sp.wait_ge(s_sc, 16 * SORT_J)
                sp.dma_start(g.rec_s[:].rearrange("p (k t) w -> p k (t w)", t=TILES),
                             as_blocks(rec_s_dram)).then_inc(s_ld, 16)
                sp.wait_ge(s_ld, 16)

        @block.scalar
        def _(act):
            lay = gather_stages(act, None, *io)[0]

            def turned(k, q, b):
                act.wait_ge(s_turn, k + 1)
                ge(act, s_t, k - 1)
                act.copy(hot_t[b % 2][:], p_hot[b % 2][:]).then_inc(s_turned, 1)

            def negative(k, q, b):
                act.wait_ge(s_v2, k + 1)
                ge(act, s_v4, k - 1)
                act.activation(neg[b % 2][:], low[b % 2][:], ACT.Exp).then_inc(s_neg, 1)

            def weight(k, q, b):
                act.wait_ge(s_val, k + 1)
                ge(act, s_msg, k - 1)
                act.activation(wgt[b % 2][:], val[b % 2][:], ACT.Exp).then_inc(s_wgt, 1)
            if layer == 1:
                pipeline(act, [(0, turned), (1, negative), (2, weight)])
            else:
                pipeline(act, [(0, lay), (3, turned), (4, weight)])

        @block.tensor
        def _(pe):
            def turn(k, q, b):
                ge(pe, s_turned, k - 1)
                pe.wait_ge(s_hot, k + 1)
                for t in range(TILES):
                    mm = pe.transpose(p_hot[b % 2][:, t * P:(t + 1) * P], hot[b][:, t, :], g.ident[:])
                mm.then_inc(s_turn, 1)

            def take(k, q, b):
                ge(pe, s_val, k - 1)
                pe.wait_ge(s_turned, k + 1)
                pe.wait_ge(s_tgt, k + 1)
                for t in range(TILES):
                    mm = pe.matmul(p_t[b % 2][:, t * T:(t + 1) * T], hot_t[b % 2][:, t * P:(t + 1) * P],
                                   tgt[b % 2][:], start=True, stop=True)
                mm.then_inc(s_t, 1)

            def mm_sum(k, q, b):
                ge(pe, s_acc, k - 1)
                pe.wait_ge(s_msg, k + 1)
                for t in range(TILES):
                    mm = pe.matmul(p_sum[b % 2][:, 0:W], hot[b][:, t, :], flat[b][:, t, :],
                                   start=(t == 0), stop=(t == TILES - 1))
                mm.then_inc(s_sum, 1)
            pipeline(pe, [(1, turn), (2, take), (4 if layer == 2 else 5, mm_sum)])

        @block.vector
        def _(v):
            v.wait_ge(s_init, 1)

            def make_hot(k, q, b):
                ge(v, s_sum, k - (UNROLL - 1))
                v.tensor_tensor(hot[b][:], g.iota[:].unsqueeze(1).broadcast_to([P, TILES, P]), rec_f(g.rec_d, k),
                                ALU.is_equal).then_inc(s_hot, 1)

            def bring_tgt(k, q, b):
                ge(v, s_t, k - 1)
                a = bin_register(v, g.bin_d, k, s_tick)
                v.tensor_copy(tgt[b % 2][:].unsqueeze(1), g.tgt[:, bass.ds(a, 1), 0:T]).then_inc(s_tgt, 1)

            def there(b):
                return p_t[b % 2][:, 0:TILES * T].rearrange("p (t w) -> p t w", t=TILES)

            def score(k, q, b):
                v.wait_ge(s_g[b], lands * (q + 1))
                v.wait_ge(s_t, k + 1)
                ge(v, s_wgt, k - 1)
                x = val[b % 2][:]
                v.tensor_tensor(x, row[b][:, :, :, f], there(b)[:, :, 0:heads], ALU.add).then_inc(s_v1, 1)
                v.wait_ge(s_v1, k + 1)
                if layer == 1:
                    v.tensor_scalar_min(low[b % 2][:], x, 0.0).then_inc(s_v2, 1)
                else:
                    v.scalar_tensor_tensor(x, x, 0.2, x, ALU.mult, ALU.max).then_inc(s_val, 1)

            def elu(k, q, b):
                x, e = val[b % 2][:], neg[b % 2][:]
                v.wait_ge(s_neg, k + 1)
                v.tensor_scalar(e, e, 0.2, -0.2, ALU.mult, ALU.add).then_inc(s_v3, 1)
                v.wait_ge(s_v3, k + 1)
                v.scalar_tensor_tensor(x, x, 0.0, e, ALU.max, ALU.add).then_inc(s_v4, 1)
                v.wait_ge(s_v4, k + 1)
                v.tensor_tensor(x, x, there(b)[:, :, heads:T], ALU.subtract).then_inc(s_val, 1)

            def message(k, q, b):
                v.wait_ge(s_wgt, k + 1)
                w = wgt[b % 2][:]
                v.tensor_copy(row[b][:, :, :, f], w)
                for t in range(TILES):
                    ins = v.tensor_tensor(row[b][:, t, :, 0:f], row[b][:, t, :, 0:f],
                                          wgt[b % 2][:, t, :].unsqueeze(2).broadcast_to([P, heads, f]), ALU.mult)
                ins.then_inc(s_msg, 1)

            add = add_sum(v, g, g.bin_d, p_sum, W, 2, s_sum, s_acc, s_tick)
            if layer == 1:
                pipeline(v, [(0, make_hot), (0, bring_tgt), (2, score), (3, elu), (4, message), (6, add)])
            else:
                pipeline(v, [(0, make_hot), (0, bring_tgt), (2, score), (3, message), (5, add)])


def graph_layers(nc, args, out):
    g = Shared()
    with ExitStack() as ctx:
        def sb(name, shape, dt=F32):
            return ctx.enter_context(nc.sbuf_tensor(name, shape, dt))

        def dram(name, shape, dt=F32):
            return nc.dram_tensor(name, shape, dt).ap()

        g.ident, g.ones, g.earlier = sb("ident", [P, P]), sb("ones", [P, P]), sb("earlier", [P, P])
        g.iota, g.iota_blocks = sb("iota", [P, P]), sb("iota_blocks", [P, N_BLOCKS])
        g.rec_d, g.rec_s = sb("rec_d", [P, N_POS // P, DW], I32), sb("rec_s", [P, N_POS // P, SW], I32)
        g.bin_d, g.bin_s = sb("bin_d", [1, N_BLOCKS], I32), sb("bin_s", [1, N_BLOCKS], I32)
        rec_d_dram, rec_s_dram = dram("rec_d_dram", [N_POS, DW], I32), dram("rec_s_dram", [N_POS, SW], I32)
        g.recs_s, g.pos_s = sb("recs_s", [SORT_P, SORT_J, SW], I32), sb("pos_s", [SORT_P, SORT_J], I32)
        g.start, g.unsorted = sb("start", [1, N_BLOCKS], I32), sb("unsorted", [1, 1], I32)
        edges_dram = dram("edges_dram", [N_EDGES, DW], I32)
        constants(nc, g)
        order_edges(nc, g, args, edges_dram, rec_d_dram, rec_s_dram)

        g.X, g.H, g.TMP = (sb(n, [P, N_BINS, D]) for n in ("X", "H", "TMP"))
        g.mu, g.var, g.std = (sb(n, [P, N_BINS]) for n in ("mu", "var", "std"))
        g.acc = sb("acc", [P, N_BINS, 136])
        g.den, g.tgt, g.top = sb("den", [P, N_BINS, 8]), sb("tgt", [P, N_BINS, 8]), sb("top", [P, N_BINS, 4])
        g.we1_src, g.we1_dst = sb("we1_src", [D, HID1]), sb("we1_dst", [D, HID1])
        g.we1_row = sb("we1_row", [IN_D, HID1])
        g.we2, g.wn1_dst, g.wn1_msg = sb("we2", [32, D]), sb("wn1_dst", [D, 64]), sb("wn1_msg", [D, 64])
        g.wn2b, g.be2, g.bias0 = sb("wn2b", [65, D]), sb("be2", [P, 1]), sb("bias0", [P, 96])
        g.w1, g.w2, g.w_self = sb("w1", [D, D]), sb("w2", [D, D]), sb("w_self", [D, D])
        g.a1, g.a2, g.bias2 = sb("a1", [P, 2, D]), sb("a2", [P, 2, D]), sb("bias2", [P, D])
        g.bases, g.coef = sb("bases", [D, N_BASES, D]), sb("coef", [P, N_REL * N_BASES])
        g.dst0 = sb("dst0", [P, N_BINS, 96])
        g.tab0, g.tab1, g.tab2 = dram("tab0", [N_ROWS, 32]), dram("tab1", [N_ROWS, 132]), dram("tab2", [N_ROWS, 136])
        g.tab3 = dram("tab3", [N_ROWS * N_REL, D])
        staged = dram("staged", [N_BLOCKS, P, TILES * 132])
        setup(nc, g, args)
        node_phase(nc, g, 0, g.tab0)
        edge_mlp(nc, g, args["edge_attr"])
        finish(nc, g, 0)
        node_phase(nc, g, 1, g.tab1)
        segment_max(nc, g, staged)
        target_terms(nc, g)
        attention_sum(nc, g, 1, staged, rec_s_dram)
        finish(nc, g, 1)
        node_phase(nc, g, 2, g.tab2)
        attention_sum(nc, g, 2, None)
        finish(nc, g, 2)
        node_phase(nc, g, 3, g.tab3)
        relation_sum(nc, g)
        finish(nc, g, 3, out)


_INS = {
    "x": "x", "src": "src", "dst": "dst", "edge_attr": "edge_attr_64", "type": "edge_type_16",
    "We1": "L0_gnn_We1", "be1": "L0_gnn_be1", "We2": "L0_gnn_We2", "be2": "L0_gnn_be2",
    "Wn1": "L0_gnn_Wn1", "bn1": "L0_gnn_bn1", "Wn2": "L0_gnn_Wn2", "bn2": "L0_gnn_bn2",
    "W1": "L1_gnn_W", "a_src": "L1_gnn_a_src", "a_tgt": "L1_gnn_a_tgt",
    "W2": "L2_gnn_W", "a_left": "L2_gnn_a_left", "a_right": "L2_gnn_a_right", "bias": "L2_gnn_bias",
    "bases": "L3_gnn_bases", "coefficients": "L3_gnn_coefficients", "w_self": "L3_gnn_w_self",
}


def kernel(**inputs):
    import numpy as _np
    import concourse.bacc as _bacc
    from concourse import mybir as _mybir
    from concourse.bass_utils import run_bass_kernel_spmd as _run

    nc = _bacc.Bacc("TRN2", target_bir_lowering=False, num_devices=1)
    arrays, args = {}, {}
    for short, name in _INS.items():
        a = _np.ascontiguousarray(inputs[name])
        arrays[f"in_{name}"] = a
        args[short] = nc.dram_tensor(f"in_{name}", a.shape, _mybir.dt.from_np(a.dtype), kind="ExternalInput").ap()
    out = nc.dram_tensor("out_x", (N_NODES, D), F32, kind="ExternalOutput").ap()
    graph_layers(nc, args, out)
    r = _run(nc, [arrays], core_ids=[0])
    return r.results[0]["out_x"]
```

```python
from contextlib import ExitStack

import concourse.bass as bass
from concourse import mybir

ALU = mybir.AluOpType
ACT = mybir.ActivationFunctionType
AX = mybir.AxisListType
F32 = mybir.dt.float32
I32 = mybir.dt.int32
BF16 = mybir.dt.bfloat16
F16 = mybir.dt.float16

P = 128
N_NODES = 3125
N_BINS = -(-N_NODES // P)
N_ROWS = N_BINS * P
FULL = N_NODES // P
LAST = N_NODES - FULL * P
D = 128
N_EDGES = 100000
SORT_P = 125
SORT_J = N_EDGES // SORT_P
TILES = 4
BLOCK = TILES * P
N_BLOCKS = (N_EDGES + N_BINS * (BLOCK - 1)) // BLOCK
UNROLL = 10
N_BLOCKS = -(-N_BLOCKS // UNROLL) * UNROLL
N_POS = N_BLOCKS * BLOCK
EDGE_D = 64
N_REL, N_BASES = 16, 8
HID1, HID2 = 32, 64
IN_D = EDGE_D + HID1
EPS = 1e-5
BIG = 1e30
DW = 4
SW = 2


def pipeline(eng, stages):
    deepest = max(lag for lag, _ in stages)
    head = -(-(deepest + UNROLL) // UNROLL) * UNROLL

    def step(k):
        for lag, fn in stages:
            if 0 <= k - lag < N_BLOCKS:
                fn(k - lag, (k - lag) // UNROLL, (k - lag) % UNROLL)

    for k in range(head):
        step(k)
    with eng.Fori(head // UNROLL, N_BLOCKS // UNROLL) as i:
        for c in range(UNROLL):
            for lag, fn in stages:
                at = c - lag
                fn(i * UNROLL + at, i + at // UNROLL, at % UNROLL)
    for k in range(N_BLOCKS, N_BLOCKS + deepest):
        step(k)


class Shared:
    pass


class Chain:

    def __init__(self, eng, sem):
        self.eng, self.sem, self.n = eng, sem, 0

    def do(self, ins):
        self.n += 1
        ins.then_inc(self.sem, 1)
        self.eng.wait_ge(self.sem, self.n)


class Core:

    def __init__(self, nc, tag):
        self.nc, self.tag, self.ctx, self.taken = nc, tag, ExitStack(), []

    def __enter__(self):
        return self

    def __exit__(self, kind, *a):
        if kind is None:
            self.ctx.close()
            self.nc.clear_and_free_semaphores(self.taken)
            self.nc.all_engine_barrier()

    def sb(self, name, shape, dt=F32):
        return self.ctx.enter_context(self.nc.sbuf_tensor(f"{self.tag}_{name}", shape, dt))

    def ps(self, name, shape=(P, 512)):
        return self.ctx.enter_context(self.nc.psum_tensor(f"{self.tag}_ps_{name}", list(shape), F32))

    def sem(self, name):
        self.taken.append(self.nc.alloc_semaphore(name=f"{self.tag}_s_{name}"))
        return self.taken[-1]

    def sems(self, name, n):
        return [self.sem(f"{name}{i}") for i in range(n)]

    def block(self):
        return self.ctx.enter_context(self.nc.Block())


def constants(nc, g):
    with Core(nc, "con") as c:
        s_c = c.sem("c")
        block = c.block()

        @block.gpsimd
        def _(gp):
            ch = Chain(gp, s_c)
            ch.do(gp.memset(g.ident[:], 0.0))
            ch.do(gp.affine_select(out=g.ident[:], in_=g.ident[:], compare_op=ALU.not_equal, fill=1.0,
                                   base=0, pattern=[[-1, P]], channel_multiplier=1))
            ch.do(gp.memset(g.ones[:], 1.0))
            ch.do(gp.affine_select(out=g.earlier[:], in_=g.ones[:], compare_op=ALU.is_gt, fill=0.0,
                                   base=0, pattern=[[1, P]], channel_multiplier=-1))
            ch.do(gp.iota(g.iota[:], pattern=[[1, P]], base=1, channel_multiplier=0,
                          allow_small_or_imprecise_dtypes=True))
            ch.do(gp.iota(g.iota_blocks[:], pattern=[[1, N_BLOCKS]], base=0, channel_multiplier=0,
                          allow_small_or_imprecise_dtypes=True))


def weight_loads(g, args):
    return [
        (g.we1_src[:], args["We1"][0:D, :]), (g.we1_dst[:], args["We1"][D:2 * D, :]),
        (g.we1_row[0:EDGE_D, :], args["We1"][2 * D:2 * D + EDGE_D, :]), (g.we2[:], args["We2"]),
        (g.wn1_dst[:], args["Wn1"][0:D, :]), (g.wn1_msg[:], args["Wn1"][D:2 * D, :]),
        (g.wn2b[0:64, :], args["Wn2"]), (g.wn2b[64:65, :], args["bn2"].unsqueeze(0)),
        (g.be2[:], args["be2"].unsqueeze(1)),
        (g.bias0[:, 0:HID2], args["bn1"].partition_broadcast(P)),
        (g.bias0[:, HID2:IN_D], args["be1"].partition_broadcast(P)),
        (g.w1[:], args["W1"]), (g.w2[:], args["W2"]),
        (g.a1[:, 0, :], args["a_src"].rearrange("h f -> (h f)").partition_broadcast(P)),
        (g.a1[:, 1, :], args["a_tgt"].rearrange("h f -> (h f)").partition_broadcast(P)),
        (g.a2[:, 0, :], args["a_left"].rearrange("c h -> (c h)").partition_broadcast(P)),
        (g.a2[:, 1, :], args["a_right"].rearrange("c h -> (c h)").partition_broadcast(P)),
        (g.bias2[:], args["bias"].partition_broadcast(P)),
        (g.w_self[:], args["w_self"]),
        (g.X[:, 0:FULL, :], args["x"][0:FULL * P, :].rearrange("(a b) f -> b a f", b=P)),
    ]


def bin_numbers(v, ch, sort, key_i):
    ch.do(v.tensor_single_scalar(sort.bin_i[:], key_i[:], P.bit_length() - 1, ALU.logical_shift_right))
    ch.do(v.tensor_copy(sort.bin_f[:], sort.bin_i[:]))


def bin_counts(v, ch, sort):
    for a in range(N_BINS):
        ins = v.tensor_scalar(sort.in_bin[:, a, :], sort.bin_f[:], float(a), 0.0, ALU.is_equal, ALU.add,
                              accum_out=sort.counts[:, a:a + 1])
    ch.do(ins)


def bin_ranks(v, ch, sort):
    for a in range(N_BINS):
        ins = v.tensor_tensor_scan(sort.rank[:, a, :], sort.in_bin[:, a, :], sort.in_bin[:, a, :], 0.0,
                                   ALU.add, ALU.max)
    ch.do(ins)


def block_tables(v, ch, g, sort, turn, bins_i, bins_f, starts):
    s_row, s_col, s_past, s_tab = turn
    total = sort.p_total[:, 0:N_BINS]
    ch.do(v.tensor_single_scalar(sort.upto[:], total, float(BLOCK - 1), ALU.add))
    ch.do(v.tensor_copy(sort.blocks_i[:], sort.upto[:]))
    ch.do(v.tensor_single_scalar(sort.blocks_i[:], sort.blocks_i[:], BLOCK.bit_length() - 1,
                                 ALU.logical_shift_right))
    ch.do(v.tensor_copy(sort.blocks[:], sort.blocks_i[:]))
    ch.do(v.tensor_tensor_scan(sort.upto[:], sort.blocks[:], sort.blocks[:], 0.0, ALU.add, ALU.max))
    ch.do(v.scalar_tensor_tensor(sort.step[:], sort.blocks[:], float(-BLOCK), total, ALU.mult, ALU.add))
    v.sem_inc(s_row, 1)
    ch.do(v.tensor_tensor(sort.base[:], sort.upto[:], sort.blocks[:], ALU.subtract))
    ch.do(v.tensor_scalar(sort.base[:], sort.base[:], float(BLOCK), -1.0, ALU.mult, ALU.add))
    ch.do(v.tensor_tensor(sort.base[0:SORT_P, :], sort.base[0:SORT_P, :], sort.p_before[0:SORT_P, 0:N_BINS],
                          ALU.add))
    v.wait_ge(s_col, 1)
    ch.do(v.tensor_copy(sort.cols[:, 0:1], sort.p_total[0:N_BINS, P:P + 1]))
    ch.do(v.tensor_copy(sort.cols[:, 1:2], sort.p_total[0:N_BINS, 2 * P:2 * P + 1]))
    blocks = g.iota_blocks[0:N_BINS, :]
    ch.do(v.tensor_scalar(sort.past[:, 0, :], blocks, sort.cols[:, 0:1], None, ALU.is_ge))
    ch.do(v.tensor_scalar(sort.past[:, 1, :], blocks, sort.cols[:, 0:1], sort.cols[:, 1:2], ALU.is_ge, ALU.mult))
    v.sem_inc(s_past, 1)
    v.wait_ge(s_tab, 1)
    ch.do(v.tensor_single_scalar(bins_f[:], sort.p_before[:, P:P + N_BLOCKS], float(N_BINS - 1), ALU.min))
    ch.do(v.tensor_copy(bins_i[:], bins_f[0:1, :]))
    if starts is None:
        return
    ch.do(v.scalar_tensor_tensor(starts[:], g.iota_blocks[:], float(BLOCK), sort.p_tab[:, 0:N_BLOCKS],
                                 ALU.mult, ALU.add))
    ch.do(v.tensor_scalar(sort.none[:], sort.p_before[:, P:P + N_BLOCKS], float(N_BINS), float(N_POS),
                          ALU.is_ge, ALU.mult))
    ch.do(v.tensor_tensor(starts[:], starts[:], sort.none[:], ALU.add))


def table_products(pe, g, sort, turn):
    s_row, s_col, s_past, s_tab = turn
    pe.wait_ge(s_row, 1)
    pe.transpose(sort.p_total[0:N_BINS, P:2 * P], sort.upto[:], g.ident[:])
    pe.transpose(sort.p_total[0:N_BINS, 2 * P:3 * P], sort.step[:], g.ident[:]).then_inc(s_col, 1)
    pe.wait_ge(s_past, 1)
    pe.matmul(sort.p_before[:, P:P + N_BLOCKS], g.ones[0:N_BINS, :], sort.past[:, 0, :], start=True, stop=True)
    pe.matmul(sort.p_tab[:, 0:N_BLOCKS], g.ones[0:N_BINS, :], sort.past[:, 1, :],
              start=True, stop=True).then_inc(s_tab, 1)


HALVES = [slice(n * SORT_J // 2, (n + 1) * SORT_J // 2) for n in range(2)]


PICKS = 4


def positions(v, ch, sort, pos_i, s_pick, s_pos):
    for a in range(N_BINS):
        if a >= PICKS:
            v.wait_ge(s_pos, a - PICKS + 1)
        v.scalar_tensor_tensor(sort.pick[:, a % PICKS, :], sort.rank[:, a, :], sort.base[0:SORT_P, a:a + 1],
                               sort.in_bin[:, a, :], ALU.add, ALU.mult).then_inc(s_pick, 1)
    v.wait_ge(s_pos, N_BINS)
    for n, half in enumerate(HALVES):
        ch.do(v.tensor_copy(pos_i[:, half], sort.p_pos[n][0:SORT_P, 0:SORT_J // 2]))


def sum_bins(pe, g, sort, s_pick, s_pos):
    for a in range(N_BINS):
        pe.wait_ge(s_pick, a + 1)
        for n, half in enumerate(HALVES):
            mm = pe.matmul(sort.p_pos[n][0:SORT_P, 0:SORT_J // 2], g.ident[0:SORT_P, 0:SORT_P],
                           sort.pick[:, a % PICKS, half], start=(a == 0), stop=(a == N_BINS - 1))
        mm.then_inc(s_pos, 1)


def as_blocks(rec_dram):
    return rec_dram.rearrange("(k p t) w -> p k (t w)", p=P, t=TILES)


def order_edges(nc, g, args, edges_dram, rec_d_dram):
    with Core(nc, "ord") as c:
        sort = Shared()
        src_i, dst_i, type_i = (c.sb(n, [SORT_P, SORT_J], I32) for n in ("src_i", "dst_i", "type_i"))
        next_i = c.sb("next_i", [SORT_P, 1], I32)
        next_f = c.sb("next_f", [SORT_P, 1])
        sort.bin_i = c.sb("bin_i", [SORT_P, SORT_J], I32)
        sort.bin_f, sort.hot = c.sb("bin_f", [SORT_P, SORT_J], BF16), c.sb("hot", [SORT_P, SORT_J])
        sort.in_bin = c.sb("in_bin", [SORT_P, N_BINS, SORT_J], BF16)
        sort.p_pos = [c.ps(f"pos{n}") for n in range(2)]
        pos_i = c.sb("pos_i", [SORT_P, SORT_J], I32)
        sort.rank = c.sb("rank", [SORT_P, N_BINS, SORT_J], F16)
        sort.pick = c.sb("pick", [SORT_P, PICKS, SORT_J])
        sort.counts = c.sb("counts", [SORT_P, N_BINS + 1])
        sort.blocks_i = c.sb("blocks_i", [P, N_BINS], I32)
        sort.blocks, sort.upto, sort.base, sort.step = (
            c.sb(n, [P, N_BINS]) for n in ("blocks", "upto", "base", "step"))
        sort.past, sort.none = c.sb("past", [N_BINS, 2, N_BLOCKS]), c.sb("none", [P, N_BLOCKS])
        sort.cols = c.sb("cols", [N_BINS, 2])
        bins_f, bins_sf = (c.sb(n, [P, N_BLOCKS]) for n in ("bins_f", "bins_sf"))
        down = c.sb("down", [SORT_P, 1])
        recs = c.sb("recs", [SORT_P, SORT_J, DW], I32)
        dst_f, id_f = (recs[:, :, w].bitcast(F32) for w in (1, 3))
        bases, coef = c.sb("bases", [D, N_BASES, D]), c.sb("coef", [P, N_REL * N_BASES])
        part = c.sb("part", [D, 4, D])
        sort.p_before, sort.p_total, sort.p_tab = c.ps("before"), c.ps("total"), c.ps("tab")
        s_in, s_z, s_v, s_cnt, s_mm, s_flag, s_recs, s_out, s_emp, s_em, s_done, s_sc, s_id, s_vu, s_w, s_wall, \
            s_pick, s_pos, s_upick, s_upos, s_node = (
                c.sem(n) for n in
                "in z v cnt mm flag recs out emp em done sc id vu w wall pick pos upick upos node".split())
        turns = [c.sems(f"turn{n}", 4) for n in range(2)]
        block = c.block()
        by_edge = "(p j) -> p j"

        @block.sync
        def _(sp):
            loads = weight_loads(g, args)
            for tile, key in ((dst_i, "dst"), (src_i, "src"), (type_i, "type")):
                sp.dma_start(tile[:], args[key].rearrange(by_edge, p=SORT_P)).then_inc(s_in, 16)
            sp.wait_ge(s_z, 3)
            sp.dma_start(next_i[0:SORT_P - 1, :],
                         args["dst"].rearrange(by_edge, p=SORT_P)[1:SORT_P, 0:1],
                         allow_slow_non_contiguous=True).then_inc(s_in, 16)
            sp.dma_start(bases[:], args["bases"].rearrange("b i o -> i b o")).then_inc(s_w, 16)
            sp.dma_start(coef[:], args["coefficients"].rearrange("r b -> (r b)").partition_broadcast(P)
                         ).then_inc(s_w, 16)
            for tile, array in loads:
                sp.dma_start(tile, array).then_inc(s_node, 16)
            sp.dma_start(g.X[0:LAST, FULL, :], args["x"][FULL * P:N_NODES, :]).then_inc(s_node, 16)
            sp.wait_ge(s_recs, 1)
            sp.dma_start(edges_dram.rearrange("(p j) w -> p (j w)", p=SORT_P),
                         recs[:].rearrange("p j w -> p (j w)")).then_inc(s_out, 16)
            sp.wait_ge(s_emp, 4)
            sp.dma_start(as_blocks(g.rec_s_dram), g.rec_s[:].rearrange("p (k t) w -> p k (t w)", t=TILES)
                         ).then_inc(s_em, 16)
            sp.dma_start(as_blocks(rec_d_dram), g.rec_d[:].rearrange("p (k t) w -> p k (t w)", t=TILES)
                         ).then_inc(s_em, 16)
            sp.wait_ge(s_out, 16)
            sp.wait_ge(s_em, 32)
            sp.wait_ge(s_node, 16 * (len(loads) + 1))
            sp.wait_ge(s_flag, 1)
            unsorted = sp.value_load(g.unsorted[0:1, 0:1], min_val=0, max_val=1)
            with sp.If(unsorted > 0):
                sp.wait_ge(s_sc, 16 * SORT_J)

        @block.vector
        def _(v):
            ch = Chain(v, s_v)
            v.memset(next_i[:], N_NODES).then_inc(s_z, 1)
            v.memset(g.X[:, FULL, :], 0.0).then_inc(s_z, 1)
            v.tensor_copy(g.we1_row[EDGE_D:IN_D, :], g.ident[EDGE_D:IN_D, EDGE_D:IN_D]).then_inc(s_z, 1)
            v.wait_ge(s_in, 64)
            ch.do(v.tensor_copy(next_f[:], next_i[:]))
            ch.do(v.tensor_copy(recs[:, :, 0], src_i[:]))
            ch.do(v.tensor_copy(dst_f, dst_i[:]))
            v.wait_ge(s_id, 1)
            ch.do(v.tensor_copy(id_f, pos_i[:]))
            ch.do(v.tensor_copy(recs[:, :, 2], pos_i[:]))
            v.sem_inc(s_recs, 1)
            ch.do(v.tensor_tensor(sort.hot[:, 0:SORT_J - 1], dst_f[:, 0:SORT_J - 1], dst_f[:, 1:SORT_J], ALU.is_gt))
            ch.do(v.tensor_tensor(sort.hot[:, SORT_J - 1:SORT_J], dst_f[:, SORT_J - 1:SORT_J], next_f[:], ALU.is_gt))
            ch.do(v.tensor_reduce(down[:], sort.hot[:], AX.X, ALU.max))
            bin_numbers(v, ch, sort, dst_i)
            bin_counts(v, ch, sort)
            ch.do(v.tensor_copy(sort.counts[:, N_BINS:N_BINS + 1], down[:]))
            v.sem_inc(s_cnt, 1)
            v.wait_ge(s_mm, 2)
            block_tables(v, ch, g, sort, turns[0], g.bin_d, bins_f, g.first)
            ch.do(v.tensor_scalar(g.shift[:], bins_f[:], float(-P), 1.0, ALU.mult, ALU.add))
            ch.do(v.tensor_single_scalar(sort.none[:], g.first[:], float(N_EDGES - BLOCK), ALU.min))
            ch.do(v.tensor_copy(g.start[:], sort.none[0:1, :]))
            ch.do(v.tensor_single_scalar(g.unsorted[:], sort.p_total[0:1, N_BINS:N_BINS + 1], 1.0, ALU.min))
            v.sem_inc(s_flag, 1)
            unsorted = v.value_load(g.unsorted[0:1, 0:1], min_val=0, max_val=1)
            with v.If(unsorted > 0):
                s_u = Chain(v, s_vu)
                bin_ranks(v, s_u, sort)
                positions(v, s_u, sort, pos_i, s_upick, s_upos)
                v.wait_ge(s_out, 16)
                s_u.do(v.memset(recs[:, :, 3:4].bitcast(F32), float(2 * N_POS)))
                v.sem_inc(s_done, 1)
            ch.do(v.tensor_copy(sort.hot[:], type_i[:]))
            ch.do(v.scalar_tensor_tensor(g.recs_s[:, :, 0], dst_f, float(N_REL), sort.hot[:], ALU.mult, ALU.add))
            ch.do(v.tensor_single_scalar(sort.bin_i[:], src_i[:], P - 1, ALU.bitwise_and))
            ch.do(v.tensor_single_scalar(g.recs_s[:, :, 1].bitcast(F32), sort.bin_i[:], 1.0, ALU.add))
            bin_numbers(v, ch, sort, src_i)
            bin_counts(v, ch, sort)
            v.sem_inc(s_cnt, 1)
            bin_ranks(v, ch, sort)
            v.wait_ge(s_mm, 4)
            block_tables(v, ch, g, sort, turns[1], g.bin_s, bins_sf, None)
            positions(v, ch, sort, g.pos_s, s_pick, s_pos)

        @block.tensor
        def _(pe):
            for n, width in enumerate((N_BINS + 1, N_BINS)):
                pe.wait_ge(s_cnt, n + 1)
                pe.matmul(sort.p_before[:, 0:width], g.earlier[0:SORT_P, :], sort.counts[:, 0:width],
                          start=True, stop=True).then_inc(s_mm, 1)
                pe.matmul(sort.p_total[:, 0:width], g.ones[0:SORT_P, :], sort.counts[:, 0:width],
                          start=True, stop=True).then_inc(s_mm, 1)
                table_products(pe, g, sort, turns[n])
                if n == 0:
                    pe.wait_ge(s_flag, 1)
                    unsorted = pe.value_load(g.unsorted[0:1, 0:1], min_val=0, max_val=1)
                    with pe.If(unsorted > 0):
                        sum_bins(pe, g, sort, s_upick, s_upos)
            sum_bins(pe, g, sort, s_pick, s_pos)

        @block.gpsimd
        def _(gp):
            gp.iota(pos_i[:], pattern=[[1, SORT_J]], base=0,
                    channel_multiplier=SORT_J).then_inc(s_id, 1)
            for n, rec in enumerate((g.rec_s, g.rec_d)):
                gp.memset(rec[:], 0).then_inc(s_emp, 1)
                gp.wait_ge(s_emp, 2 * n + 1)
                gp.memset(rec[:, :, 1:2].bitcast(F32), float(-2 * N_ROWS)).then_inc(s_emp, 1)
                gp.wait_ge(s_emp, 2 * n + 2)
            ch = Chain(gp, s_wall)
            gp.wait_ge(s_w, 32)
            wide = [D, 4, D]
            per_base = coef[:].rearrange("p (r b) -> p r b", b=N_BASES)
            for r in range(0, N_REL, 4):
                wall = g.wall[:, r:r + 4, :]
                for b in range(N_BASES):
                    ch.do(gp.tensor_tensor(wall if b == 0 else part[:],
                                           bases[:, b, :].unsqueeze(1).broadcast_to(wide),
                                           per_base[:, r:r + 4, b:b + 1].broadcast_to(wide), ALU.mult))
                    if b:
                        ch.do(gp.tensor_tensor(wall, wall, part[:], ALU.add))
            gp.wait_ge(s_flag, 1)
            unsorted = gp.value_load(g.unsorted[0:1, 0:1], min_val=0, max_val=1)
            with gp.If(unsorted > 0):
                gp.wait_ge(s_done, 1)
                gp.wait_ge(s_em, 32)
                for j in range(SORT_J):
                    gp.indirect_dma_start(rec_d_dram, bass.IndirectOffsetOnAxis(pos_i[:, j:j + 1], axis=0),
                                          recs[:, j, :], None).then_inc(s_sc, 16)


SHARES = {"mlp": N_BLOCKS // 2, "n0": 42, "n1": 35, "att1": 0, "n2": 38, "n3": 118}
SHARES["att1"] = SORT_J - sum(SHARES.values())
ENDS = [sum(list(SHARES.values())[:n]) for n in range(len(SHARES) + 1)]
SCATTER = {phase: (ENDS[n], ENDS[n + 1]) for n, phase in enumerate(SHARES)}


def scatter_by_source(gp, g, phase, s_sc):
    for j in range(*SCATTER[phase]):
        gp.indirect_dma_start(g.rec_s_dram, bass.IndirectOffsetOnAxis(g.pos_s[:, j:j + 1], axis=0),
                              g.recs_s[:, j, :], None).then_inc(s_sc, 16)


def scattered(sp, phase, s_sc):
    first, end = SCATTER[phase]
    sp.wait_ge(s_sc, 16 * (end - first))


def layer_norm(v, ch, g, s_var, s_std):
    full = [P, N_BINS, D]
    ch.do(v.tensor_reduce(g.mu[:], g.X[:], AX.X, ALU.add))
    ch.do(v.tensor_single_scalar(g.mu[:], g.mu[:], 1.0 / D, ALU.mult))
    ch.do(v.tensor_tensor(g.H[:], g.X[:], g.mu[:].unsqueeze(2).broadcast_to(full), ALU.subtract))
    ch.do(v.tensor_tensor(g.TMP[:], g.H[:], g.H[:], ALU.mult))
    ch.do(v.tensor_reduce(g.var[:], g.TMP[:], AX.X, ALU.add))
    ch.do(v.tensor_scalar(g.var[:], g.var[:], 1.0 / D, EPS, ALU.mult, ALU.add))
    v.sem_inc(s_var, 1)
    v.wait_ge(s_std, 1)
    ch.do(v.reciprocal(g.var[:], g.std[:]))
    ch.do(v.scalar_tensor_tensor(g.H[:], g.H[:], 0.0, g.var[:].unsqueeze(2).broadcast_to(full),
                                 ALU.max, ALU.mult))


def node_phase(nc, g, layer, tables):
    with Core(nc, f"n{layer}") as c:
        ht = c.sb("ht", [D, N_ROWS])
        wt = c.sb("wt", [D, D])
        p_t = [c.ps(f"t{i}") for i in range(2)]
        p_m = [c.ps(f"m{i}") for i in range(5)]
        s_var, s_std, s_h, s_v = c.sem("var"), c.sem("std"), c.sem("h"), c.sem("v")
        s_t, s_tc, s_w, s_wc, s_m, s_mc, s_tab = (c.sem(n) for n in ("t", "tc", "w", "wc", "m", "mc", "tab"))
        s_row, s_ma, s_sc, s_ld = (c.sem(n) for n in "row ma sc ld".split())
        groups = [range(a, min(a + 4, N_BINS)) for a in range(0, N_BINS, 4)]
        if layer == 0:
            stage = c.sb("stage", [P, N_BINS, 32])
        if layer in (1, 2):
            heads = 4 if layer == 1 else 8
            f = D // heads
            stage = c.sb("stage", [P, N_BINS, heads, f + 1])
        if layer == 3:
            ring = 3
            stage = c.sb("stage", [P, ring, N_REL * D])
            s_out = c.sems("out", ring)
        block = c.block()

        @block.scalar
        def _(act):
            act.wait_ge(s_var, 1)
            act.activation(g.std[:], g.var[:], ACT.Sqrt).then_inc(s_std, 1)
            for n, bins in enumerate(groups):
                act.wait_ge(s_t, n + 1)
                act.copy(ht[:, bins[0] * P:(bins[-1] + 1) * P],
                         p_t[n % 2][:, 0:len(bins) * P]).then_inc(s_tc, 1)
            if layer in (1, 2):
                for a in range(N_BINS):
                    act.wait_ge(s_m, a + 1)
                    act.copy(stage[:, a, :, 0:f],
                             p_m[a % 4][:, 0:D].rearrange("p (h f) -> p h f", h=heads)).then_inc(s_mc, 1)
            if layer == 3:
                for a in range(N_BINS):
                    for part in (1, 3):
                        n = 5 * a + part
                        act.wait_ge(s_m, n + 1)
                        if part == 1 and a >= ring:
                            act.wait_ge(s_out[a % ring], 16 * (a // ring))
                        act.copy(stage[:, a % ring, (part - 1) * 512:part * 512], p_m[n % 5][:]).then_inc(s_ma, 1)

        @block.tensor
        def _(pe):
            if layer in (2, 3):
                pe.transpose(p_m[3][:, 0:D], (g.w2 if layer == 2 else g.w_self)[:], g.ident[:]).then_inc(s_w, 1)
            pe.wait_ge(s_h, 1)
            for n, bins in enumerate(groups):
                if n >= 2:
                    pe.wait_ge(s_tc, n - 1)
                for a in bins:
                    mm = pe.transpose(p_t[n % 2][:, (a - bins[0]) * P:(a - bins[0] + 1) * P],
                                      g.H[:, a, :], g.ident[:])
                mm.then_inc(s_t, 1)
            if layer in (2, 3):
                pe.wait_ge(s_wc, 1)
            n_m = 0
            for a in range(N_BINS):
                pe.wait_ge(s_tc, a // 4 + 1)
                lhs = ht[:, a * P:(a + 1) * P]

                def out(parts):
                    nonlocal n_m
                    if layer == 3 and n_m >= 5:
                        a_, part = divmod(n_m - 5, 5)
                        if part % 2:
                            pe.wait_ge(s_ma, 2 * a_ + part // 2 + 1)
                        else:
                            pe.wait_ge(s_mc, 3 * a_ + part // 2 + 1)
                    if layer != 3 and n_m >= 4:
                        pe.wait_ge(s_mc, n_m - 3)
                    bank = p_m[n_m % (5 if layer == 3 else 4)]
                    for at, w in parts:
                        mm = pe.matmul(bank[:, at:at + w.shape[-1]], lhs, w, start=True, stop=True)
                    mm.then_inc(s_m, 1)
                    n_m += 1

                if layer == 0:
                    out([(0, g.we1_src[:]), (HID1, g.wn1_dst[:]), (HID1 + HID2, g.we1_dst[:])])
                if layer == 1:
                    out([(0, g.w1[:])])
                if layer == 2:
                    out([(0, wt[:])])
                if layer == 3:
                    out([(0, wt[:])])
                    for r in range(0, N_REL, 4):
                        out([(0, g.wall[:, r:r + 4, :].rearrange("i r o -> i (r o)"))])

        @block.vector
        def _(v):
            ch = Chain(v, s_v)
            if layer in (2, 3):
                v.wait_ge(s_w, 1)
                v.tensor_copy(wt[:], p_m[3][:, 0:D]).then_inc(s_wc, 1)
            layer_norm(v, ch, g, s_var, s_std)
            v.sem_inc(s_h, 1)
            if layer == 0:
                for a in range(N_BINS):
                    v.wait_ge(s_m, a + 1)
                    v.tensor_copy(stage[:, a, :], p_m[a % 4][:, 0:32])
                    v.tensor_tensor(g.dst0[:, a, :], p_m[a % 4][:, 32:P], g.bias0[:], ALU.add).then_inc(s_mc, 1)
                v.wait_ge(s_mc, N_BINS)
                v.sem_inc(s_tab, 1)
                ch.do(v.tensor_tensor(g.X[:], g.X[:], g.H[:], ALU.add))
            if layer in (1, 2):
                for side in range(2):
                    if layer == 1:
                        a_row = g.a1[:, side, :].rearrange("p (h f) -> p h f", h=heads)
                    else:
                        a_row = g.a2[:, side, :].rearrange("p (f h) -> p h f", h=heads)
                    prod = g.TMP[:].rearrange("p a (h f) -> p a h f", h=heads)
                    for a in range(N_BINS):
                        if side == 0:
                            v.wait_ge(s_mc, a + 1)
                        ins = v.tensor_tensor(prod[:, a], stage[:, a, :, 0:f], a_row, ALU.mult)
                    ch.do(ins)
                    where = stage[:, :, :, f] if side == 0 else g.tgt[:, :, 0:heads]
                    ch.do(v.tensor_reduce(where, prod, AX.X, ALU.add))
                    if side == 0:
                        v.sem_inc(s_tab, 1)
            if layer == 3:
                for a in range(N_BINS):
                    for part in (0, 2, 4):
                        n = 5 * a + part
                        v.wait_ge(s_m, n + 1)
                        if part == 0:
                            v.tensor_tensor(g.X[:, a, :], g.X[:, a, :], p_m[n % 5][:, 0:D],
                                            ALU.add).then_inc(s_mc, 1)
                            continue
                        if part == 2 and a >= ring:
                            v.wait_ge(s_out[a % ring], 16 * (a // ring))
                        v.tensor_copy(stage[:, a % ring, (part - 1) * 512:part * 512],
                                      p_m[n % 5][:]).then_inc(s_mc, 1)

        @block.gpsimd
        def _(gp):
            scatter_by_source(gp, g, f"n{layer}", s_sc)

        @block.sync
        def _(sp):
            if layer == 3:
                rows = tables.rearrange("(a n r) f -> a n (r f)", a=N_BINS, n=P)
                for a in range(N_BINS):
                    sp.wait_ge(s_mc, 3 * a + 3)
                    sp.wait_ge(s_ma, 2 * a + 2)
                    sp.dma_start(rows[a], stage[:, a % ring, :]).then_inc(s_out[a % ring], 16)
                for n in range(ring):
                    sp.wait_ge(s_out[n], 16 * len(range(n, N_BINS, ring)))
            else:
                sp.wait_ge(s_tab, 1)
                src = stage[:] if layer == 0 else stage[:].rearrange("p a h f -> p a (h f)")
                sp.dma_start(tables.rearrange("(a n) f -> n a f", a=N_BINS), src).then_inc(s_row, 16)
                sp.wait_ge(s_row, 16)
            scattered(sp, f"n{layer}", s_sc)
            if layer == 3:
                sp.dma_start(g.rec_s[:].rearrange("p (k t) w -> p k (t w)", t=TILES),
                             as_blocks(g.rec_s_dram)).then_inc(s_ld, 16)
                sp.wait_ge(s_ld, 16)


def rec_f(rec, k):
    return rec[:, bass.ds(k * TILES, TILES), 1:2].bitcast(F32).broadcast_to([P, TILES, P])


def ge(eng, sem, value):
    if isinstance(value, int) and value <= 0:
        return
    eng.wait_ge(sem, value)


def tick(eng, sem):
    eng.sem_inc(sem, 1)


def gather_stages(act, gp, rec, words, index, rows, tables, s_ix, s_g, s_tick, s_free):
    per = 16 * TILES * len(rows)

    def lay(k, q, b):
        ge(act, s_g[b], q * per)
        for n, w in enumerate(words):
            ins = act.copy(index[b][:, n, :], rec[:, bass.ds(k * TILES, TILES), w])
        ins.then_inc(s_ix, 1)

    def gather(k, q, b):
        ge(gp, s_free, k - (UNROLL - 1))
        gp.wait_ge(s_ix, k + 1)
        tick(gp, s_tick)
        for n in range(len(rows)):
            for t in range(TILES):
                gp.indirect_dma_start(rows[n][b][:, t, :], None, tables[n],
                                      bass.IndirectOffsetOnAxis(index[b][:, n, t:t + 1], axis=0)).then_inc(s_g[b], 16)

    return lay, gather


def edge_mlp(nc, g, edge_attr, edges_dram, rec_d_dram):
    with Core(nc, "mlp") as c:
        hot = [c.sb(f"hot{b}", [P, TILES, P]) for b in range(UNROLL)]
        index = [c.sb(f"index{b}", [P, 2, TILES], I32) for b in range(UNROLL)]
        row = [c.sb(f"row{b}", [P, TILES, IN_D]) for b in range(UNROLL)]
        hot_t = [c.sb(f"hot_t{b}", [P, BLOCK]) for b in range(2)]
        row_t = [c.sb(f"row_t{b}", [IN_D, BLOCK]) for b in range(2)]
        dst = [c.sb(f"dst{b}", [P, IN_D]) for b in range(UNROLL)]
        h1 = [c.sb(f"h1{b}", [32, BLOCK]) for b in range(2)]
        em = [c.sb(f"em{b}", [P, BLOCK]) for b in range(2)]
        h2 = [c.sb(f"h2{b}", [EDGE_D + 1, BLOCK]) for b in range(2)]
        nm = [c.sb(f"nm{b}", [P, TILES, D]) for b in range(2)]
        p_hot, p_row, p_em, p_nm, p_sum = (c.ps(n) for n in "hot row em nm sum".split())
        p_h = [c.ps(f"h{b}") for b in range(2)]
        s_g, s_tick = c.sems("g", UNROLL), c.sem("tick")
        (s_ix, s_init, s_hot, s_turn, s_turned, s_dst, s_h1, s_h1r, s_em, s_emr, s_h2, s_h2r, s_nm, s_nmr,
         s_sum, s_acc) = (c.sem(n) for n in "ix init hot turn turned dst h1 h1r em emr h2 h2r nm nmr sum acc".split())
        s_e, s_r = c.sems("e", UNROLL), c.sems("r", UNROLL)
        own = [c.sb(f"own{b}", [P, TILES]) for b in range(2)]
        s_own, s_loc, s_sc = c.sem("own"), c.sem("loc"), c.sems("sc", UNROLL)
        place = [c.sb(f"place{b}", [SORT_P, 1], I32) for b in range(UNROLL)]
        moved = [c.sb(f"moved{b}", [SORT_P, SW], I32) for b in range(UNROLL)]
        block = c.block()
        src_rows = [r[:, :, EDGE_D:IN_D] for r in row]
        io = (g.rec_d, (0, 2), index, (src_rows,), (g.tab0,), s_ix, s_g, s_tick, s_turn)

        @block.gpsimd
        def _(gp):
            for b in range(2):
                gp.memset(h2[b][EDGE_D:EDGE_D + 1, :], 1.0).then_inc(s_init, 1)
                gp.wait_ge(s_init, b + 1)
            gp.memset(g.acc[:, :, 0:D], 0.0).then_inc(s_init, 1)
            unsorted = gp.value_load(g.unsorted[0:1, 0:1], min_val=0, max_val=1)

            def gather_edges(k, q, b):
                with gp.If(unsorted > 0):
                    for t in range(TILES):
                        gp.indirect_dma_start(row[b][:, t, 0:EDGE_D], None, edge_attr,
                                              bass.IndirectOffsetOnAxis(index[b][:, 1, t:t + 1], axis=0)
                                              ).then_inc(s_e[b], 16)

            def scatter(k, q, b):
                if b % 2:
                    return
                gp.indirect_dma_start(g.rec_s_dram, bass.IndirectOffsetOnAxis(place[b][:], axis=0),
                                      moved[b][:], None).then_inc(s_sc[b], 16)
            pipeline(gp, [(0, gather_stages(None, gp, *io)[1]), (0, gather_edges), (0, scatter)])

        @block.sync
        def _(sp):
            unsorted = sp.value_load(g.unsorted[0:1, 0:1], min_val=0, max_val=1)

            def records_to(k):
                return g.rec_d[:, bass.ds(k * TILES, TILES), :].rearrange("p t w -> p (t w)")

            def load_run(k, q, b):
                ge(sp, s_turn, k - (UNROLL - 1))
                tick(sp, s_tick)
                start = sp.value_load(g.start[0:1, bass.ds(k, 1)], min_val=0, max_val=N_EDGES - BLOCK)
                sp.dma_start(records_to(k), edges_dram[bass.ds(start, BLOCK), :].rearrange("(p t) w -> p (t w)", p=P)
                             ).then_inc(s_r[b], 16)
                sp.dma_start(row[b][:, :, 0:EDGE_D],
                             edge_attr[bass.ds(start, BLOCK), :].rearrange("(p t) f -> p t f", p=P)
                             ).then_inc(s_e[b], 16 * TILES)

            def load_sorted(k, q, b):
                ge(sp, s_turn, k - (UNROLL - 1))
                tick(sp, s_tick)
                sp.dma_start(records_to(k), rec_d_dram[bass.ds(k * BLOCK, BLOCK), :].rearrange(
                    "(p t) w -> p (t w)", p=P)).then_inc(s_r[b], 16)

            with sp.If(unsorted < 1):
                pipeline(sp, [(0, load_run)])
            with sp.If(unsorted > 0):
                pipeline(sp, [(0, load_sorted)])
            for b in range(0, UNROLL, 2):
                sp.wait_ge(s_sc[b], 16 * (N_BLOCKS // UNROLL))

        @block.scalar
        def _(act):
            lay = gather_stages(act, None, *io)[0]

            def lay_both(k, q, b):
                ge(act, s_e[b], 16 * TILES * q)
                act.wait_ge(s_r[b], 16 * (q + 1))
                if b % 2 == 0:
                    j = q * (UNROLL // 2) + b // 2
                    ge(act, s_sc[b], 16 * q)
                    act.copy(place[b][:], g.pos_s[:, bass.ds(j, 1)])
                    act.copy(moved[b][:, 0:1], g.recs_s[:, bass.ds(j, 1), 0])
                    act.copy(moved[b][:, 1:2].bitcast(F32), g.recs_s[:, bass.ds(j, 1), 1].bitcast(F32))
                lay(k, q, b)

            def turned(k, q, b):
                act.wait_ge(s_turn, k + 1)
                ge(act, s_h1, k - 1)
                act.copy(hot_t[b % 2][:], p_hot[:])
                act.copy(row_t[b % 2][:], p_row[0:IN_D, :]).then_inc(s_turned, 1)

            def h1_relu(k, q, b):
                act.wait_ge(s_h1, k + 1)
                ge(act, s_em, k - 1)
                act.activation(h1[b % 2][:], p_h[b % 2][HID2:HID2 + HID1, :], ACT.Relu).then_inc(s_h1r, 1)

            def em_relu(k, q, b):
                act.wait_ge(s_em, k + 1)
                ge(act, s_h2, k - 1)
                act.activation(em[b % 2][:], p_em[:], ACT.Relu, bias=g.be2[:]).then_inc(s_emr, 1)

            def h2_relu(k, q, b):
                act.wait_ge(s_h2, k + 1)
                ge(act, s_nm, k - 1)
                act.activation(h2[b % 2][0:HID2, :], p_h[b % 2][0:HID2, :], ACT.Relu).then_inc(s_h2r, 1)

            pipeline(act, [(0, lay_both), (3, turned), (5, h2_relu), (4, h1_relu), (4, em_relu)])

        @block.tensor
        def _(pe):
            pe.wait_ge(s_init, 3)

            def turn(k, q, b):
                ge(pe, s_turned, k)
                pe.wait_ge(s_hot, k + 1)
                for t in range(TILES):
                    pe.transpose(p_hot[:, t * P:(t + 1) * P], hot[b][:, t, :], g.ident[:])
                pe.wait_ge(s_e[b], 16 * TILES * (q + 1))
                pe.wait_ge(s_g[b], 16 * TILES * (q + 1))
                tick(pe, s_tick)
                for t in range(TILES):
                    mm = pe.transpose(p_row[0:IN_D, t * P:(t + 1) * P], row[b][:, t, :], g.ident[:])
                mm.then_inc(s_turn, 1)

            def mm_h1(k, q, b):
                ge(pe, s_h2r, k - 1)
                pe.wait_ge(s_turned, k + 1)
                pe.wait_ge(s_dst, k + 1)
                tick(pe, s_tick)
                pe.matmul(p_h[b % 2][0:IN_D, :], dst[b][:], hot_t[b % 2][:], start=True, stop=False)
                pe.matmul(p_h[b % 2][HID2:HID2 + HID1, :], g.we1_row[:], row_t[b % 2][:],
                          start=False, stop=True).then_inc(s_h1, 1)

            def mm_em(k, q, b):
                ge(pe, s_emr, k)
                pe.wait_ge(s_h1r, k + 1)
                tick(pe, s_tick)
                pe.matmul(p_em[:], g.we2[:], h1[b % 2][:], start=True, stop=True).then_inc(s_em, 1)

            def mm_h2(k, q, b):
                pe.wait_ge(s_emr, k + 1)
                tick(pe, s_tick)
                pe.matmul(p_h[b % 2][0:HID2, :], g.wn1_msg[:], em[b % 2][:],
                          start=False, stop=True).then_inc(s_h2, 1)

            def mm_nm(k, q, b):
                ge(pe, s_nmr, k)
                pe.wait_ge(s_h2r, k + 1)
                tick(pe, s_tick)
                for t in range(TILES):
                    mm = pe.matmul(p_nm[:, t * P:(t + 1) * P], h2[b % 2][:, t * P:(t + 1) * P], g.wn2b[:],
                                   start=True, stop=True)
                mm.then_inc(s_nm, 1)

            def mm_sum(k, q, b):
                ge(pe, s_acc, k)
                pe.wait_ge(s_nmr, k + 1)
                for t in range(TILES):
                    mm = pe.matmul(p_sum[:, 0:D], hot[b][:, t, :], nm[b % 2][:, t, :],
                                   start=(t == 0), stop=(t == TILES - 1))
                mm.then_inc(s_sum, 1)

            pipeline(pe, [(1, turn), (3, mm_h2), (2, mm_h1), (4, mm_sum), (2, mm_em), (3, mm_nm)])

        @block.vector
        def _(v):
            v.wait_ge(s_init, 3)

            def localize(k, q, b):
                words = g.rec_d[:, bass.ds(k * TILES, TILES), :]
                target, edge = words[:, :, 1].bitcast(F32), words[:, :, 3].bitcast(F32)
                v.wait_ge(s_r[b], 16 * (q + 1))
                v.tensor_scalar(own[b % 2][:], edge, g.first[:, bass.ds(k, 1)], None, ALU.is_ge).then_inc(s_own, 1)
                v.wait_ge(s_own, k + 1)
                v.scalar_tensor_tensor(target, target, g.shift[:, bass.ds(k, 1)], own[b % 2][:],
                                       ALU.add, ALU.mult).then_inc(s_loc, 1)

            def make_hot(k, q, b):
                v.wait_ge(s_loc, k + 1)
                ge(v, s_sum, k - (UNROLL - 1))
                v.tensor_tensor(hot[b][:], g.iota[:].unsqueeze(1).broadcast_to([P, TILES, P]), rec_f(g.rec_d, k),
                                ALU.is_equal).then_inc(s_hot, 1)

            def bring_dst(k, q, b):
                ge(v, s_h1, k - (UNROLL - 1))
                a = bin_register(v, g.bin_d, k, s_tick)
                v.tensor_copy(dst[b][:].unsqueeze(1), g.dst0[:, bass.ds(a, 1), :]).then_inc(s_dst, 1)

            def nm_relu(k, q, b):
                v.wait_ge(s_nm, k + 1)
                ge(v, s_sum, k - 1)
                v.tensor_scalar_max(nm[b % 2][:].rearrange("p t f -> p (t f)"), p_nm[:], 0.0).then_inc(s_nmr, 1)

            pipeline(v, [(0, localize), (0, make_hot), (0, bring_dst), (4, nm_relu),
                         (5, add_sum(v, g, g.bin_d, p_sum, D, 1, s_sum, s_acc, s_tick))])


def bin_register(v, bin_of, k, s_tick):
    tick(v, s_tick)
    return v.value_load(bin_of[0:1, bass.ds(k, 1)], min_val=0, max_val=N_BINS - 1)


def add_sum(v, g, bin_of, p_sum, width, ring, s_sum, s_acc, s_tick):
    def fn(k, q, b):
        bank = p_sum if ring == 1 else p_sum[b % ring]
        v.wait_ge(s_sum, k + 1)
        ge(v, s_acc, k)
        a = bin_register(v, bin_of, k, s_tick)
        there = g.acc[:, bass.ds(a, 1), 0:width]
        v.tensor_tensor(there, there, bank[:, 0:width].unsqueeze(1), ALU.add).then_inc(s_acc, 1)
    return fn


def finish(nc, g, layer, out=None):
    with Core(nc, f"f{layer}") as c:
        s_v, s_sum, s_o = c.sem("v"), c.sem("sum"), c.sem("o")
        block = c.block()

        @block.vector
        def _(v):
            ch = Chain(v, s_v)
            if layer in (1, 2):
                heads = 4 if layer == 1 else 8
                f = D // heads
                acc = g.acc[:, :, 0:heads * (f + 1)].rearrange("p a (h f) -> p a h f", h=heads)
                den = g.den[:, :, 0:heads]
                tmp = g.TMP[:].rearrange("p a (h f) -> p a h f", h=heads)
                ch.do(v.scalar_tensor_tensor(den, acc[:, :, :, f], 0.0, acc[:, :, :, f], ALU.is_equal, ALU.add))
                ch.do(v.reciprocal(den, den))
                for a in range(N_BINS):
                    ins = v.tensor_tensor(tmp[:, a], acc[:, a, :, 0:f],
                                          den[:, a, :].unsqueeze(2).broadcast_to([P, heads, f]), ALU.mult)
                ch.do(ins)
                if layer == 2:
                    ch.do(v.tensor_tensor(g.TMP[:], g.TMP[:],
                                          g.bias2[:].unsqueeze(1).broadcast_to([P, N_BINS, D]), ALU.add))
                ch.do(v.tensor_tensor(g.X[:], g.X[:], g.TMP[:], ALU.add))
            else:
                ch.do(v.tensor_tensor(g.X[:], g.X[:], g.acc[:, :, 0:D], ALU.add))
            v.sem_inc(s_sum, 1)

        if out is not None:
            @block.sync
            def _(sp):
                sp.wait_ge(s_sum, 1)
                sp.dma_start(out[0:FULL * P, :].rearrange("(a b) f -> b a f", b=P), g.X[:, 0:FULL, :]).then_inc(s_o, 16)
                sp.dma_start(out[FULL * P:N_NODES, :], g.X[0:LAST, FULL, :]).then_inc(s_o, 16)
                sp.wait_ge(s_o, 32)


def relation_sum(nc, g):
    with Core(nc, "rel") as c:
        hot = [c.sb(f"hot{b}", [P, TILES, P]) for b in range(UNROLL)]
        index = [c.sb(f"index{b}", [P, 1, TILES], I32) for b in range(UNROLL)]
        row = [c.sb(f"row{b}", [P, TILES, D]) for b in range(UNROLL)]
        p_sum = [c.ps(f"sum{b}") for b in range(2)]
        s_g, s_tick = c.sems("g", UNROLL), c.sem("tick")
        s_ix, s_init, s_hot, s_sum, s_acc = (c.sem(n) for n in "ix init hot sum acc".split())
        block = c.block()
        io = (g.rec_s, (0,), index, (row,), (g.tab3,), s_ix, s_g, s_tick, s_sum)

        @block.gpsimd
        def _(gp):
            gp.memset(g.acc[:, :, 0:D], 0.0).then_inc(s_init, 1)
            pipeline(gp, [(0, gather_stages(None, gp, *io)[1])])

        @block.scalar
        def _(act):
            pipeline(act, [(0, gather_stages(act, None, *io)[0])])

        @block.tensor
        def _(pe):
            def mm_sum(k, q, b):
                ge(pe, s_acc, k - 1)
                pe.wait_ge(s_hot, k + 1)
                pe.wait_ge(s_g[b], 16 * TILES * (q + 1))
                for t in range(TILES):
                    mm = pe.matmul(p_sum[b % 2][:, 0:D], hot[b][:, t, :], row[b][:, t, :],
                                   start=(t == 0), stop=(t == TILES - 1))
                mm.then_inc(s_sum, 1)
            pipeline(pe, [(0, mm_sum)])

        @block.vector
        def _(v):
            v.wait_ge(s_init, 1)

            def make_hot(k, q, b):
                ge(v, s_sum, k - (UNROLL - 1))
                v.tensor_tensor(hot[b][:], g.iota[:].unsqueeze(1).broadcast_to([P, TILES, P]), rec_f(g.rec_s, k),
                                ALU.is_equal).then_inc(s_hot, 1)
            pipeline(v, [(0, make_hot), (1, add_sum(v, g, g.bin_s, p_sum, D, 2, s_sum, s_acc, s_tick))])


def segment_max(nc, g, staged):
    HEADS, W = 4, 132
    with Core(nc, "max") as c:
        hot = [c.sb(f"hot{b}", [P, TILES, P]) for b in range(UNROLL)]
        index = [c.sb(f"index{b}", [P, 1, TILES], I32) for b in range(UNROLL)]
        row = [c.sb(f"row{b}", [P, TILES, W]) for b in range(UNROLL)]
        mask = [c.sb(f"mask{b}", [P, BLOCK]) for b in range(2)]
        junk = c.sb("junk", [P, HEADS, BLOCK])
        top = [c.sb(f"top{b}", [P, HEADS]) for b in range(UNROLL)]
        p_hot = [c.ps(f"hot{b}") for b in range(2)]
        p_s = [c.ps(f"s{h}") for h in range(HEADS)]
        s_g, s_st, s_tick = c.sems("g", UNROLL), c.sems("st", UNROLL), c.sem("tick")
        s_ix, s_init, s_hot, s_turn, s_mask, s_all, s_red, s_top = (
            c.sem(n) for n in "ix init hot turn mask all red top".split())
        s_used = c.sem("used")
        block = c.block()
        io = (g.rec_d, (0,), index, (row,), (g.tab1,), s_ix, s_g, s_tick, s_used)

        @block.gpsimd
        def _(gp):
            gp.memset(g.top[:], -BIG).then_inc(s_init, 1)
            pipeline(gp, [(0, gather_stages(None, gp, *io)[1])])

        @block.sync
        def _(sp):
            def keep(k, q, b):
                sp.wait_ge(s_g[b], 16 * TILES * (q + 1))
                sp.dma_start(staged[bass.ds(k, 1)].rearrange("k p f -> (k p) f"),
                             row[b][:].rearrange("p t f -> p (t f)")).then_inc(s_st[b], 16)

            def kept(k, q, b):
                sp.wait_ge(s_st[b], 16 * (q + 1))
                tick(sp, s_tick)
                sp.wait_ge(s_all, HEADS * (k + 1))
                sp.sem_inc(s_used, 1)
            pipeline(sp, [(0, keep), (3, kept)])

        @block.scalar
        def _(act):
            lay = gather_stages(act, None, *io)[0]

            def make_mask(k, q, b):
                act.wait_ge(s_turn, k + 1)
                ge(act, s_red, HEADS * (k - 1))
                act.activation(mask[b % 2][:], p_hot[b % 2][:], ACT.Copy, scale=BIG, bias=-BIG).then_inc(s_mask, 1)
            pipeline(act, [(0, lay), (2, make_mask)])

        @block.tensor
        def _(pe):
            def turn(k, q, b):
                ge(pe, s_mask, k - 1)
                pe.wait_ge(s_hot, k + 1)
                for t in range(TILES):
                    mm = pe.transpose(p_hot[b % 2][:, t * P:(t + 1) * P], hot[b][:, t, :], g.ident[:])
                mm.then_inc(s_turn, 1)

            def spread(k, q, b):
                pe.wait_ge(s_g[b], 16 * TILES * (q + 1))
                for h in range(HEADS):
                    ge(pe, s_red, HEADS * (k - 1) + h + 1)
                    for t in range(TILES):
                        at = h * 33 + 32
                        mm = pe.transpose(p_s[h][:, t * P:(t + 1) * P],
                                          row[b][:, t, at:at + 1].broadcast_to([P, P]), g.ident[:])
                    mm.then_inc(s_all, 1)
            pipeline(pe, [(1, turn), (2, spread)])

        @block.vector
        def _(v):
            v.wait_ge(s_init, 1)

            def make_hot(k, q, b):
                ge(v, s_turn, k - (UNROLL - 1))
                v.tensor_tensor(hot[b][:], g.iota[:].unsqueeze(1).broadcast_to([P, TILES, P]), rec_f(g.rec_d, k),
                                ALU.is_equal).then_inc(s_hot, 1)

            def reduce(k, q, b):
                v.wait_ge(s_mask, k + 1)
                ge(v, s_top, k - (UNROLL - 1))
                for h in range(HEADS):
                    v.wait_ge(s_all, HEADS * k + h + 1)
                    ge(v, s_red, HEADS * (k - 1) + h + 1)
                    tick(v, s_tick)
                    v.tensor_tensor_reduce(out=junk[:, h, :], in0=mask[b % 2][:], in1=p_s[h][:], scale=1.0,
                                           scalar=-BIG, op0=ALU.add, op1=ALU.max,
                                           accum_out=top[b][:, h:h + 1]).then_inc(s_red, 1)

            def keep_top(k, q, b):
                v.wait_ge(s_red, HEADS * (k + 1))
                ge(v, s_top, k)
                a = bin_register(v, g.bin_d, k, s_tick)
                there = g.top[:, bass.ds(a, 1), :]
                v.tensor_tensor(there, there, top[b][:].unsqueeze(1), ALU.max).then_inc(s_top, 1)
            pipeline(v, [(0, make_hot), (2, reduce), (3, keep_top)])


def target_terms(nc, g):
    H = 4
    with Core(nc, "tt") as c:
        low = c.sb("low", [P, N_BINS, H])
        ex = c.sb("ex", [P, N_BINS, H])
        s_v, s_lo, s_ex = c.sem("v"), c.sem("lo"), c.sem("ex")
        block = c.block()

        @block.vector
        def _(v):
            ch = Chain(v, s_v)
            top = g.tgt[:, :, H:2 * H]
            ch.do(v.tensor_tensor(top, g.top[:], g.tgt[:, :, 0:H], ALU.add))
            ch.do(v.tensor_single_scalar(low[:], top, 0.0, ALU.min))
            v.sem_inc(s_lo, 1)
            v.wait_ge(s_ex, 1)
            ch.do(v.tensor_scalar(ex[:], ex[:], 0.2, -0.2, ALU.mult, ALU.add))
            ch.do(v.scalar_tensor_tensor(top, top, 0.0, ex[:], ALU.max, ALU.add))

        @block.scalar
        def _(act):
            act.wait_ge(s_lo, 1)
            act.activation(ex[:], low[:], ACT.Exp).then_inc(s_ex, 1)


def attention_sum(nc, g, layer, staged):
    heads = 4 if layer == 1 else 8
    f = D // heads
    W = heads * (f + 1)
    T = 2 * heads if layer == 1 else heads
    with Core(nc, f"att{layer}") as c:
        hot = [c.sb(f"hot{b}", [P, TILES, P]) for b in range(UNROLL)]
        index = [c.sb(f"index{b}", [P, 1, TILES], I32) for b in range(UNROLL)]
        row = [c.sb(f"row{b}", [P, TILES, heads, f + 1]) for b in range(UNROLL)]
        hot_t = [c.sb(f"hot_t{b}", [P, BLOCK]) for b in range(2)]
        tgt = [c.sb(f"tgt{b}", [P, T]) for b in range(UNROLL)]
        val = [c.sb(f"val{b}", [P, TILES, heads]) for b in range(UNROLL)]
        low = [c.sb(f"low{b}", [P, TILES, heads]) for b in range(UNROLL)]
        neg = [c.sb(f"neg{b}", [P, TILES, heads]) for b in range(UNROLL)]
        wgt = [c.sb(f"wgt{b}", [P, TILES, heads]) for b in range(UNROLL)]
        p_hot = [c.ps(f"hot{b}") for b in range(2)]
        p_t = [c.ps(f"t{b}") for b in range(2)]
        p_sum = [c.ps(f"sum{b}") for b in range(2)]
        s_g, s_tick = c.sems("g", UNROLL), c.sem("tick")
        (s_ix, s_init, s_hot, s_turn, s_turned, s_tgt, s_t, s_v2, s_neg, s_v3, s_v4, s_val, s_wgt, s_msg,
         s_sum, s_acc) = (c.sem(n) for n in
                          "ix init hot turn turned tgt t v2 neg v3 v4 val wgt msg sum acc".split())
        block = c.block()
        s_sc, s_read = c.sem("sc"), c.sem("read")
        most = [c.sb(f"most{b}", [P, TILES, heads]) for b in range(UNROLL)]
        lands = 16 if layer == 1 else 16 * TILES
        flat = [r[:].rearrange("p t h f -> p t (h f)") for r in row]
        io = (g.rec_d, (0,), index, (flat,), (g.tab2,), s_ix, s_g, s_tick, s_sum)

        @block.gpsimd
        def _(gp):
            gp.memset(g.acc[:, :, 0:W], 0.0).then_inc(s_init, 1)
            if layer == 2:
                pipeline(gp, [(0, gather_stages(None, gp, *io)[1])])
            else:
                scatter_by_source(gp, g, "att1", s_sc)

        if layer == 1:
            @block.sync
            def _(sp):
                def load(k, q, b):
                    ge(sp, s_sum, k - (UNROLL - 1))
                    sp.dma_start(row[b][:].rearrange("p t h f -> p (t h f)"),
                                 staged[bass.ds(k, 1)].rearrange("k p f -> (k p) f")).then_inc(s_g[b], 16)
                pipeline(sp, [(0, load)])
                scattered(sp, "att1", s_sc)

        @block.scalar
        def _(act):
            lay = gather_stages(act, None, *io)[0]

            def bring_tgt(k, q, b):
                ge(act, s_t, k - (UNROLL - 1))
                a = bin_register(act, g.bin_d, k, s_tick)
                act.copy(tgt[b][:].unsqueeze(1), g.tgt[:, bass.ds(a, 1), 0:T]).then_inc(s_tgt, 1)

            def turned(k, q, b):
                act.wait_ge(s_turn, k + 1)
                ge(act, s_t, k - 1)
                act.copy(hot_t[b % 2][:], p_hot[b % 2][:]).then_inc(s_turned, 1)

            def negative(k, q, b):
                act.wait_ge(s_v2, k + 1)
                ge(act, s_v4, k - (UNROLL - 1))
                act.activation(neg[b][:], low[b][:], ACT.Exp).then_inc(s_neg, 1)

            def weight(k, q, b):
                act.wait_ge(s_val, k + 1)
                ge(act, s_msg, k - (UNROLL - 1))
                act.activation(wgt[b][:], val[b][:], ACT.Exp).then_inc(s_wgt, 1)
            if layer == 1:
                pipeline(act, [(0, bring_tgt), (1, turned), (3, negative), (4, weight)])
            else:
                pipeline(act, [(0, lay), (3, bring_tgt), (3, turned), (5, weight)])

        @block.tensor
        def _(pe):
            def turn(k, q, b):
                ge(pe, s_turned, k - 1)
                pe.wait_ge(s_hot, k + 1)
                for t in range(TILES):
                    mm = pe.transpose(p_hot[b % 2][:, t * P:(t + 1) * P], hot[b][:, t, :], g.ident[:])
                mm.then_inc(s_turn, 1)

            def take(k, q, b):
                ge(pe, s_read, k - 1)
                pe.wait_ge(s_turned, k + 1)
                pe.wait_ge(s_tgt, k + 1)
                for t in range(TILES):
                    mm = pe.matmul(p_t[b % 2][:, t * T:(t + 1) * T], hot_t[b % 2][:, t * P:(t + 1) * P],
                                   tgt[b][:], start=True, stop=True)
                mm.then_inc(s_t, 1)

            def mm_sum(k, q, b):
                ge(pe, s_acc, k - 1)
                pe.wait_ge(s_msg, k + 1)
                for t in range(TILES):
                    mm = pe.matmul(p_sum[b % 2][:, 0:W], hot[b][:, t, :], flat[b][:, t, :],
                                   start=(t == 0), stop=(t == TILES - 1))
                mm.then_inc(s_sum, 1)
            pipeline(pe, [(3, take), (1, turn), (5 if layer == 2 else 7, mm_sum)])

        @block.vector
        def _(v):
            v.wait_ge(s_init, 1)

            def make_hot(k, q, b):
                ge(v, s_sum, k - (UNROLL - 1))
                v.tensor_tensor(hot[b][:], g.iota[:].unsqueeze(1).broadcast_to([P, TILES, P]), rec_f(g.rec_d, k),
                                ALU.is_equal).then_inc(s_hot, 1)

            def there(b):
                return p_t[b % 2][:, 0:TILES * T].rearrange("p (t w) -> p t w", t=TILES)

            def score(k, q, b):
                v.wait_ge(s_g[b], lands * (q + 1))
                v.wait_ge(s_t, k + 1)
                ge(v, s_wgt, k - (UNROLL - 1))
                x = val[b][:]
                ins = v.tensor_tensor(x, row[b][:, :, :, f], there(b)[:, :, 0:heads], ALU.add)
                if layer == 1:
                    ins = v.tensor_copy(most[b][:], there(b)[:, :, heads:T])
                ins.then_inc(s_read, 1)
                if layer == 2:
                    v.wait_ge(s_read, k + 1)
                    v.scalar_tensor_tensor(x, x, 0.2, x, ALU.mult, ALU.max).then_inc(s_val, 1)

            def cut(k, q, b):
                v.wait_ge(s_read, k + 1)
                v.tensor_scalar_min(low[b][:], val[b][:], 0.0).then_inc(s_v2, 1)

            def scale(k, q, b):
                v.wait_ge(s_neg, k + 1)
                v.tensor_scalar(neg[b][:], neg[b][:], 0.2, -0.2, ALU.mult, ALU.add).then_inc(s_v3, 1)

            def elu(k, q, b):
                v.wait_ge(s_v3, k + 1)
                v.scalar_tensor_tensor(val[b][:], val[b][:], 0.0, neg[b][:], ALU.max, ALU.add).then_inc(s_v4, 1)

            def less_most(k, q, b):
                v.wait_ge(s_v4, k + 1)
                v.tensor_tensor(val[b][:], val[b][:], most[b][:], ALU.subtract).then_inc(s_val, 1)

            def message(k, q, b):
                v.wait_ge(s_wgt, k + 1)
                v.tensor_copy(row[b][:, :, :, f], wgt[b][:])
                for t in range(TILES):
                    ins = v.tensor_tensor(row[b][:, t, :, 0:f], row[b][:, t, :, 0:f],
                                          wgt[b][:, t, :].unsqueeze(2).broadcast_to([P, heads, f]), ALU.mult)
                ins.then_inc(s_msg, 1)

            add = add_sum(v, g, g.bin_d, p_sum, W, 2, s_sum, s_acc, s_tick)
            if layer == 1:
                pipeline(v, [(3, score), (4, scale), (0, make_hot), (3, cut), (4, elu), (6, message), (8, add),
                             (4, less_most)])
            else:
                pipeline(v, [(0, make_hot), (3, score), (4, message), (6, add)])


def graph_layers(nc, args, out):
    g = Shared()
    with ExitStack() as ctx:
        def sb(name, shape, dt=F32):
            return ctx.enter_context(nc.sbuf_tensor(name, shape, dt))

        def dram(name, shape, dt=F32):
            return nc.dram_tensor(name, shape, dt).ap()

        g.ident, g.ones, g.earlier = sb("ident", [P, P]), sb("ones", [P, P]), sb("earlier", [P, P])
        g.iota, g.iota_blocks = sb("iota", [P, P]), sb("iota_blocks", [P, N_BLOCKS])
        g.rec_d, g.rec_s = sb("rec_d", [P, N_POS // P, DW], I32), sb("rec_s", [P, N_POS // P, SW], I32)
        g.bin_d, g.bin_s = sb("bin_d", [1, N_BLOCKS], I32), sb("bin_s", [1, N_BLOCKS], I32)
        rec_d_dram, g.rec_s_dram = dram("rec_d_dram", [N_POS, DW], I32), dram("rec_s_dram", [N_POS, SW], I32)
        g.recs_s, g.pos_s = sb("recs_s", [SORT_P, SORT_J, SW], I32), sb("pos_s", [SORT_P, SORT_J], I32)
        g.start, g.unsorted = sb("start", [1, N_BLOCKS], I32), sb("unsorted", [1, 1], I32)
        g.first, g.shift = sb("first", [P, N_BLOCKS]), sb("shift", [P, N_BLOCKS])
        g.wall = sb("wall", [D, N_REL, D])
        edges_dram = dram("edges_dram", [N_EDGES, DW], I32)
        g.X = sb("X", [P, N_BINS, D])
        g.we1_src, g.we1_dst = sb("we1_src", [D, HID1]), sb("we1_dst", [D, HID1])
        g.we1_row = sb("we1_row", [IN_D, HID1])
        g.we2, g.wn1_dst, g.wn1_msg = sb("we2", [32, D]), sb("wn1_dst", [D, 64]), sb("wn1_msg", [D, 64])
        g.wn2b, g.be2, g.bias0 = sb("wn2b", [65, D]), sb("be2", [P, 1]), sb("bias0", [P, 96])
        g.w1, g.w2, g.w_self = sb("w1", [D, D]), sb("w2", [D, D]), sb("w_self", [D, D])
        g.a1, g.a2, g.bias2 = sb("a1", [P, 2, D]), sb("a2", [P, 2, D]), sb("bias2", [P, D])
        constants(nc, g)
        order_edges(nc, g, args, edges_dram, rec_d_dram)

        g.H, g.TMP = sb("H", [P, N_BINS, D]), sb("TMP", [P, N_BINS, D])
        g.mu, g.var, g.std = (sb(n, [P, N_BINS]) for n in ("mu", "var", "std"))
        g.acc = sb("acc", [P, N_BINS, 136])
        g.den, g.tgt, g.top = sb("den", [P, N_BINS, 8]), sb("tgt", [P, N_BINS, 8]), sb("top", [P, N_BINS, 4])
        g.dst0 = sb("dst0", [P, N_BINS, 96])
        g.tab0, g.tab1, g.tab2 = dram("tab0", [N_ROWS, 32]), dram("tab1", [N_ROWS, 132]), dram("tab2", [N_ROWS, 136])
        g.tab3 = dram("tab3", [N_ROWS * N_REL, D])
        staged = dram("staged", [N_BLOCKS, P, TILES * 132])
        node_phase(nc, g, 0, g.tab0)
        edge_mlp(nc, g, args["edge_attr"], edges_dram, rec_d_dram)
        finish(nc, g, 0)
        node_phase(nc, g, 1, g.tab1)
        segment_max(nc, g, staged)
        target_terms(nc, g)
        attention_sum(nc, g, 1, staged)
        finish(nc, g, 1)
        node_phase(nc, g, 2, g.tab2)
        attention_sum(nc, g, 2, None)
        finish(nc, g, 2)
        node_phase(nc, g, 3, g.tab3)
        relation_sum(nc, g)
        finish(nc, g, 3, out)


_INS = {
    "x": "x", "src": "src", "dst": "dst", "edge_attr": "edge_attr_64", "type": "edge_type_16",
    "We1": "L0_gnn_We1", "be1": "L0_gnn_be1", "We2": "L0_gnn_We2", "be2": "L0_gnn_be2",
    "Wn1": "L0_gnn_Wn1", "bn1": "L0_gnn_bn1", "Wn2": "L0_gnn_Wn2", "bn2": "L0_gnn_bn2",
    "W1": "L1_gnn_W", "a_src": "L1_gnn_a_src", "a_tgt": "L1_gnn_a_tgt",
    "W2": "L2_gnn_W", "a_left": "L2_gnn_a_left", "a_right": "L2_gnn_a_right", "bias": "L2_gnn_bias",
    "bases": "L3_gnn_bases", "coefficients": "L3_gnn_coefficients", "w_self": "L3_gnn_w_self",
}


def kernel(**inputs):
    import numpy as _np
    import concourse.bacc as _bacc
    from concourse import mybir as _mybir
    from concourse.bass_utils import run_bass_kernel_spmd as _run

    nc = _bacc.Bacc("TRN2", target_bir_lowering=False, num_devices=1)
    arrays, args = {}, {}
    for short, name in _INS.items():
        a = _np.ascontiguousarray(inputs[name])
        arrays[f"in_{name}"] = a
        args[short] = nc.dram_tensor(f"in_{name}", a.shape, _mybir.dt.from_np(a.dtype), kind="ExternalInput").ap()
    out = nc.dram_tensor("out_x", (N_NODES, D), F32, kind="ExternalOutput").ap()
    graph_layers(nc, args, out)
    r = _run(nc, [arrays], core_ids=[0])
    return r.results[0]["out_x"]
```
